# Optimizing a Trainium2 kernel written in Bass

```python
import numpy as np
import jax
import jax.numpy as jnp

def _softmax(x, axis=-1):
    return jax.nn.softmax(x, axis=axis)

def _gelu(x):
    return jax.nn.gelu(x, approximate=True)

def _silu(x):
    return jax.nn.silu(x)

def _sigmoid(x):
    return jax.nn.sigmoid(x)

def _layernorm(x, axis=-1, eps=1e-05):
    m = jnp.mean(x, axis=axis, keepdims=True)
    v = jnp.var(x, axis=axis, keepdims=True)
    return (x - m) / jnp.sqrt(v + eps)

def _scatter_add(tgt, idx, src, axis=0):
    return tgt.at[idx].add(src)

def _segment_sum(src, seg, n):
    return jax.ops.segment_sum(src, seg, n)
kernel_name = 'mk_lm_tower_d1_tok_ids1024_r4_a6d61a'

def setup_inputs(seed: int=0):
    np.random.seed(seed)
    _w = jnp.asarray

    def _rec_inputs():
        import jax
        import jax.numpy as jnp
        _rk = jax.random.key(seed)
        x = jax.random.randint(jax.random.fold_in(_rk, 1), (8, 256), 0, 31993, jnp.int32)
        return x
    x = _rec_inputs()

    def _L0_tok_setup():
        import jax, jax.numpy as jnp
        import numpy as np
        EPS = 1e-05

        def layernorm(x, s, b):
            m = jnp.mean(x, axis=-1, keepdims=True)
            v = jnp.mean(jnp.square(x - m), axis=-1, keepdims=True)
            return (x - m) * jax.lax.rsqrt(v + EPS) * s + b

        def ssm(x, a_diag, Bm, Cm, Dm):
            a = jax.nn.sigmoid(a_diag)
            u = jnp.einsum('btd,ds->bts', x, Bm)

            def step(h, u_t):
                h = a * h + u_t
                return (h, h)
            h0 = jnp.zeros((x.shape[0], a.shape[0]), x.dtype)
            _, H = jax.lax.scan(step, h0, jnp.swapaxes(u, 0, 1))
            H = jnp.swapaxes(H, 0, 1)
            return jnp.einsum('bts,sd->btd', H, Cm) + jnp.einsum('btd,de->bte', x, Dm)
        key = jax.random.key(seed)
        ks = jax.random.split(key, 12)
        Bn, T = (4, 512)
        V, Dm, S, L, F = (8000, 256, 64, 4, 1024)

        def xavier(k, shape):
            fan_in, fan_out = (shape[-2], shape[-1])
            lim = float(np.sqrt(6.0 / (fan_in + fan_out)))
            return jax.random.uniform(k, shape, jnp.float32, -lim, lim)
        return {'tokens': jax.random.randint(ks[0], (Bn, T), 0, V), 'emb': jax.random.normal(ks[1], (V, Dm), jnp.float32), 'pos_emb': jax.random.normal(ks[2], (1024, Dm), jnp.float32), 'A_diag': jax.random.uniform(ks[3], (L, S), jnp.float32, -0.5, 0.5), 'B': xavier(ks[4], (L, Dm, S)), 'C': xavier(ks[5], (L, S, Dm)), 'D': xavier(ks[6], (L, Dm, Dm)) * 0.1, 'w1': xavier(ks[7], (L, Dm, F)), 'b1': jnp.zeros((L, F), jnp.float32), 'w2': xavier(ks[8], (L, F, Dm)), 'b2': jnp.zeros((L, Dm), jnp.float32), 'ln1_s': jnp.ones((L, Dm), jnp.float32), 'ln1_b': jnp.zeros((L, Dm), jnp.float32), 'ln2_s': jnp.ones((L, Dm), jnp.float32), 'ln2_b': jnp.zeros((L, Dm), jnp.float32), 'lnf_s': jnp.ones((Dm,), jnp.float32), 'lnf_b': jnp.zeros((Dm,), jnp.float32)}
    _L0_tok_all = _L0_tok_setup()
    _L0_tok_in = {k: v for k, v in _L0_tok_all.items() if k in ('emb', 'pos_emb', 'A_diag', 'B', 'C', 'D', 'w1', 'b1', 'w2', 'b2', 'ln1_s', 'ln1_b', 'ln2_s', 'ln2_b', 'lnf_s', 'lnf_b')}
    del _L0_tok_all

    def _L0_attn_setup():
        import jax, jax.numpy as jnp
        import numpy as np
        import math
        B, S, E, H = (2, 512, 256, 16)
        D = E // H
        SCALE = 1.0 / math.sqrt(D)
        key = jax.random.key(seed)
        ks = jax.random.split(key, 5)
        std = 0.02
        return {'q': jax.random.normal(ks[0], (B, S, E), dtype=jnp.float32), 'Wq': jax.random.normal(ks[1], (E, H * D), dtype=jnp.float32) * std, 'Wk': jax.random.normal(ks[2], (E, H * D), dtype=jnp.float32) * std, 'Wv': jax.random.normal(ks[3], (E, H * D), dtype=jnp.float32) * std, 'Wo': jax.random.normal(ks[4], (H * D, E), dtype=jnp.float32) * std, 'gamma': jnp.ones((H,), dtype=jnp.float32)}
    _L0_attn_all = _L0_attn_setup()
    _L0_attn_in = {k: v for k, v in _L0_attn_all.items() if k in ('Wq', 'Wk', 'Wv', 'Wo', 'gamma')}
    del _L0_attn_all

    def _L0_ffn_setup():
        import jax, jax.numpy as jnp
        import numpy as np
        DIM = 256
        DEPTH = 2
        HEADS = 8
        DIM_HEAD = 64
        WINDOW = 128
        INNER = HEADS * DIM_HEAD
        HID = int(DIM * 4 * 2 / 3)
        B, N = (2, 2048)
        QK_SCALE = 8.0

        def shift_token(t):
            t1, t2 = jnp.split(t, 2, axis=-1)
            t2 = jnp.pad(t2, ((0, 0), (1, 0), (0, 0)))[:, :-1]
            return jnp.concatenate([t1, t2], axis=-1)

        def l2norm(t):
            return t / jnp.clip(jnp.linalg.norm(t, axis=-1, keepdims=True), 1e-12)

        def rotate_half(x):
            x1, x2 = jnp.split(x, 2, axis=-1)
            return jnp.concatenate([-x2, x1], axis=-1)

        def rotary_xpos(q, k):
            n = q.shape[-2]
            half_idx = jnp.arange(0, DIM_HEAD, 2, dtype=jnp.float32)
            inv_freq = 1.0 / 10000.0 ** (half_idx / DIM_HEAD)
            t = jnp.arange(n, dtype=jnp.float32)
            freqs = t[:, None] * inv_freq[None, :]
            freqs = jnp.concatenate([freqs, freqs], axis=-1)
            base = (half_idx + 0.4 * DIM_HEAD) / (1.4 * DIM_HEAD)
            power = (t - n // 2) / float(WINDOW // 2)
            scale = base[None, :] ** power[:, None]
            scale = jnp.concatenate([scale, scale], axis=-1)
            cos, sin = (jnp.cos(freqs), jnp.sin(freqs))
            q = q * cos * scale + rotate_half(q) * sin * scale
            k = k * cos / scale + rotate_half(k) * sin / scale
            return (q, k)

        def local_attention(q, k, v):
            b, h, n, d = q.shape
            w = n // WINDOW
            bq = q.reshape(b, h, w, WINDOW, d) * QK_SCALE
            bk = k.reshape(b, h, w, WINDOW, d)
            bv = v.reshape(b, h, w, WINDOW, d)

            def look_around(t):
                p = jnp.pad(t, ((0, 0), (0, 0), (1, 0), (0, 0), (0, 0)))
                return jnp.concatenate([p[:, :, :w], p[:, :, 1:]], axis=3)
            bk, bv = (look_around(bk), look_around(bv))
            bt = jnp.arange(n).reshape(w, WINDOW)
            btp = jnp.pad(bt, ((1, 0), (0, 0)), constant_values=-1)
            btk = jnp.concatenate([btp[:w], btp[1:]], axis=1)
            sim = jnp.einsum('bhwid,bhwjd->bhwij', bq, bk)
            i = bt[:, :, None]
            j = btk[:, None, :]
            mask = (i < j) | (i > j + WINDOW) | (j == -1)
            sim = jnp.where(mask, -jnp.finfo(sim.dtype).max, sim)
            attn = jax.nn.softmax(sim, axis=-1)
            out = jnp.einsum('bhwij,bhwjd->bhwid', attn, bv)
            return out.reshape(b, h, n, d)

        def _layer(x, wqkv, qs, ksc, wo, lg, lb, w1, b1, w2, b2):
            b, n, _ = x.shape
            h = shift_token(x)
            qkv = h @ wqkv
            q, k, v = jnp.split(qkv, 3, axis=-1)
            to_heads = lambda t: t.reshape(b, n, HEADS, DIM_HEAD).transpose(0, 2, 1, 3)
            q, k, v = (to_heads(q), to_heads(k), to_heads(v))
            q = l2norm(q) * qs
            k = l2norm(k) * ksc
            q, k = rotary_xpos(q, k)
            o = local_attention(q, k, v)
            o = o.transpose(0, 2, 1, 3).reshape(b, n, INNER)
            x = x + o @ wo
            h = shift_token(x)
            mu = h.mean(-1, keepdims=True)
            var = h.var(-1, keepdims=True)
            h = (h - mu) / jnp.sqrt(var + 1e-05) * lg + lb
            h = h @ w1 + b1
            a, g = jnp.split(h, 2, axis=-1)
            h = a * jax.nn.gelu(g, approximate=False)
            x = x + h @ w2 + b2
            return x
        key = jax.random.key(seed)
        ks = jax.random.split(key, 6)
        return {'x': jax.random.normal(ks[0], (B, N, DIM), jnp.float32), 'wqkv': jax.random.normal(ks[1], (DEPTH, DIM, 3 * INNER), jnp.float32) * 0.02, 'q_scale': jnp.ones((DEPTH, DIM_HEAD), jnp.float32), 'k_scale': jnp.ones((DEPTH, DIM_HEAD), jnp.float32), 'wo': jax.random.normal(ks[2], (DEPTH, INNER, DIM), jnp.float32) * 0.02, 'ln_g': jnp.ones((DEPTH, DIM), jnp.float32), 'ln_b': jnp.zeros((DEPTH, DIM), jnp.float32), 'w1': jax.random.normal(ks[3], (DEPTH, DIM, 2 * HID), jnp.float32) * 0.02, 'b1': jnp.zeros((DEPTH, 2 * HID), jnp.float32), 'w2': jax.random.normal(ks[4], (DEPTH, HID, DIM), jnp.float32) * 0.02, 'b2': jnp.zeros((DEPTH, DIM), jnp.float32)}
    _L0_ffn_all = _L0_ffn_setup()
    _L0_ffn_in = {k: v for k, v in _L0_ffn_all.items() if k in ('wqkv', 'q_scale', 'k_scale', 'wo', 'ln_g', 'ln_b', 'w1', 'b1', 'w2', 'b2')}
    del _L0_ffn_all
    return {'x': x, 'L0_tok_emb': _L0_tok_in['emb'], 'L0_tok_pos_emb': _L0_tok_in['pos_emb'], 'L0_tok_A_diag': _L0_tok_in['A_diag'], 'L0_tok_B': _L0_tok_in['B'], 'L0_tok_C': _L0_tok_in['C'], 'L0_tok_D': _L0_tok_in['D'], 'L0_tok_w1': _L0_tok_in['w1'], 'L0_tok_b1': _L0_tok_in['b1'], 'L0_tok_w2': _L0_tok_in['w2'], 'L0_tok_b2': _L0_tok_in['b2'], 'L0_tok_ln1_s': _L0_tok_in['ln1_s'], 'L0_tok_ln1_b': _L0_tok_in['ln1_b'], 'L0_tok_ln2_s': _L0_tok_in['ln2_s'], 'L0_tok_ln2_b': _L0_tok_in['ln2_b'], 'L0_tok_lnf_s': _L0_tok_in['lnf_s'], 'L0_tok_lnf_b': _L0_tok_in['lnf_b'], 'L0_attn_Wq': _L0_attn_in['Wq'], 'L0_attn_Wk': _L0_attn_in['Wk'], 'L0_attn_Wv': _L0_attn_in['Wv'], 'L0_attn_Wo': _L0_attn_in['Wo'], 'L0_attn_gamma': _L0_attn_in['gamma'], 'L0_ffn_wqkv': _L0_ffn_in['wqkv'], 'L0_ffn_q_scale': _L0_ffn_in['q_scale'], 'L0_ffn_k_scale': _L0_ffn_in['k_scale'], 'L0_ffn_wo': _L0_ffn_in['wo'], 'L0_ffn_ln_g': _L0_ffn_in['ln_g'], 'L0_ffn_ln_b': _L0_ffn_in['ln_b'], 'L0_ffn_w1': _L0_ffn_in['w1'], 'L0_ffn_b1': _L0_ffn_in['b1'], 'L0_ffn_w2': _L0_ffn_in['w2'], 'L0_ffn_b2': _L0_ffn_in['b2']}

def reference(x, L0_tok_emb, L0_tok_pos_emb, L0_tok_A_diag, L0_tok_B, L0_tok_C, L0_tok_D, L0_tok_w1, L0_tok_b1, L0_tok_w2, L0_tok_b2, L0_tok_ln1_s, L0_tok_ln1_b, L0_tok_ln2_s, L0_tok_ln2_b, L0_tok_lnf_s, L0_tok_lnf_b, L0_attn_Wq, L0_attn_Wk, L0_attn_Wv, L0_attn_Wo, L0_attn_gamma, L0_ffn_wqkv, L0_ffn_q_scale, L0_ffn_k_scale, L0_ffn_wo, L0_ffn_ln_g, L0_ffn_ln_b, L0_ffn_w1, L0_ffn_b1, L0_ffn_w2, L0_ffn_b2):
    import jax
    import jax.numpy as jnp

    def _L0_tok_ref(tokens, emb, pos_emb, A_diag, B, C, D, w1, b1, w2, b2, ln1_s, ln1_b, ln2_s, ln2_b, lnf_s, lnf_b):
        import jax, jax.numpy as jnp
        import numpy as np
        EPS = 1e-05

        def layernorm(x, s, b):
            m = jnp.mean(x, axis=-1, keepdims=True)
            v = jnp.mean(jnp.square(x - m), axis=-1, keepdims=True)
            return (x - m) * jax.lax.rsqrt(v + EPS) * s + b

        def ssm(x, a_diag, Bm, Cm, Dm):
            a = jax.nn.sigmoid(a_diag)
            u = jnp.einsum('btd,ds->bts', x, Bm)

            def step(h, u_t):
                h = a * h + u_t
                return (h, h)
            h0 = jnp.zeros((x.shape[0], a.shape[0]), x.dtype)
            _, H = jax.lax.scan(step, h0, jnp.swapaxes(u, 0, 1))
            H = jnp.swapaxes(H, 0, 1)
            return jnp.einsum('bts,sd->btd', H, Cm) + jnp.einsum('btd,de->bte', x, Dm)
        T = tokens.shape[1]
        x = emb[tokens] + pos_emb[:T][None]
        L = A_diag.shape[0]
        for l in range(L):
            x = x + ssm(layernorm(x, ln1_s[l], ln1_b[l]), A_diag[l], B[l], C[l], D[l])
            h = layernorm(x, ln2_s[l], ln2_b[l])
            h = jax.nn.gelu(jnp.einsum('btd,df->btf', h, w1[l]) + b1[l], approximate=False)
            x = x + jnp.einsum('btf,fd->btd', h, w2[l]) + b2[l]
        return layernorm(x, lnf_s, lnf_b)

    def _L0_attn_ref(q, Wq, Wk, Wv, Wo, gamma):
        import jax, jax.numpy as jnp
        import numpy as np
        import math
        B, S, E, H = (2, 512, 256, 16)
        D = E // H
        SCALE = 1.0 / math.sqrt(D)
        Bq, Sq, _ = q.shape
        qh = (q @ Wq).reshape(Bq, Sq, H, D).transpose(0, 2, 1, 3)
        kh = (q @ Wk).reshape(Bq, Sq, H, D).transpose(0, 2, 1, 3)
        vh = (q @ Wv).reshape(Bq, Sq, H, D).transpose(0, 2, 1, 3)
        q_norm = jnp.sum(qh * qh, axis=-1, keepdims=True)
        k_norm = jnp.sum(kh * kh, axis=-1, keepdims=True)
        qk = jnp.einsum('bhsd,bhtd->bhst', qh, kh)
        dist = jnp.maximum(q_norm - 2.0 * qk + jnp.swapaxes(k_norm, -2, -1), 0.0)
        scores = jnp.exp(-gamma[None, :, None, None] * SCALE * dist)
        mask = jnp.triu(jnp.ones((Sq, Sq), dtype=bool), k=1)
        scores = jnp.where(mask, scores, 0.0)
        out = jnp.einsum('bhst,bhtd->bhsd', scores, vh)
        out = out.transpose(0, 2, 1, 3).reshape(Bq, Sq, H * D)
        return out @ Wo

    def _L0_ffn_ref(x, wqkv, q_scale, k_scale, wo, ln_g, ln_b, w1, b1, w2, b2):
        import jax, jax.numpy as jnp
        import numpy as np
        DIM = 256
        DEPTH = 2
        HEADS = 8
        DIM_HEAD = 64
        WINDOW = 128
        INNER = HEADS * DIM_HEAD
        HID = int(DIM * 4 * 2 / 3)
        B, N = (2, 2048)
        QK_SCALE = 8.0

        def shift_token(t):
            t1, t2 = jnp.split(t, 2, axis=-1)
            t2 = jnp.pad(t2, ((0, 0), (1, 0), (0, 0)))[:, :-1]
            return jnp.concatenate([t1, t2], axis=-1)

        def l2norm(t):
            return t / jnp.clip(jnp.linalg.norm(t, axis=-1, keepdims=True), 1e-12)

        def rotate_half(x):
            x1, x2 = jnp.split(x, 2, axis=-1)
            return jnp.concatenate([-x2, x1], axis=-1)

        def rotary_xpos(q, k):
            n = q.shape[-2]
            half_idx = jnp.arange(0, DIM_HEAD, 2, dtype=jnp.float32)
            inv_freq = 1.0 / 10000.0 ** (half_idx / DIM_HEAD)
            t = jnp.arange(n, dtype=jnp.float32)
            freqs = t[:, None] * inv_freq[None, :]
            freqs = jnp.concatenate([freqs, freqs], axis=-1)
            base = (half_idx + 0.4 * DIM_HEAD) / (1.4 * DIM_HEAD)
            power = (t - n // 2) / float(WINDOW // 2)
            scale = base[None, :] ** power[:, None]
            scale = jnp.concatenate([scale, scale], axis=-1)
            cos, sin = (jnp.cos(freqs), jnp.sin(freqs))
            q = q * cos * scale + rotate_half(q) * sin * scale
            k = k * cos / scale + rotate_half(k) * sin / scale
            return (q, k)

        def local_attention(q, k, v):
            b, h, n, d = q.shape
            w = n // WINDOW
            bq = q.reshape(b, h, w, WINDOW, d) * QK_SCALE
            bk = k.reshape(b, h, w, WINDOW, d)
            bv = v.reshape(b, h, w, WINDOW, d)

            def look_around(t):
                p = jnp.pad(t, ((0, 0), (0, 0), (1, 0), (0, 0), (0, 0)))
                return jnp.concatenate([p[:, :, :w], p[:, :, 1:]], axis=3)
            bk, bv = (look_around(bk), look_around(bv))
            bt = jnp.arange(n).reshape(w, WINDOW)
            btp = jnp.pad(bt, ((1, 0), (0, 0)), constant_values=-1)
            btk = jnp.concatenate([btp[:w], btp[1:]], axis=1)
            sim = jnp.einsum('bhwid,bhwjd->bhwij', bq, bk)
            i = bt[:, :, None]
            j = btk[:, None, :]
            mask = (i < j) | (i > j + WINDOW) | (j == -1)
            sim = jnp.where(mask, -jnp.finfo(sim.dtype).max, sim)
            attn = jax.nn.softmax(sim, axis=-1)
            out = jnp.einsum('bhwij,bhwjd->bhwid', attn, bv)
            return out.reshape(b, h, n, d)

        def _layer(x, wqkv, qs, ksc, wo, lg, lb, w1, b1, w2, b2):
            b, n, _ = x.shape
            h = shift_token(x)
            qkv = h @ wqkv
            q, k, v = jnp.split(qkv, 3, axis=-1)
            to_heads = lambda t: t.reshape(b, n, HEADS, DIM_HEAD).transpose(0, 2, 1, 3)
            q, k, v = (to_heads(q), to_heads(k), to_heads(v))
            q = l2norm(q) * qs
            k = l2norm(k) * ksc
            q, k = rotary_xpos(q, k)
            o = local_attention(q, k, v)
            o = o.transpose(0, 2, 1, 3).reshape(b, n, INNER)
            x = x + o @ wo
            h = shift_token(x)
            mu = h.mean(-1, keepdims=True)
            var = h.var(-1, keepdims=True)
            h = (h - mu) / jnp.sqrt(var + 1e-05) * lg + lb
            h = h @ w1 + b1
            a, g = jnp.split(h, 2, axis=-1)
            h = a * jax.nn.gelu(g, approximate=False)
            x = x + h @ w2 + b2
            return x
        for l in range(DEPTH):
            x = _layer(x, wqkv[l], q_scale[l], k_scale[l], wo[l], ln_g[l], ln_b[l], w1[l], b1[l], w2[l], b2[l])
        return x
    h = _L0_tok_ref(x, L0_tok_emb, L0_tok_pos_emb, L0_tok_A_diag, L0_tok_B, L0_tok_C, L0_tok_D, L0_tok_w1, L0_tok_b1, L0_tok_w2, L0_tok_b2, L0_tok_ln1_s, L0_tok_ln1_b, L0_tok_ln2_s, L0_tok_ln2_b, L0_tok_lnf_s, L0_tok_lnf_b)
    h = h + _L0_attn_ref(_layernorm(h, axis=-1), L0_attn_Wq, L0_attn_Wk, L0_attn_Wv, L0_attn_Wo, L0_attn_gamma)
    h = h + _L0_ffn_ref(_layernorm(h, axis=-1), L0_ffn_wqkv, L0_ffn_q_scale, L0_ffn_k_scale, L0_ffn_wo, L0_ffn_ln_g, L0_ffn_ln_b, L0_ffn_w1, L0_ffn_b1, L0_ffn_w2, L0_ffn_b2)
    return h

_drawn_inputs = setup_inputs


def setup_inputs(seed=0):
    import zlib

    import numpy as np

    out = dict(_drawn_inputs(seed))
    spreads = {'L0_tok_b1': (0.0, 0.1),
     'L0_tok_b2': (0.0, 0.1),
     'L0_tok_ln1_s': (1.0, 0.2),
     'L0_tok_ln1_b': (0.0, 0.1),
     'L0_tok_ln2_s': (1.0, 0.2),
     'L0_tok_ln2_b': (0.0, 0.1),
     'L0_tok_lnf_s': (1.0, 0.2),
     'L0_tok_lnf_b': (0.0, 0.1),
     'L0_attn_gamma': (1.0, 0.2),
     'L0_ffn_q_scale': (1.0, 0.6),
     'L0_ffn_k_scale': (1.0, 0.6),
     'L0_ffn_ln_g': (1.0, 0.6),
     'L0_ffn_ln_b': (0.0, 0.8),
     'L0_ffn_b1': (0.0, 0.8),
     'L0_ffn_b2': (0.0, 2.0)}
    factors = {'L0_ffn_w1': 7.585, 'L0_ffn_w2': 6.95}
    for name, (base, spread) in spreads.items():
        noise = np.random.default_rng([zlib.crc32(name.encode()), seed]).standard_normal(out[name].shape)
        drawn = base * np.exp(spread * noise) if base else spread * noise
        out[name] = jnp.asarray(drawn.astype(out[name].dtype))
    for name, factor in factors.items():
        out[name] = (out[name] * factor).astype(out[name].dtype)
    return out
```

```python
import concourse.bass as bass
from concourse import mybir
from contextlib import ExitStack
import numpy as np

F32 = mybir.dt.float32
F32R = mybir.dt.float32r
I32 = mybir.dt.int32
U32 = mybir.dt.uint32
ALU = mybir.AluOpType
ACT = mybir.ActivationFunctionType
AX = mybir.AxisListType
ds = bass.ds

P = 128
NT = 16
GT = 4
GTOK = GT * P
NG = NT // GT
D = 256
DC = D // P
EPS = 1e-5


def reach(eng, sem, value):
    if not isinstance(value, int):
        value = eng.to_reg(value)
    eng.wait_ge(sem, 1)
    eng.wait_ge(sem, value)


def tower_phase(nc, sems, X, dram):
    L, S, F = 4, 64, 1024
    FC = F // P
    V = dram["L0_tok_emb"].shape[0]
    STEPS = NG
    VECS = 8

    with ExitStack() as ctx:
        def sb(name, shape, dt=F32):
            return ctx.enter_context(nc.sbuf_tensor("t_" + name, shape, dt))

        def sem(name):
            sems.append(nc.alloc_semaphore("t_" + name))
            return sems[-1]

        raw_b = sb("raw_b", [P, DC, S])
        raw_c = sb("raw_c", [P, D])
        raw_d = sb("raw_d", [P, DC, D])
        raw_1 = sb("raw_1", [P, DC, F])
        raw_2 = sb("raw_2", [P, FC, D])
        b_cat = sb("b_cat", [P, DC, 2 * S], F32R)
        b_hiz = sb("b_hiz", [P, DC, 2 * S], F32R)
        c_hi = sb("c_hi", [P, D], F32R)
        c_lo = sb("c_lo", [P, D], F32R)
        d_hi = sb("d_hi", [P, DC, D], F32R)
        d_lo = sb("d_lo", [P, DC, D], F32R)
        w1_hi = sb("w1_hi", [P, DC, F], F32R)
        w1_lo = sb("w1_lo", [P, DC, F], F32R)
        w2_hi = sb("w2_hi", [P, FC, D], F32R)
        w2_lo = sb("w2_lo", [P, FC, D], F32R)
        ln_all = sb("ln_all", [P, 4, L * DC])
        ln_cur = sb("ln_cur", [P, 4, DC])
        fb_all = sb("fb_all", [P, L * FC])
        fb_cur = sb("fb_cur", [P, FC])
        b2_all = sb("b2_all", [P, L * D])
        a_raw = sb("a_raw", [P, L])
        a_all = sb("a_all", [P, L])
        keep = sb("keep", [P, GTOK])
        decay = sb("decay", [P, GTOK])
        neghalf = sb("neghalf", [P, GT])
        ids = sb("ids", [P, NT], I32)
        idm = sb("idm", [P, NT])
        idf = sb("idf", [P, NT])
        idx = sb("idx", [P, NT], U32)
        pos = sb("pos", [P, 2, D])
        ident = sb("ident", [P, P])
        st = [sb(f"st{k}", [P, GT, 6]) for k in (1, 2)]
        mv = [sb(f"mv{k}", [P, GT, 2]) for k in (1, 2)]
        ve = [sb(f"ve{k}", [P, GT]) for k in (1, 2)]
        rs = [sb(f"rs{k}", [P, GT]) for k in (1, 2)]
        xn = [sb(f"xn{k}", [P, GT, D]) for k in (1, 2)]
        nf = [sb(f"nf{k}", [P, DC, GTOK]) for k in (1, 2)]
        nh = [sb(f"nh{k}", [P, DC, GTOK], F32R) for k in (1, 2)]
        nl = [sb(f"nl{k}", [P, DC, GTOK], F32R) for k in (1, 2)]
        hs = sb("hs", [P, GTOK])
        hs_hi = sb("hs_hi", [P, GTOK], F32R)
        hs_lo = sb("hs_lo", [P, GTOK], F32R)
        gf = sb("gf", [P, 2, GTOK])
        g_hi = sb("g_hi", [P, 4, GTOK], F32R)
        g_lo = sb("g_lo", [P, 4, GTOK], F32R)

        def bank(name, n=1):
            return ctx.enter_context(nc.psum_tensor("t_" + name, [P, n, 512], F32))

        ps_t = bank("ps_t", 2)
        ps_u = bank("ps_u")
        ps_f = bank("ps_f", 2)
        ps_o = bank("ps_o", 2)

        s_ids, s_idm, s_idf, s_idx = sem("ids"), sem("idm"), sem("idf"), sem("idx")
        s_vec, s_pos, s_gather = sem("vec"), sem("pos"), [sem(f"gather{g}") for g in range(NG)]
        s_ident, s_keep, s_decay, s_sig = sem("ident"), sem("keep"), sem("decay"), sem("sig")
        raw_front, raw_w1, raw_w2 = sem("raw_front"), sem("raw_w1"), sem("raw_w2")
        front_hi, front_split = sem("front_hi"), sem("front_split")
        w1_h, w1_split, w2_h, w2_split = sem("w1_h"), sem("w1_split"), sem("w2_h"), sem("w2_split")
        cur_ready = sem("cur_ready")
        x_ready, xb_ready, xy_ready = sem("x_ready"), sem("xb_ready"), sem("xy_ready")
        st_done = [sem(f"st_done{k}") for k in (1, 2)]
        mv_done = [sem(f"mv_done{k}") for k in (1, 2)]
        ve_done = [sem(f"ve_done{k}") for k in (1, 2)]
        rs_done = [sem(f"rs_done{k}") for k in (1, 2)]
        xn_ready = [sem(f"xn_ready{k}") for k in (1, 2)]
        t_full = [sem(f"t_full{k}") for k in (1, 2)]
        nf_done = [sem(f"nf_done{k}") for k in (1, 2)]
        n_split = [sem(f"n_split{k}") for k in (1, 2)]
        pf_free = sem("pf_free")
        u_full, scanned, hs_hi_done, hs_split = sem("u_full"), sem("scanned"), sem("hs_hi_done"), sem("hs_split")
        y_full, f_full = sem("y_full"), sem("f_full")
        g_hi_done, g_split, g_used = sem("g_hi_done"), sem("g_split"), sem("g_used")

        def tiles(g):
            return range(GT * g, GT * g + GT)

        block = ctx.enter_context(nc.Block())

        def num(l, g):
            return l * STEPS + g

        def after(l, g, k):
            return (l + (g + k) // STEPS, (g + k) % STEPS)

        @block.sync
        def _(sp):
            sp.dma_start(ids[:, :], dram["x"].rearrange("s (t p) -> p (s t)", p=P)).then_inc(s_ids, 16)
            sp.dma_start(pos[:, :, :], dram["L0_tok_pos_emb"][0:2 * P, :].rearrange("(t p) d -> p t d", p=P)).then_inc(s_pos, 16)
            for l in range(L):
                if l >= 1:
                    sp.wait_ge(front_split, l)
                sp.dma_start(raw_b[:, :, :], dram["L0_tok_B"][l].rearrange("(c p) s -> p c s", p=P)).then_inc(raw_front, 16)
                sp.dma_start(raw_c[0:S, :], dram["L0_tok_C"][l]).then_inc(raw_front, 16)
                sp.dma_start(raw_c[S:2 * S, :], dram["L0_tok_C"][l]).then_inc(raw_front, 16)
                sp.dma_start(raw_d[:, :, :], dram["L0_tok_D"][l].rearrange("(c p) s -> p c s", p=P)).then_inc(raw_front, 16)
                if l >= 1:
                    sp.wait_ge(w1_split, FC * l)
                sp.dma_start(raw_1[:, :, :], dram["L0_tok_w1"][l].rearrange("(c p) s -> p c s", p=P)).then_inc(raw_w1, 16)
                if l >= 1:
                    sp.wait_ge(w2_split, FC * l)
                sp.dma_start(raw_2[:, :, :], dram["L0_tok_w2"][l].rearrange("(c p) s -> p c s", p=P)).then_inc(raw_w2, 16)

        @block.tensor
        def _(pe):
            def transposes(k, l, g):
                n = num(l, g)
                pe.wait_ge(xn_ready[k], n + 1)
                if k == 0:
                    pe.wait_ge(nf_done[1], n * DC + 1)
                for c in range(DC):
                    for t in range(GT):
                        mm = pe.transpose(ps_t[:, c, t * P:(t + 1) * P], xn[k][:, t, c * P:(c + 1) * P], ident[:, :])
                mm.then_inc(t_full[k], 1)

            def state_in(l, g):
                n = num(l, g)
                if g == 0:
                    pe.wait_ge(front_split, l + 1)
                pe.wait_ge(n_split[0], n * 2 + 2)
                pe.wait_ge(scanned, n + 1)
                for c in range(DC):
                    pe.matmul(ps_u[:, 0, :], b_cat[:, c, :], nh[0][:, c, :], start=(c == 0), stop=False)
                    mm = pe.matmul(ps_u[:, 0, :], b_hiz[:, c, :], nl[0][:, c, :], start=False, stop=(c == DC - 1))
                mm.then_inc(u_full, 1)

            def state_out(l, g):
                n = num(l, g)
                pe.wait_ge(hs_split, n + 1)
                for t in range(GT):
                    tok = slice(t * P, (t + 1) * P)
                    out = ps_t[:, t // 2, (t % 2) * D:(t % 2 + 1) * D]
                    passes = [(nh[0][:, c, tok], w[:, c, :]) for c in range(DC) for w in (d_hi, d_lo)]
                    passes += [(nl[0][:, c, tok], d_hi[:, c, :]) for c in range(DC)]
                    passes += [(hs_hi[:, tok], c_hi[:, :]), (hs_hi[:, tok], c_lo[:, :]), (hs_lo[:, tok], c_hi[:, :])]
                    for i, (a, w) in enumerate(passes):
                        mm = pe.matmul(out, a, w, start=(t % 2 == 0 and i == 0),
                                       stop=(t % 2 == 1 and i == len(passes) - 1), skip_group_check=True)
                mm.then_inc(y_full, 1)

            def hidden(l, g, j):
                n = num(l, g)
                if g == 0:
                    pe.wait_ge(w1_split, l * FC + j + 1)
                if j == 0:
                    pe.wait_ge(n_split[1], n * 2 + 2)
                pe.wait_ge(pf_free, n * FC + j + 1)
                col = slice(j * P, (j + 1) * P)
                for c in range(DC):
                    pe.matmul(ps_f[:, j % 2, :], w1_hi[:, c, col], nh[1][:, c, :], start=(c == 0), stop=False)
                    pe.matmul(ps_f[:, j % 2, :], w1_lo[:, c, col], nh[1][:, c, :], start=False, stop=False)
                    mm = pe.matmul(ps_f[:, j % 2, :], w1_hi[:, c, col], nl[1][:, c, :], start=False, stop=(c == DC - 1))
                mm.then_inc(f_full, 1)

            def output(l, g, j):
                n = num(l, g)
                if g == 0:
                    pe.wait_ge(w2_split, l * FC + j + 1)
                if j == 0:
                    pe.wait_ge(x_ready, n + NG)
                pe.wait_ge(g_split, n * FC + j + 3)
                for t in range(GT):
                    tok = slice(t * P, (t + 1) * P)
                    out = ps_o[:, t // 2, (t % 2) * D:(t % 2 + 1) * D]
                    pe.matmul(out, g_hi[:, j % 4, tok], w2_hi[:, j, :], start=(j == 0 and t % 2 == 0), stop=False, skip_group_check=True)
                    pe.matmul(out, g_hi[:, j % 4, tok], w2_lo[:, j, :], start=False, stop=False, skip_group_check=True)
                    mm = pe.matmul(out, g_lo[:, j % 4, tok], w2_hi[:, j, :], start=False,
                                   stop=(j == FC - 1 and t % 2 == 1), skip_group_check=True)
                mm.then_inc(g_used, 1)

            def step(l, g, front):
                nx = after(l, g, 1)
                hidden(l, g, 0)
                hidden(l, g, 1)
                if front:
                    transposes(0, *nx)
                output(l, g, 0)
                hidden(l, g, 2)
                if front:
                    state_in(*nx)
                output(l, g, 1)
                hidden(l, g, 3)
                output(l, g, 2)
                if front:
                    state_out(*nx)
                for j in range(4, FC):
                    hidden(l, g, j)
                    if j < FC - 1:
                        output(l, g, j - 1)
                if front:
                    transposes(1, *nx)
                output(l, g, FC - 2)
                output(l, g, FC - 1)

            for s in (t_full[0], t_full[1], nf_done[0], nf_done[1], scanned):
                pe.sem_inc(s, 1)
            pe.sem_inc(pf_free, 2)
            pe.wait_ge(s_ident, 2)
            transposes(0, 0, 0)
            state_in(0, 0)
            state_out(0, 0)
            transposes(1, 0, 0)
            with pe.Fori(0, L - 1) as l:
                for g in range(STEPS):
                    step(l, g, True)
            for g in range(STEPS):
                step(L - 1, g, g < STEPS - 1)

        @block.scalar
        def _(act):
            def spread(k, l, g):
                n = num(l, g)
                act.wait_ge(t_full[k], n + 2)
                for c in range(DC):
                    s = ln_cur[:, 2 * k, c:c + 1]
                    b = ln_cur[:, 2 * k + 1, c:c + 1]
                    act.activation(nf[k][:, c, :], ps_t[:, c, :], ACT.Identity, bias=b, scale=s)
                    ins = act.activation(nh[k][:, c, :], ps_t[:, c, :], ACT.Identity, bias=b, scale=s)
                    ins.then_inc(nf_done[k], 1)

            def state_hi(l, g):
                act.wait_ge(scanned, num(l, g) + 2)
                act.activation(hs_hi[:, :], hs[:, :], ACT.Copy).then_inc(hs_hi_done, 1)

            def gelu(l, g, j):
                n = num(l, g) * FC + j
                act.wait_ge(f_full, n + 1)
                act.wait_ge(g_used, n + 1)
                act.wait_ge(g_split, n + 1)
                act.activation(gf[:, j % 2, :], ps_f[:, j % 2, :], ACT.Gelu, bias=fb_cur[:, j:j + 1]).then_inc(pf_free, 1)
                act.wait_ge(pf_free, n + 3)
                act.activation(g_hi[:, j % 4, :], gf[:, j % 2, :], ACT.Copy).then_inc(g_hi_done, 1)

            def take_ln(l, count):
                act.activation(ln_cur[:, :, :], ln_all[:, :, ds(l * DC, DC)], ACT.Copy).then_inc(cur_ready, 1)
                act.wait_ge(cur_ready, count)

            def take_fb(l, count):
                act.activation(fb_cur[:, :], fb_all[:, ds(l * FC, FC)], ACT.Copy).then_inc(cur_ready, 1)
                act.wait_ge(cur_ready, count)

            def w1_hi_part(l, j, used):
                act.wait_ge(raw_w1, l * 16 + 16)
                if used is not None:
                    act.wait_ge(f_full, used)
                act.activation(w1_hi[:, :, j * P:(j + 1) * P], raw_1[:, :, j * P:(j + 1) * P], ACT.Copy).then_inc(w1_h, 1)

            def w2_hi_part(l, j, used):
                act.wait_ge(raw_w2, l * 16 + 16)
                if used is not None:
                    act.wait_ge(g_used, used)
                act.activation(w2_hi[:, j, :], raw_2[:, j, :], ACT.Copy).then_inc(w2_h, 1)

            def step(l, g, front):
                nx = after(l, g, 1)
                n = num(l, g) * FC
                prep = front and g == STEPS - 1
                if g == 0:
                    act.wait_ge(pf_free, n + 2)
                    take_fb(l, l * 2 + 2)
                if prep:
                    act.wait_ge(nf_done[1], num(l, g) * DC + DC + 1)
                    take_ln(l + 1, l * 2 + 3)
                for j in range(FC):
                    gelu(l, g, j)
                    if front and j == 1:
                        spread(0, *nx)
                    if front and j == 3:
                        state_hi(*nx)
                    if prep:
                        w1_hi_part(l + 1, j, n + j + 1)
                        if j >= 3:
                            w2_hi_part(l + 1, j - 3, n + 4 + j - 2)
                if front:
                    spread(1, *nx)
                if prep:
                    for j in range(FC - 3, FC):
                        w2_hi_part(l + 1, j, n + 4 + j + 1)

            act.sem_inc(g_used, 4)
            act.sem_inc(g_split, 2)
            act.wait_ge(s_vec, 16 * VECS)
            act.activation(a_all[:, :], a_raw[:, :], ACT.Sigmoid).then_inc(s_sig, 1)
            take_ln(0, 1)
            spread(0, 0, 0)
            for j in range(FC):
                w1_hi_part(0, j, None)
            state_hi(0, 0)
            spread(1, 0, 0)
            for j in range(FC):
                w2_hi_part(0, j, None)
            with act.Fori(0, L - 1) as l:
                for g in range(STEPS):
                    step(l, g, True)
            for g in range(STEPS):
                step(L - 1, g, g < STEPS - 1)


        @block.vector
        def _(dve):
            def grp(g):
                return X[:, GT * g:GT * g + GT, :]

            def stats(k, l, g):
                n = num(l, g)
                if k == 0:
                    reach(dve, x_ready, n + 1)
                else:
                    reach(dve, xy_ready, n + 1)
                for t in range(GT):
                    ins = dve.bn_stats(st[k][:, t, :], X[:, GT * g + t, :])
                ins.then_inc(st_done[k], 1)
                reach(dve, st_done[k], n + 1)
                for t in range(GT):
                    ins = dve.bn_aggr(mv[k][:, t, :], st[k][:, t, :])
                ins.then_inc(mv_done[k], 1)
                dve.wait_ge(mv_done[k], n + 1)
                dve.tensor_scalar(ve[k][:, :], mv[k][:, :, 1], EPS, None, ALU.add).then_inc(ve_done[k], 1)

            def norm(k, l, g):
                n = num(l, g)
                dve.wait_ge(rs_done[k], n + 1)
                dve.wait_ge(t_full[k], n + 1)
                for t in range(GT):
                    ins = dve.tensor_scalar(xn[k][:, t, :], X[:, GT * g + t, :], mv[k][:, t, 0:1], rs[k][:, t:t + 1],
                                            ALU.subtract, ALU.mult)
                ins.then_inc(xn_ready[k], 1)

            def spread_lo(k, l, g):
                n = num(l, g)
                for c in range(DC):
                    dve.wait_ge(nf_done[k], n * DC + c + 2)
                    dve.tensor_tensor(nl[k][:, c, :], nf[k][:, c, :], nh[k][:, c, :].bitcast(F32),
                                      ALU.subtract).then_inc(n_split[k], 1)

            def scan(l, g):
                n = num(l, g)
                dve.wait_ge(u_full, n + 1)
                dve.tensor_tensor_scan(hs[:, :], decay[:, :], ps_u[:, 0, :], 0.0, ALU.mult, ALU.add).then_inc(scanned, 1)

            def state_lo(l, g):
                n = num(l, g)
                dve.wait_ge(hs_hi_done, n + 1)
                dve.tensor_tensor(hs_lo[:, :], hs[:, :], hs_hi[:, :].bitcast(F32), ALU.subtract).then_inc(hs_split, 1)

            def add_state(l, g):
                n = num(l, g)
                dve.wait_ge(y_full, n + 1)
                for h in range(2):
                    x2 = X[:, GT * g + 2 * h:GT * g + 2 * h + 2, :].rearrange("p t d -> p (t d)")
                    ins = dve.tensor_tensor(x2, ps_t[:, h, :], x2, ALU.add)
                ins.then_inc(xy_ready, 1)

            def gelu_lo(l, g, j):
                n = num(l, g) * FC + j
                dve.wait_ge(g_hi_done, n + 1)
                dve.tensor_tensor(g_lo[:, j % 4, :], gf[:, j % 2, :], g_hi[:, j % 4, :].bitcast(F32),
                                  ALU.subtract).then_inc(g_split, 1)

            def add_output(l, g):
                n = num(l, g)
                dve.wait_ge(xb_ready, n + 1)
                dve.wait_ge(g_used, n * FC + FC + 4)
                for h in range(2):
                    x2 = X[:, GT * g + 2 * h:GT * g + 2 * h + 2, :].rearrange("p t d -> p (t d)")
                    ins = dve.tensor_tensor(x2, ps_o[:, h, :], x2, ALU.add)
                ins.then_inc(x_ready, 1)

            def set_decay(l, count):
                dve.tensor_scalar(decay[:, :], keep[:, :], a_all[:, ds(l, 1)], None, ALU.mult).then_inc(s_decay, 1)
                dve.wait_ge(s_decay, count)

            def step(l, g, front, ahead):
                nx, n2 = after(l, g, 1), after(l, g, 2)
                if front and g == STEPS - 1:
                    set_decay(l + 1, l + 2)
                gelu_lo(l, g, 0)
                gelu_lo(l, g, 1)
                if front:
                    spread_lo(0, *nx)
                gelu_lo(l, g, 2)
                if front:
                    scan(*nx)
                gelu_lo(l, g, 3)
                if front:
                    state_lo(*nx)
                gelu_lo(l, g, 4)
                if front:
                    add_state(*nx)
                    stats(1, *nx)
                gelu_lo(l, g, 5)
                if front:
                    norm(1, *nx)
                if ahead:
                    stats(0, *n2)
                gelu_lo(l, g, 6)
                if ahead:
                    norm(0, *n2)
                gelu_lo(l, g, 7)
                if front:
                    spread_lo(1, *nx)
                add_output(l, g)

            dve.wait_ge(s_ids, 16)
            dve.tensor_scalar(idm[:, :], ids[:, :], 0.0, float(V), ALU.is_lt, ALU.mult).then_inc(s_idm, 1)
            dve.wait_ge(s_idm, 1)
            dve.tensor_tensor(idf[:, :], ids[:, :], idm[:, :], ALU.add).then_inc(s_idf, 1)
            dve.wait_ge(s_idf, 1)
            dve.tensor_scalar(idx[:, :], idf[:, :], 0.0, float(V - 1), ALU.max, ALU.min).then_inc(s_idx, 1)
            dve.memset(keep[:, :], 1.0).then_inc(s_keep, 1)
            dve.wait_ge(s_keep, 1)
            dve.memset(keep[:, :].rearrange("p (s t) -> p s t", t=2 * P)[:, :, 0:1], 0.0).then_inc(s_keep, 1)
            dve.memset(neghalf[:, :], -0.5).then_inc(s_keep, 1)
            dve.memset(b_hiz[:, :, :].bitcast(F32), 0.0).then_inc(s_keep, 1)
            dve.wait_ge(s_sig, 1)
            dve.wait_ge(s_keep, 4)
            set_decay(0, 1)
            dve.wait_ge(s_pos, 16)
            for g in range(NG):
                dve.wait_ge(s_gather[g], 16 * GT)
                for h in range(2):
                    x2 = X[:, GT * g + 2 * h:GT * g + 2 * h + 2, :]
                    ins = dve.tensor_tensor(x2, x2, pos[:, :, :], ALU.add)
                ins.then_inc(x_ready, 1)
                if g == 0:
                    stats(0, 0, 0)
                    norm(0, 0, 0)
                    spread_lo(0, 0, 0)
            scan(0, 0)
            state_lo(0, 0)
            add_state(0, 0)
            stats(1, 0, 0)
            norm(1, 0, 0)
            stats(0, 0, 1)
            norm(0, 0, 1)
            spread_lo(1, 0, 0)
            with dve.Fori(0, L - 1) as l:
                for g in range(STEPS):
                    step(l, g, True, True)
            for g in range(STEPS):
                step(L - 1, g, g < STEPS - 1, g < STEPS - 2)

        @block.gpsimd
        def _(pool):
            def rstd(k, l, g):
                pool.wait_ge(ve_done[k], num(l, g) + 1)
                pool.tensor_tensor(rs[k][:, :], ve[k][:, :], neghalf[:, :], ALU.pow).then_inc(rs_done[k], 1)

            def add_bias(l, g):
                reach(pool, xn_ready[1], num(l, g) + 1)
                for t in tiles(g):
                    ins = pool.tensor_tensor(X[:, t, :], X[:, t, :], b2_all[:, ds(l * D, D)], ALU.add)
                ins.then_inc(xb_ready, 1)

            def split_front(l, first):
                pool.wait_ge(raw_front, l * 64 + 64)
                if not first:
                    reach(pool, y_full, l * STEPS)
                pool.tensor_copy(b_cat[:, :, 0:S], raw_b[:, :, :])
                pool.tensor_copy(b_hiz[:, :, 0:S], raw_b[:, :, :])
                pool.tensor_copy(c_hi[:, :], raw_c[:, :])
                pool.tensor_copy(d_hi[:, :, :], raw_d[:, :, :]).then_inc(front_hi, 1)
                pool.wait_ge(front_hi, l + 1)
                pool.tensor_tensor(b_cat[:, :, S:2 * S], raw_b[:, :, :], b_cat[:, :, 0:S].bitcast(F32), ALU.subtract)
                pool.tensor_tensor(c_lo[:, :], raw_c[:, :], c_hi[:, :].bitcast(F32), ALU.subtract)
                pool.tensor_tensor(d_lo[:, :, :], raw_d[:, :, :], d_hi[:, :, :].bitcast(F32), ALU.subtract).then_inc(front_split, 1)

            def w1_lo_part(l, j):
                pool.wait_ge(w1_h, l * FC + j + 1)
                col = slice(j * P, (j + 1) * P)
                pool.tensor_tensor(w1_lo[:, :, col], raw_1[:, :, col], w1_hi[:, :, col].bitcast(F32), ALU.subtract).then_inc(w1_split, 1)

            def w2_lo_part(l, j):
                pool.wait_ge(w2_h, l * FC + j + 1)
                pool.tensor_tensor(w2_lo[:, j, :], raw_2[:, j, :], w2_hi[:, j, :].bitcast(F32), ALU.subtract).then_inc(w2_split, 1)

            def step(l, g, front, ahead):
                nx, n2 = after(l, g, 1), after(l, g, 2)
                prep = front and g == STEPS - 1
                if prep:
                    for j in range(4):
                        w1_lo_part(l + 1, j)
                if front and g == STEPS - 2 and ahead:
                    split_front(l + 1, False)
                if front:
                    rstd(1, *nx)
                    add_bias(*nx)
                if ahead:
                    rstd(0, *n2)
                if prep:
                    for j in range(4, FC):
                        w1_lo_part(l + 1, j)
                    for j in range(FC):
                        w2_lo_part(l + 1, j)

            pool.memset(ident[:, :], 0.0).then_inc(s_ident, 1)
            pool.wait_ge(s_idx, 1)
            for t in range(NT):
                pool.indirect_dma_start(X[:, t, :], None, dram["L0_tok_emb"][:, :],
                                        bass.IndirectOffsetOnAxis(ap=idx[:, t:t + 1], axis=0)).then_inc(s_gather[t // GT], 16)
            pool.wait_ge(s_ident, 1)
            pool.affine_select(out=ident[:, :], in_=ident[:, :], compare_op=ALU.not_equal, fill=1.0, base=0,
                               pattern=[[-1, P]], channel_multiplier=1).then_inc(s_ident, 1)
            for k, name in enumerate(("L0_tok_ln1_s", "L0_tok_ln1_b", "L0_tok_ln2_s", "L0_tok_ln2_b")):
                pool.dma_start(ln_all[:, k, :], dram[name].rearrange("l (c p) -> p (l c)", p=P)).then_inc(s_vec, 16)
            pool.dma_start(fb_all[:, :], dram["L0_tok_b1"].rearrange("l (c p) -> p (l c)", p=P)).then_inc(s_vec, 16)
            pool.dma_start(b2_all[:, :], dram["L0_tok_b2"].rearrange("(a l) d -> a (l d)", a=1).broadcast_to([P, L * D])).then_inc(s_vec, 16)
            pool.dma_start(a_raw[0:S, :], dram["L0_tok_A_diag"].rearrange("l s -> s l")).then_inc(s_vec, 16)
            pool.dma_start(a_raw[S:2 * S, :], dram["L0_tok_A_diag"].rearrange("l s -> s l")).then_inc(s_vec, 16)
            pool.wait_ge(s_keep, 4)
            rstd(0, 0, 0)
            split_front(0, True)
            rstd(1, 0, 0)
            pool.wait_ge(s_vec, 16 * VECS)
            add_bias(0, 0)
            rstd(0, 0, 1)
            for j in range(FC):
                w1_lo_part(0, j)
            for j in range(FC):
                w2_lo_part(0, j)
            with pool.Fori(0, L - 1) as l:
                for g in range(STEPS):
                    step(l, g, True, True)
            for g in range(STEPS):
                step(L - 1, g, g < STEPS - 1, g < STEPS - 2)


def attention_phase(nc, sems, X, dram):
    H, HD = 16, 16
    ROW = 64
    HP = H // 2
    QUAD, HQ = 4, H // 4
    SCALE = HD ** -0.5
    SEQS = 2
    SCORES = 3 * P
    AHEAD = 2
    VECS = 3
    NS = SEQS * H

    with ExitStack() as ctx:
        def sb(name, shape, dt=F32):
            return ctx.enter_context(nc.sbuf_tensor("a_" + name, shape, dt))

        def sem(name):
            sems.append(nc.alloc_semaphore("a_" + name))
            return sems[-1]

        def bank(name, n=1):
            return ctx.enter_context(nc.psum_tensor("a_" + name, [P, n, 512], F32))

        raw_w = sb("raw_w", [P, DC, 3 * D])
        w_hi = sb("w_hi", [P, DC, 3 * D], F32R)
        w_lo = sb("w_lo", [P, DC, 3 * D], F32R)
        raw_o = sb("raw_o", [P, HQ, D])
        wo_hi = sb("wo_hi", [P, HQ, D], F32R)
        wo_lo = sb("wo_lo", [P, HQ, D], F32R)
        fs = sb("fs", [P, D])
        fb = sb("fb", [P, D])
        gam = sb("gam", [P, H])
        gsc = sb("gsc", [P, H])
        neghalf = sb("neghalf", [P, GT])
        ident = sb("ident", [P, P])
        st = sb("st", [P, GT, 6])
        mv = sb("mv", [P, GT, 2])
        ve = sb("ve", [P, GT])
        rs = sb("rs", [P, GT])
        xn = sb("xn", [P, GT, D])
        nh = sb("nh", [P, DC, GTOK], F32R)
        nl = sb("nl", [P, DC, GTOK], F32R)
        sq = sb("sq", [P, 2 * D])
        nrm = sb("nrm", [P, 2 * H])
        qs = [sb(f"qs{i}", [P, H, ROW], F32R) for i in range(2)]
        ks = [sb(f"ks{i}", [P, H, ROW], F32R) for i in range(2)]
        v = sb("v", [P, GT, H, 2 * HD])
        qt = sb("qt", [P, HP, GTOK], F32R)
        kt = sb("kt", [P, HP, GTOK], F32R)
        dist = sb("dist", [P, 2, SCORES])
        e = sb("e", [P, 4, SCORES])
        ot_hi = sb("ot_hi", [P, HQ, 2 * P], F32R)
        ot_lo = sb("ot_lo", [P, HQ, 2 * P], F32R)

        ps_t = bank("ps_t", 2)
        ps_qk, ps_v = bank("ps_qk"), bank("ps_v")
        ps_d = bank("ps_d", 2)
        ps_o = bank("ps_o", 2)

        s_w, s_wo, s_vec, s_zero, s_ident, s_gsc = (sem(x) for x in ("w", "wo", "vec", "zero", "ident", "gsc"))
        w_h, w_split, s_pad = sem("w_h"), sem("w_split"), sem("pad")
        st_done, mv_done, ve_done, rs_done, xn_ready = (sem(x) for x in ("st", "mv", "ve", "rs", "xn"))
        h_mul, h_ready = sem("h_mul"), sem("h_ready")
        t_full, nh_done, n_split = sem("t_full"), sem("nh_done"), sem("n_split")
        qk_full, v_full, sq_done, qk_hi, qk_read, v_done = (sem(x) for x in ("qk_full", "v_full", "sq_done", "qk_hi", "qk_read", "v_done"))
        nrm_done, nrm_hi, stacked, s_full, qt_done, kt_done = (sem(x) for x in ("nrm", "nrm_hi", "stacked", "s_full", "qt_done", "kt_done"))
        d_full, relu_done, exp_done, masked, pv_done = (sem(x) for x in ("d_full", "relu", "exp", "masked", "pv"))
        ot_h, ot_split, y_full, y_added = sem("ot_h"), sem("ot_split"), sem("y_full"), sem("y_added")

        block = ctx.enter_context(nc.Block())

        @block.sync
        def _(sp):
            for i, name in enumerate(("L0_attn_Wq", "L0_attn_Wk", "L0_attn_Wv")):
                sp.dma_start(raw_w[:, :, D * i:D * i + D], dram[name].rearrange("(c p) n -> p c n", p=P)).then_inc(s_w, 16)
            sp.dma_start(fs[:, :], dram["L0_tok_lnf_s"].rearrange("(a d) -> a d", a=1).broadcast_to([P, D])).then_inc(s_vec, 16)
            sp.dma_start(fb[:, :], dram["L0_tok_lnf_b"].rearrange("(a d) -> a d", a=1).broadcast_to([P, D])).then_inc(s_vec, 16)
            sp.dma_start(gam[:, :], dram["L0_attn_gamma"].rearrange("(a d) -> a d", a=1).broadcast_to([P, H])).then_inc(s_vec, 16)
            sp.wait_ge(s_zero, 1)
            wo = dram["L0_attn_Wo"].rearrange("(q j d) n -> j d q n", j=QUAD, d=HD)
            for j in range(QUAD):
                sp.dma_start(raw_o[32 * j:32 * j + HD, :, :], wo[j]).then_inc(s_wo, 16)

        @block.tensor
        def _(pe):
            def group(g):
                pe.wait_ge(xn_ready, g * 2 + 2)
                pe.wait_ge(y_added, g * SEQS + 1)
                for c in range(DC):
                    for t in range(GT):
                        mm = pe.transpose(ps_t[:, c, t * P:(t + 1) * P], xn[:, t, c * P:(c + 1) * P], ident[:, :])
                mm.then_inc(t_full, 1)

                def project(t):
                    tok = slice(t * P, (t + 1) * P)
                    pe.wait_ge(qk_read, g * GT + t + 1)
                    for out, lo, hi, full in ((ps_qk[:, 0, :], 0, 2 * D, qk_full), (ps_v[:, 0, 0:D], 2 * D, 3 * D, v_full)):
                        if lo:
                            pe.wait_ge(v_done, g * GT + t + 1)
                        for c in range(DC):
                            pe.matmul(out, nh[:, c, tok], w_hi[:, c, lo:hi], start=(c == 0), stop=False)
                            pe.matmul(out, nh[:, c, tok], w_lo[:, c, lo:hi], start=False, stop=False)
                            mm = pe.matmul(out, nl[:, c, tok], w_hi[:, c, lo:hi], start=False, stop=(c == DC - 1))
                        mm.then_inc(full, 1)

                def turn(t):
                    pe.wait_ge(stacked, g * GT + t + 2)
                    pe.wait_ge(qt_done, g * GT + t + 1)
                    pe.wait_ge(kt_done, g * GT + t + 1)
                    for dst, src in ((ps_t, qs[t % 2]), (ps_d, ks[t % 2])):
                        for hp in range(HP):
                            mm = pe.transpose(dst[:, hp // 4, (hp % 4) * P:(hp % 4 + 1) * P],
                                              src[:, 2 * hp:2 * hp + 2, :].rearrange("p h r -> p (h r)").bitcast(F32), ident[:, :])
                        mm.then_inc(s_full, 1)

                def distances(s, h):
                    n = g * NS + s * H + h
                    if h == 0:
                        pe.wait_ge(qt_done, g * GT + GT + 1)
                        pe.wait_ge(kt_done, g * GT + GT + 1)
                    pe.wait_ge(relu_done, n + 1)
                    rows = slice(ROW * (h % 2), ROW * (h % 2) + ROW)
                    t0, t1 = 2 * s * P, (2 * s + 1) * P
                    pe.matmul(ps_d[:, h % 2, 0:2 * P], kt[rows, h // 2, t1:t1 + P], qt[rows, h // 2, t0:t0 + 2 * P], start=True, stop=True)
                    pe.matmul(ps_d[:, h % 2, 2 * P:3 * P], kt[rows, h // 2, t0:t0 + P], qt[rows, h // 2, t0:t0 + P],
                              start=True, stop=True).then_inc(d_full, 1)

                def values(s, h):
                    n = g * NS + s * H + h
                    if h == 0:
                        pe.wait_ge(ot_split, g * SEQS + s + 1)
                    pe.wait_ge(masked, n + 1)
                    j, q = h % QUAD, h // QUAD
                    out = ps_o[32 * j:32 * j + 32, q // 2, (q % 2) * 2 * P:(q % 2 + 1) * 2 * P]
                    pe.matmul(out, v[:, 2 * s + 1, h, :], e[:, h % 4, 0:2 * P], start=True, stop=False, skip_group_check=True)
                    pe.matmul(out[:, 0:P], v[:, 2 * s, h, :], e[:, h % 4, 2 * P:3 * P], start=False, stop=True,
                              skip_group_check=True).then_inc(pv_done, 1)

                def project_out(s):
                    pe.wait_ge(ot_split, g * SEQS + s + 2)
                    for t in range(2):
                        out = ps_t[:, s, t * D:(t + 1) * D]
                        for q in range(HQ):
                            tok = slice(t * P, (t + 1) * P)
                            pe.matmul(out, ot_hi[:, q, tok], wo_hi[:, q, :], start=(t == 0 and q == 0), stop=False, skip_group_check=True)
                            pe.matmul(out, ot_hi[:, q, tok], wo_lo[:, q, :], start=False, stop=False, skip_group_check=True)
                            mm = pe.matmul(out, ot_lo[:, q, tok], wo_hi[:, q, :], start=False, stop=(t == 1 and q == HQ - 1), skip_group_check=True)
                    mm.then_inc(y_full, 1)

                pe.wait_ge(w_split, 2)
                pe.wait_ge(n_split, g * DC + DC)
                for t in range(GT):
                    project(t)
                    if t >= 1:
                        turn(t - 1)
                turn(GT - 1)
                for s in range(SEQS):
                    for h in range(H + AHEAD):
                        if h < H:
                            distances(s, h)
                        if h >= AHEAD:
                            values(s, h - AHEAD)
                    project_out(s)

            for s in (y_added, qk_read, v_done, qt_done, kt_done, ot_split, nrm_done, s_full, y_full, t_full, stacked):
                pe.sem_inc(s, 1)
            pe.sem_inc(relu_done, 2)
            pe.wait_ge(s_ident, 2)
            pe.wait_ge(s_pad, 5)
            with pe.Fori(0, NG) as g:
                group(g)

        @block.scalar
        def _(act):
            def group(g):
                act.wait_ge(t_full, g + 2)
                for c in range(DC):
                    act.activation(nh[:, c, :], ps_t[:, c, :], ACT.Copy).then_inc(nh_done, 1)

                def stack(t):
                    n = g * GT + t
                    q = ps_qk[:, 0, 0:D].rearrange("p (h d) -> p h d", h=H)
                    k = ps_qk[:, 0, D:2 * D].rearrange("p (h d) -> p h d", h=H)
                    act.wait_ge(qk_full, n + 1)
                    act.wait_ge(nrm_done, n + 1)
                    act.activation(sq[:, :], ps_qk[:, 0, :], ACT.Square).then_inc(sq_done, 1)
                    act.wait_ge(s_full, (g * GT + max(t - 1, 0)) * 2 + 1)
                    act.activation(qs[t % 2][:, :, 0:HD], q, ACT.Copy)
                    act.activation(qs[t % 2][:, :, HD:2 * HD], q, ACT.Copy).then_inc(qk_hi, 1)
                    act.activation(ks[t % 2][:, :, 0:HD], k, ACT.Copy, scale=-2.0)
                    act.activation(ks[t % 2][:, :, 2 * HD:3 * HD], k, ACT.Copy, scale=-2.0).then_inc(qk_hi, 1)
                    act.wait_ge(v_full, n + 1)
                    act.wait_ge(pv_done, g * NS + 4)
                    act.activation(v[:, t, :, 0:HD], ps_v[:, 0, 0:D].rearrange("p (h d) -> p h d", h=H), ACT.Copy).then_inc(v_done, 1)

                def turned(t):
                    n = g * GT + t
                    act.wait_ge(s_full, n * 2 + 2)
                    act.activation(qt[:, :, t * P:(t + 1) * P], ps_t[:, :, :].rearrange("p b (h t) -> p (b h) t", t=P), ACT.Copy).then_inc(qt_done, 1)

                for t in range(GT):
                    stack(t)
                    if t >= 1:
                        turned(t - 1)
                turned(GT - 1)
                for s in range(SEQS):
                    for h in range(H):
                        n = g * NS + s * H + h
                        act.wait_ge(relu_done, n + 3)
                        act.wait_ge(pv_done, n + 1)
                        act.activation(e[:, h % 4, :], dist[:, h % 2, :], ACT.Exp, scale=gsc[:, h:h + 1]).then_inc(exp_done, 1)
                    act.wait_ge(pv_done, g * NS + (s + 1) * H + 4)
                    act.wait_ge(y_full, g * SEQS + s + 1)
                    for b in range(2):
                        act.activation(ot_hi[:, 2 * b:2 * b + 2, :].rearrange("p q t -> p (q t)"), ps_o[:, b, :], ACT.Copy).then_inc(ot_h, 1)

            act.sem_inc(pv_done, 4)
            act.wait_ge(s_w, 48)
            act.activation(w_hi[:, :, :], raw_w[:, :, :], ACT.Copy).then_inc(w_h, 1)
            act.wait_ge(s_wo, 64)
            act.activation(wo_hi[:, :, :], raw_o[:, :, :], ACT.Copy).then_inc(w_h, 1)
            act.wait_ge(s_gsc, 1)
            act.wait_ge(s_pad, 5)
            with act.Fori(0, NG) as g:
                group(g)

        @block.vector
        def _(dve):
            def norm(g, k):
                n = g * 2 + k
                if k:
                    reach(dve, h_ready, g + 1)
                else:
                    dve.wait_ge(s_pad, 5)
                    dve.wait_ge(y_added, g * SEQS + 1)
                for t in range(GT):
                    ins = dve.bn_stats(st[:, t, :], X[:, ds(g * GT + t, 1), :].rearrange("p a d -> p (a d)"))
                ins.then_inc(st_done, 1)
                reach(dve, st_done, n + 1)
                for t in range(GT):
                    ins = dve.bn_aggr(mv[:, t, :], st[:, t, :])
                ins.then_inc(mv_done, 1)
                dve.wait_ge(mv_done, n + 1)
                dve.tensor_scalar(ve[:, :], mv[:, :, 1], EPS, None, ALU.add).then_inc(ve_done, 1)
                dve.wait_ge(rs_done, n + 1)
                if k == 0:
                    dve.wait_ge(t_full, g + 1)
                for t in range(GT):
                    ins = dve.tensor_scalar(xn[:, t, :], X[:, ds(g * GT + t, 1), :].rearrange("p a d -> p (a d)"), mv[:, t, 0:1], rs[:, t:t + 1],
                                            ALU.subtract, ALU.mult)
                ins.then_inc(xn_ready, 1)

            def group(g):
                norm(g, 0)
                norm(g, 1)
                for c in range(DC):
                    dve.wait_ge(nh_done, g * DC + c + 1)
                    dve.tensor_tensor(nl[:, c, :], ps_t[:, c, :], nh[:, c, :].bitcast(F32), ALU.subtract).then_inc(n_split, 1)

                def stack(t):
                    n = g * GT + t
                    q = ps_qk[:, 0, 0:D].rearrange("p (h d) -> p h d", h=H)
                    k = ps_qk[:, 0, D:2 * D].rearrange("p (h d) -> p h d", h=H)
                    dve.wait_ge(sq_done, n + 1)
                    dve.wait_ge(stacked, n + 1)
                    dve.tensor_reduce(nrm[:, :], sq[:, :].rearrange("p (h d) -> p h d", d=HD), AX.X, ALU.add).then_inc(nrm_done, 1)
                    dve.wait_ge(qk_hi, n * 2 + 2)
                    dve.tensor_tensor(qs[t % 2][:, :, 2 * HD:3 * HD], q, qs[t % 2][:, :, 0:HD].bitcast(F32), ALU.subtract)
                    dve.wait_ge(nrm_done, n + 2)
                    dve.tensor_copy(qs[t % 2][:, :, 3 * HD:3 * HD + 1], nrm[:, 0:H].unsqueeze(2))
                    dve.tensor_copy(ks[t % 2][:, :, 3 * HD + 2:3 * HD + 3], nrm[:, H:2 * H].unsqueeze(2)).then_inc(nrm_hi, 1)
                    dve.scalar_tensor_tensor(ks[t % 2][:, :, HD:2 * HD], k, -2.0, ks[t % 2][:, :, 0:HD].bitcast(F32),
                                             ALU.mult, ALU.subtract).then_inc(qk_read, 1)
                    dve.wait_ge(nrm_hi, n + 1)
                    dve.tensor_tensor(qs[t % 2][:, :, 3 * HD + 1:3 * HD + 2], nrm[:, 0:H].unsqueeze(2),
                                      qs[t % 2][:, :, 3 * HD:3 * HD + 1].bitcast(F32), ALU.subtract)
                    dve.tensor_tensor(ks[t % 2][:, :, 3 * HD + 3:3 * HD + 4], nrm[:, H:2 * H].unsqueeze(2),
                                      ks[t % 2][:, :, 3 * HD + 2:3 * HD + 3].bitcast(F32), ALU.subtract).then_inc(stacked, 1)

                def turned(t):
                    n = g * GT + t
                    dve.wait_ge(s_full, n * 2 + 3)
                    dve.tensor_copy(kt[:, :, t * P:(t + 1) * P], ps_d[:, :, :].rearrange("p b (h t) -> p (b h) t", t=P)).then_inc(kt_done, 1)

                for t in range(GT):
                    stack(t)
                    if t >= 1:
                        turned(t - 1)
                turned(GT - 1)
                for s in range(SEQS):
                    for h in range(H):
                        n = g * NS + s * H + h
                        dve.wait_ge(d_full, n + 1)
                        dve.wait_ge(exp_done, n + 1)
                        dve.tensor_scalar(dist[:, h % 2, :], ps_d[:, h % 2, 0:SCORES], 0.0, None, ALU.max).then_inc(relu_done, 1)
                    for b in range(2):
                        dve.wait_ge(ot_h, (g * SEQS + s) * 2 + b + 1)
                        ins = dve.tensor_tensor(ot_lo[:, 2 * b:2 * b + 2, :].rearrange("p q t -> p (q t)"), ps_o[:, b, :],
                                                ot_hi[:, 2 * b:2 * b + 2, :].rearrange("p q t -> p (q t)").bitcast(F32), ALU.subtract)
                    ins.then_inc(ot_split, 1)
                    dve.wait_ge(y_full, g * SEQS + s + 2)
                    x2 = X[:, ds(g * GT + 2 * s, 2), :].rearrange("p t d -> p (t d)")
                    dve.tensor_tensor(x2, ps_t[:, s, :], x2, ALU.add).then_inc(y_added, 1)

            dve.sem_inc(exp_done, 2)
            dve.memset(neghalf[:, :], -0.5).then_inc(s_pad, 1)
            for i in range(2):
                dve.memset(qs[i][:, :, 3 * HD + 2:3 * HD + 4].bitcast(F32), 1.0)
                dve.memset(qs[i][:, :, 3 * HD + 4:ROW].bitcast(F32), 0.0)
                dve.memset(ks[i][:, :, 3 * HD:3 * HD + 2].bitcast(F32), 1.0)
                dve.memset(ks[i][:, :, 3 * HD + 4:ROW].bitcast(F32), 0.0).then_inc(s_pad, 1)
            dve.memset(v[:, :, :, HD:2 * HD], 0.0).then_inc(s_pad, 1)
            dve.wait_ge(s_vec, 16 * VECS)
            dve.tensor_scalar(gsc[:, :], gam[:, :], -SCALE, None, ALU.mult).then_inc(s_gsc, 1)
            dve.memset(ve[:, :], 1.0).then_inc(s_pad, 1)
            dve.wait_ge(s_pad, 5)
            with dve.Fori(0, NG) as g:
                group(g)

        @block.gpsimd
        def _(pool):
            def group(g):
                pool.wait_ge(ve_done, g * 2 + 1)
                pool.tensor_tensor(rs[:, :], ve[:, :], neghalf[:, :], ALU.pow).then_inc(rs_done, 1)
                reach(pool, xn_ready, g * 2 + 1)
                for t in range(GT):
                    ins = pool.tensor_tensor(X[:, ds(g * GT + t, 1), :].rearrange("p a d -> p (a d)"), xn[:, t, :], fs[:, :], ALU.mult)
                ins.then_inc(h_mul, 1)
                reach(pool, h_mul, g + 1)
                for t in range(GT):
                    xt = X[:, ds(g * GT + t, 1), :].rearrange("p a d -> p (a d)")
                    ins = pool.tensor_tensor(xt, xt, fb[:, :], ALU.add)
                ins.then_inc(h_ready, 1)
                pool.wait_ge(ve_done, g * 2 + 2)
                pool.tensor_tensor(rs[:, :], ve[:, :], neghalf[:, :], ALU.pow).then_inc(rs_done, 1)
                for s in range(SEQS):
                    for h in range(H):
                        n = g * NS + s * H + h
                        reach(pool, exp_done, n + 3)
                        diag = e[:, h % 4, P:3 * P]
                        pool.affine_select(out=diag, in_=diag, compare_op=ALU.is_gt, fill=zero, base=0,
                                           pattern=[[0, 2], [-1, P]], channel_multiplier=1).then_inc(masked, 1)

            pool.memset(ident[:, :], 0.0).then_inc(s_ident, 1)
            pool.memset(raw_o[:, :, :], 0.0).then_inc(s_zero, 1)
            pool.wait_ge(s_ident, 1)
            pool.affine_select(out=ident[:, :], in_=ident[:, :], compare_op=ALU.not_equal, fill=1.0, base=0,
                               pattern=[[-1, P]], channel_multiplier=1).then_inc(s_ident, 1)
            pool.wait_ge(w_h, 1)
            pool.tensor_tensor(w_lo[:, :, :], raw_w[:, :, :], w_hi[:, :, :].bitcast(F32), ALU.subtract).then_inc(w_split, 1)
            pool.wait_ge(w_h, 2)
            pool.tensor_tensor(wo_lo[:, :, :], raw_o[:, :, :], wo_hi[:, :, :].bitcast(F32), ALU.subtract).then_inc(w_split, 1)
            pool.wait_ge(s_vec, 16 * VECS)
            pool.wait_ge(s_pad, 5)
            zero = pool.to_reg(0.0)
            with pool.Fori(0, NG) as g:
                group(g)


WINDOW, HEADS3, HD3 = 128, 8, 64


def constants():
    n, f = 2 * P, np.float32
    half = np.arange(0, HD3, 2).astype(f)
    inv_freq = (f(1.0) / np.power(f(10000.0), half / f(HD3))).astype(f)
    t = np.arange(n).astype(f)
    freqs = np.concatenate([t[:, None] * inv_freq[None, :]] * 2, axis=-1).astype(f)
    base = ((half + f(0.4 * HD3)) / f(1.4 * HD3)).astype(f)
    power = ((t - f(n // 2)) / f(WINDOW // 2)).astype(f)
    scale = np.power(base[None, :].astype(np.float64), power[:, None])
    scale = np.concatenate([scale, scale], axis=-1)
    cos, sin = np.cos(freqs.astype(np.float64)), np.sin(freqs.astype(np.float64))
    sin = sin * np.where(np.arange(HD3) < HD3 // 2, -1.0, 1.0)[None, :]
    return {"rotary": np.stack([8 * cos * scale, 8 * sin * scale, cos / scale, sin / scale]).astype(f)}


def window_phase(nc, sems, X, dram, out):
    L, H, HD, INNER, HID = 2, HEADS3, HD3, HEADS3 * HD3, 682
    FC = -(-HID // P)
    HIDP = FC * P
    LAST = HID - (FC - 1) * P
    IC = INNER // P
    SEQS = 2
    NH = SEQS * H
    SC = 3 * P
    NEG = float(-np.finfo(np.float32).max)
    VECS = 2 * 6 + 2 * 1

    with ExitStack() as ctx:
        def sb(name, shape, dt=F32):
            return ctx.enter_context(nc.sbuf_tensor("w_" + name, shape, dt))

        def sem(name):
            sems.append(nc.alloc_semaphore("w_" + name))
            return sems[-1]

        def bank(name, n=1):
            return ctx.enter_context(nc.psum_tensor("w_" + name, [P, n, 512], F32))

        raw = sb("raw", [P, DC * 2 * HIDP + FC * D])
        raw_qkv = raw[:, 0:DC * 3 * INNER].rearrange("p (c n) -> p c n", c=DC)
        raw_o = raw[:, DC * 3 * INNER:DC * 3 * INNER + IC * D].rearrange("p (c n) -> p c n", c=IC)
        raw_1 = raw[:, 0:DC * 2 * HIDP].rearrange("p (c u n) -> p c u n", c=DC, u=2)
        raw_2 = raw[:, DC * 2 * HIDP:].rearrange("p (c n) -> p c n", c=FC)
        qkv_hi = sb("qkv_hi", [P, DC, 3 * INNER], F32R)
        qkv_lo = sb("qkv_lo", [P, DC, 3 * INNER], F32R)
        wo_hi = sb("wo_hi", [P, IC, D], F32R)
        wo_lo = sb("wo_lo", [P, IC, D], F32R)
        w1_hi = sb("w1_hi", [P, DC, 2, HIDP], F32R)
        w1_lo = sb("w1_lo", [P, DC, 2, HIDP], F32R)
        w2_hi = sb("w2_hi", [P, FC, D], F32R)
        w2_lo = sb("w2_lo", [P, FC, D], F32R)
        ln_all = sb("ln_all", [P, 2, L * DC])
        ln_cur = sb("ln_cur", [P, 2, DC])
        b1_all = sb("b1_all", [P, L, 2, FC])
        b1_cur = sb("b1_cur", [P, 2, FC])
        b2_all = sb("b2_all", [P, L * D])
        scl = sb("scl", [P, 2, 2, L * HD])
        rot = sb("rot", [P, 4, 2, HD])
        tab = sb("tab", [P, 4, 2, HD])
        neghalf = sb("neghalf", [P, 2 * H])
        ident = sb("ident", [P, P])
        mask = sb("mask", [P, SC])
        st = sb("st", [P, GT, 2, 6])
        mv = sb("mv", [P, GT, 2])
        ve = sb("ve", [P, GT])
        rs = sb("rs", [P, GT])
        xn = sb("xn", [P, GT, D])
        xs = sb("xs", [P, GT, P])
        nf = sb("nf", [P, DC, GTOK])
        nh = sb("nh", [P, DC, GTOK], F32R)
        nl = sb("nl", [P, DC, GTOK], F32R)
        sq = sb("sq", [P, 2, INNER])
        ss = sb("ss", [P, 2, H])
        sc = sb("sc", [P, 2, H])
        rn = sb("rn", [P, 2, H])
        m1 = sb("m1", [P, 2, INNER])
        m2 = sb("m2", [P, 2, INNER])
        qt = sb("qt", [P, IC, GTOK])
        kt = sb("kt", [P, IC, GTOK])
        v = sb("v", [P, GT, INNER])
        sm = sb("sm", [P, 2, SC])
        mx = sb("mx", [P, NH, 2])
        rsum = sb("rsum", [P, 2, H])
        rinv = sb("rinv", [P, 2, H])
        pr = sb("pr", [P, 2, SC])
        pt = sb("pt", [P, 2, SC])
        o = sb("o", [P, 2, INNER])
        ot_hi = sb("ot_hi", [P, 2, IC, P], F32R)
        ot_lo = sb("ot_lo", [P, 2, IC, P], F32R)
        gate = sb("gate", [P, 2, GTOK])
        hid = sb("hid", [P, 2, GTOK])
        h_hi = sb("h_hi", [P, 2, GTOK], F32R)
        h_lo = sb("h_lo", [P, 2, GTOK], F32R)
        hres = xn
        zer = sb("zer", [P, 2])

        ps_q = bank("ps_q", 3)
        ps_p = bank("ps_p")
        ps_d = bank("ps_d", 2)
        ps_o = bank("ps_o", 2)
        val_bank = [ps_q[:, 0, :], ps_q[:, 1, :]]
        gate_bank = [ps_q[:, 2, :], ps_p[:, 0, :]]

        names = ("h_out h_in stored vec ident maskz mask pad fill raw_a raw_b hi_a hi_b split_a split_b cur tab x_ready "
                 "x0_st x0_mv x0_ve x0_rs staged t1_full nh1 split1 q_full k_full v_full sq_q sq_k v_done qk_read ss_done sc_done "
                 "rn_done rotm rota roted s_full qt_done kt_done d_full sm_done p_done p_full pt_done pv_done ri o_done ot_full "
                 "ot_h ot_split y_full x_mid shifted st mv ve rs xn t2_full nf_done split2 a_full g_full gate_done gated h_hi "
                 "h_split h_used xb padp fin")
        S = {x: sem(x) for x in names.split()}
        block = ctx.enter_context(nc.Block())

        def xt(g, t):
            return X[:, ds(g * GT + t, 1), :].rearrange("p a d -> p (a d)")

        def x2(g, s):
            return X[:, ds(g * GT + 2 * s, 2), :].rearrange("p t d -> p (t d)")

        out_v = out.rearrange("s (t p) d -> p (s t) d", p=P)

        @block.sync
        def _(sp):
            for g in range(NG):
                sp.dma_start(out_v[:, GT * g:GT * g + GT, :], X[:, GT * g:GT * g + GT, :]).then_inc(S["h_out"], 16)
            sp.dma_start(rot[:, :, :, :].rearrange("p k t d -> p (k t) d"), dram["rotary"].rearrange("k (t p) d -> p (k t) d", p=P)).then_inc(S["vec"], 16)
            for k, name in enumerate(("L0_ffn_ln_g", "L0_ffn_ln_b")):
                sp.dma_start(ln_all[:, k, :], dram[name].rearrange("l (c p) -> p (l c)", p=P)).then_inc(S["vec"], 16)
            sp.dma_start(b2_all[:, :], dram["L0_ffn_b2"].rearrange("(a l) d -> a (l d)", a=1).broadcast_to([P, L * D])).then_inc(S["vec"], 16)
            for k, name in enumerate(("L0_ffn_q_scale", "L0_ffn_k_scale")):
                src = dram[name].rearrange("(a l) (u d) -> a l u d", a=1, u=2)
                sp.dma_start(scl[:, k, 0, :], dram[name].rearrange("(a l) d -> a (l d)", a=1).broadcast_to([P, L * HD])).then_inc(S["vec"], 16)
                for l in range(L):
                    for u in range(2):
                        sp.dma_start(scl[:, k, 1, l * HD + u * (HD // 2):l * HD + (u + 1) * (HD // 2)],
                                     src[:, l, 1 - u, :].broadcast_to([P, HD // 2])).then_inc(S["vec"], 16)
            sp.wait_ge(S["pad"], 1)
            for l in range(L):
                for u in range(2):
                    b1 = dram["L0_ffn_b1"][l, u * HID:(u + 1) * HID]
                    sp.dma_start(b1_all[:, l, u, 0:FC - 1], b1[0:(FC - 1) * P].rearrange("(c p) -> p c", p=P)).then_inc(S["vec"], 16)
                    sp.dma_start(b1_all[0:LAST, l, u, FC - 1:FC], b1[(FC - 1) * P:HID].rearrange("(p c) -> p c", c=1)).then_inc(S["vec"], 16)
            with sp.Fori(0, L) as l:
                sp.wait_ge(S["split_b"], l + 1)
                sp.dma_start(raw_qkv, dram["L0_ffn_wqkv"][ds(l, 1)].rearrange("a (c p) n -> p (a c) n", p=P)).then_inc(S["raw_a"], 16)
                sp.dma_start(raw_o, dram["L0_ffn_wo"][ds(l, 1)].rearrange("a (c p) n -> p (a c) n", p=P)).then_inc(S["raw_a"], 16)
                sp.wait_ge(S["split_a"], l + 1)
                w1 = dram["L0_ffn_w1"][ds(l, 1)].rearrange("a (c p) (u n) -> p (a c) u n", p=P, u=2)
                for u in range(2):
                    sp.dma_start(raw_1[:, :, u, 0:HID], w1[:, :, u, :]).then_inc(S["raw_b"], 16)
                w2 = dram["L0_ffn_w2"][ds(l, 1)]
                sp.dma_start(raw_2[:, 0:FC - 1, :], w2[:, 0:(FC - 1) * P, :].rearrange("a (c p) n -> p (a c) n", p=P)).then_inc(S["raw_b"], 16)
                sp.dma_start(raw_2[0:LAST, FC - 1, :], w2[:, (FC - 1) * P:HID, :].rearrange("a p n -> p (a n)")).then_inc(S["raw_b"], 16)

        ALLV = 16 * (4 + 2 * (1 + 2 * L) + 4 * L)

        @block.tensor
        def _(pe):
            def turn_x():
                for c in range(DC):
                    for t in range(GT):
                        mm = pe.transpose(ps_d[:, c, t * P:(t + 1) * P], xn[:, t, c * P:(c + 1) * P], ident[:, :])
                return mm

            def step(l, g):
                n = l * NG + g
                pe.wait_ge(S["staged"], n + 1)
                pe.wait_ge(S["split2"], n * DC + 1)
                turn_x().then_inc(S["t1_full"], 1)
                pe.wait_ge(S["split_a"], l + 1)
                pe.wait_ge(S["split1"], n * DC + DC)

                def project(t):
                    m = n * GT + t
                    tok = slice(t * P, (t + 1) * P)
                    if t == 0:
                        pe.wait_ge(S["gated"], n * FC + 2)
                    for i, full in enumerate(("q_full", "k_full", "v_full")):
                        pe.wait_ge(S["v_done" if i == 2 else "qk_read"], m + 1 if i == 2 else 2 * m + 1)
                        cols = slice(i * INNER, (i + 1) * INNER)
                        for c in range(DC):
                            pe.matmul(ps_q[:, i, :], nh[:, c, tok], qkv_hi[:, c, cols], start=(c == 0), stop=False)
                            pe.matmul(ps_q[:, i, :], nh[:, c, tok], qkv_lo[:, c, cols], start=False, stop=False)
                            mm = pe.matmul(ps_q[:, i, :], nl[:, c, tok], qkv_hi[:, c, cols], start=False, stop=(c == DC - 1))
                        mm.then_inc(S[full], 1)

                def turn(t):
                    m = n * GT + t
                    for i, free in enumerate(("qt_done", "kt_done")):
                        pe.wait_ge(S["roted"], 2 * m + i + 1)
                        pe.wait_ge(S[free], m + 1)
                        for c in range(IC):
                            mm = pe.transpose(ps_d[:, i, c * P:(c + 1) * P], m1[:, i, c * P:(c + 1) * P], ident[:, :])
                        mm.then_inc(S["s_full"], 1)

                def scores(s, h):
                    m = n * NH + s * H + h
                    if s == 0 and h == 0:
                        pe.wait_ge(S["qt_done"], n * GT + GT + 1)
                        pe.wait_ge(S["kt_done"], n * GT + GT + 1)
                    if s == 1 and h == 0:
                        pe.wait_ge(S["ot_split"], n * GT + 2)
                    pe.wait_ge(S["sm_done"], m + 1)
                    rows = slice(HD * (h % 2), HD * (h % 2) + HD)
                    t0, t1, t2 = 2 * s * P, (2 * s + 1) * P, (2 * s + 2) * P
                    b = ps_d[:, h % 2, :]
                    pe.matmul(b[:, 0:P], qt[rows, h // 2, t0:t1], kt[rows, h // 2, t0:t1], start=True, stop=True)
                    pe.matmul(b[:, P:SC], qt[rows, h // 2, t1:t2], kt[rows, h // 2, t0:t2], start=True, stop=True).then_inc(S["d_full"], 1)

                def turn_p(s, h):
                    m = n * NH + s * H + h
                    pe.wait_ge(S["p_done"], m + 3)
                    pe.wait_ge(S["pt_done"], m + 2)
                    for b in range(3):
                        mm = pe.transpose(ps_p[:, 0, b * P:(b + 1) * P], pr[:, h % 2, b * P:(b + 1) * P], ident[:, :])
                    mm.then_inc(S["p_full"], 1)

                def values(s, h):
                    m = n * NH + s * H + h
                    if h == 0:
                        pe.wait_ge(S["o_done"], 2 * (n * SEQS + s) + 1)
                        if s == 0:
                            pe.wait_ge(S["x_ready"], n + NG)
                    pe.wait_ge(S["pt_done"], m + 3)
                    vs = slice(h * HD, (h + 1) * HD)
                    pe.matmul(ps_o[:, 0, vs], pt[:, h % 2, 0:P], v[:, 2 * s, vs], start=True, stop=True)
                    pe.matmul(ps_o[:, 1, vs], pt[:, h % 2, P:2 * P], v[:, 2 * s, vs], start=True, stop=False)
                    pe.matmul(ps_o[:, 1, vs], pt[:, h % 2, 2 * P:3 * P], v[:, 2 * s + 1, vs], start=False, stop=True).then_inc(S["pv_done"], 1)

                def turn_o(s):
                    for w in range(2):
                        m = (n * SEQS + s) * 2 + w
                        pe.wait_ge(S["o_done"], m + 2)
                        for c in range(IC):
                            mm = pe.transpose(ps_d[:, w, c * P:(c + 1) * P], o[:, w, c * P:(c + 1) * P], ident[:, :])
                        mm.then_inc(S["ot_full"], 1)

                def project_out(s):
                    for w in range(2):
                        m = (n * SEQS + s) * 2 + w
                        pe.wait_ge(S["ot_split"], m + 1)
                        dst = ps_q[:, s, w * D:(w + 1) * D]
                        for c in range(IC):
                            pe.matmul(dst, ot_hi[:, w, c, :], wo_hi[:, c, :], start=(w == 0 and c == 0), stop=False, skip_group_check=True)
                            pe.matmul(dst, ot_hi[:, w, c, :], wo_lo[:, c, :], start=False, stop=False, skip_group_check=True)
                            mm = pe.matmul(dst, ot_lo[:, w, c, :], wo_hi[:, c, :], start=False, stop=(w == 1 and c == IC - 1), skip_group_check=True)
                    mm.then_inc(S["y_full"], 1)

                for t in range(GT):
                    project(t)
                    if t >= 1:
                        turn(t - 1)
                turn(GT - 1)
                for s in range(SEQS):
                    if s == 0:
                        pe.wait_ge(S["qk_read"], 2 * (n * GT + GT) + 1)
                    for h in range(H + 2):
                        if h < H:
                            scores(s, h)
                        if 1 <= h <= H:
                            turn_p(s, h - 1)
                        if h >= 2:
                            values(s, h - 2)
                    turn_o(s)
                    project_out(s)

                pe.wait_ge(S["xn"], n + 2)
                turn_x().then_inc(S["t2_full"], 1)
                pe.wait_ge(S["split_b"], l + 2)
                pe.wait_ge(S["split2"], n * DC + DC + 1)
                pe.wait_ge(S["x_mid"], n * SEQS + SEQS + 1)

                def hidden(j):
                    m = n * FC + j
                    pe.wait_ge(S["gated"], m + 1)
                    for u, (dst, full) in enumerate(((val_bank[j % 2], "a_full"), (gate_bank[j % 2], "g_full"))):
                        cols = slice(j * P, (j + 1) * P)
                        for c in range(DC):
                            pe.matmul(dst, w1_hi[:, c, u, cols], nh[:, c, :], start=(c == 0), stop=False)
                            pe.matmul(dst, w1_lo[:, c, u, cols], nh[:, c, :], start=False, stop=False)
                            mm = pe.matmul(dst, w1_hi[:, c, u, cols], nl[:, c, :], start=False, stop=(c == DC - 1))
                        mm.then_inc(S[full], 1)

                def output(j):
                    m = n * FC + j
                    pe.wait_ge(S["h_split"], m + 2)
                    for t in range(GT):
                        tok = slice(t * P, (t + 1) * P)
                        dst = ps_o[:, t // 2, (t % 2) * D:(t % 2 + 1) * D]
                        pe.matmul(dst, h_hi[:, j % 2, tok], w2_hi[:, j, :], start=(j == 0 and t % 2 == 0), stop=False, skip_group_check=True)
                        pe.matmul(dst, h_hi[:, j % 2, tok], w2_lo[:, j, :], start=False, stop=False, skip_group_check=True)
                        mm = pe.matmul(dst, h_lo[:, j % 2, tok], w2_hi[:, j, :], start=False, stop=(j == FC - 1 and t % 2 == 1), skip_group_check=True)
                    mm.then_inc(S["h_used"], 1)

                for j in range(FC + 1):
                    if j < FC:
                        hidden(j)
                    if j >= 1:
                        output(j - 1)

            for s in ("split2 qk_read v_done qt_done kt_done o_done ss_done pv_done ri y_full xn x_mid h_split split_b t2_full "
                      "rn_done s_full ot_full").split():
                pe.sem_inc(S[s], 1)
            pe.sem_inc(S["sm_done"], 2)
            pe.sem_inc(S["pt_done"], 2)
            pe.sem_inc(S["gated"], 2)
            pe.wait_ge(S["ident"], 2)
            pe.wait_ge(S["fill"], 1)
            with pe.Fori(0, L) as l:
                with pe.Fori(0, NG) as g:
                    step(l, g)

        @block.scalar
        def _(act):
            def step(l, g):
                n = l * NG + g
                act.wait_ge(S["t1_full"], n + 1)
                act.activation(nh[:, 0, :], ps_d[:, 0, :], ACT.Copy).then_inc(S["nh1"], 1)
                act.activation(nh[:, 1, :].rearrange("p (s t) -> p s t", s=SEQS)[:, :, 1:2 * P],
                               ps_d[:, 1, :].rearrange("p (s t) -> p s t", s=SEQS)[:, :, 0:2 * P - 1], ACT.Copy)
                act.activation(nh[:, 1, :].rearrange("p (s t) -> p s t", s=SEQS)[:, :, 0:1], zeros, ACT.Copy).then_inc(S["nh1"], 1)

                def squares(t):
                    m = n * GT + t
                    act.wait_ge(S["ss_done"], 2 * m + 1)
                    act.wait_ge(S["q_full"], m + 1)
                    act.activation(sq[:, 0, :], ps_q[:, 0, :], ACT.Square).then_inc(S["sq_q"], 1)
                    act.wait_ge(S["k_full"], m + 1)
                    act.activation(sq[:, 1, :], ps_q[:, 1, :], ACT.Square).then_inc(S["sq_k"], 1)
                    act.wait_ge(S["v_full"], m + 1)
                    act.wait_ge(S["pv_done"], n * NH + 1)
                    act.activation(v[:, t, :], ps_q[:, 2, :], ACT.Copy).then_inc(S["v_done"], 1)

                def turned(t):
                    m = n * GT + t
                    act.wait_ge(S["s_full"], 2 * m + 2)
                    act.activation(qt[:, :, t * P:(t + 1) * P], ps_d[:, 0, :].rearrange("p (c t) -> p c t", t=P), ACT.Copy).then_inc(S["qt_done"], 1)

                for t in range(GT):
                    squares(t)
                    if t >= 1:
                        turned(t - 1)
                turned(GT - 1)
                for s in range(SEQS):
                    act.wait_ge(S["ri"], n * SEQS + s + 1)
                    for h in range(H):
                        m = n * NH + s * H + h
                        act.wait_ge(S["sm_done"], m + 3)
                        act.wait_ge(S["p_full"], m + 1)
                        act.activation(pr[:, h % 2, 0:P], sm[:, h % 2, 0:P], ACT.Exp, scale=-1.0,
                                       bias=mx[:, s * H + h, 0:1], accum_out=rsum[:, 0, h:h + 1])
                        act.activation(pr[:, h % 2, P:SC], sm[:, h % 2, P:SC], ACT.Exp, scale=-1.0,
                                       bias=mx[:, s * H + h, 1:2], accum_out=rsum[:, 1, h:h + 1]).then_inc(S["p_done"], 1)
                    for w in range(2):
                        m = (n * SEQS + s) * 2 + w
                        act.wait_ge(S["ot_full"], m + 2)
                        act.wait_ge(S["y_full"], n * SEQS + s + 1)
                        act.activation(ot_hi[:, w, :, :].rearrange("p c t -> p (c t)"), ps_d[:, w, :], ACT.Copy).then_inc(S["ot_h"], 1)
                act.wait_ge(S["x_mid"], n * SEQS + SEQS + 1)
                act.wait_ge(S["xn"], n + 1)
                xg = X[:, ds(g * GT, GT), :]
                act.dma_start(xs[1:P, :, :], xg[0:P - 1, :, P:D]).then_inc(S["shifted"], 16)
                act.dma_start(xs[0:1, :, :].rearrange("p (s t) d -> p s t d", s=SEQS)[:, :, 1, :],
                              xg[P - 1:P, :, P:D].rearrange("p (s t) d -> p s t d", s=SEQS)[:, :, 0, :]).then_inc(S["shifted"], 16)
                act.wait_ge(S["t2_full"], n + 2)
                for c in range(DC):
                    act.activation(nf[:, c, :], ps_d[:, c, :], ACT.Identity, bias=ln_cur[:, 1, c:c + 1], scale=ln_cur[:, 0, c:c + 1])
                    act.activation(nh[:, c, :], ps_d[:, c, :], ACT.Identity, bias=ln_cur[:, 1, c:c + 1], scale=ln_cur[:, 0, c:c + 1]).then_inc(S["nf_done"], 1)
                for j in range(FC):
                    m = n * FC + j
                    act.wait_ge(S["g_full"], m + 1)
                    act.wait_ge(S["gated"], m + 1)
                    act.activation(gate[:, j % 2, :], gate_bank[j % 2], ACT.Gelu, bias=b1_cur[:, 1, j:j + 1]).then_inc(S["gate_done"], 1)
                    act.wait_ge(S["gated"], m + 3)
                    act.wait_ge(S["h_used"], m + 1)
                    act.activation(h_hi[:, j % 2, :], hid[:, j % 2, :], ACT.Copy).then_inc(S["h_hi"], 1)

            zeros = zer[:, :].rearrange("p (s t) -> p s t", s=SEQS)
            act.sem_inc(S["p_full"], 2)
            act.sem_inc(S["h_used"], 2)
            act.wait_ge(S["vec"], ALLV)
            act.wait_ge(S["fill"], 1)
            with act.Fori(0, L) as l:
                act.wait_ge(S["raw_a"], l * 32 + 32)
                act.wait_ge(S["x_mid"], l * NG * SEQS + 1)
                act.activation(qkv_hi[:, :, :], raw_qkv, ACT.Copy)
                act.activation(wo_hi[:, :, :], raw_o, ACT.Copy).then_inc(S["hi_a"], 1)
                act.wait_ge(S["h_split"], l * NG * FC + 1)
                act.activation(ln_cur[:, :, :], ln_all[:, :, ds(l * DC, DC)], ACT.Copy)
                act.activation(b1_cur[:, :, :], b1_all[:, ds(l, 1), :, :].rearrange("p a u c -> p (a u) c"), ACT.Copy).then_inc(S["cur"], 1)
                act.wait_ge(S["cur"], l + 1)
                act.wait_ge(S["raw_b"], l * 64 + 64)
                act.wait_ge(S["h_used"], l * NG * FC + 2)
                act.activation(w1_hi[:, :, :, 0:HID].rearrange("p c u n -> p (c u) n"), raw_1[:, :, :, 0:HID].rearrange("p c u n -> p (c u) n"), ACT.Copy)
                act.activation(w2_hi[0:LAST, FC - 1, :], raw_2[0:LAST, FC - 1, :], ACT.Copy)
                act.activation(w2_hi[:, 0:FC - 1, :], raw_2[:, 0:FC - 1, :], ACT.Copy).then_inc(S["hi_b"], 1)
                with act.Fori(0, NG) as g:
                    step(l, g)

        @block.vector
        def _(dve):
            def step(l, g):
                n = l * NG + g
                dve.wait_ge(S["x_ready"], n + 1)
                dve.wait_ge(S["t2_full"], n + 1)
                dve.tensor_copy(xn[:, :, :], X[:, ds(g * GT, GT), :]).then_inc(S["staged"], 1)
                dve.wait_ge(S["nh1"], n * DC + 1)
                dve.tensor_tensor(nl[:, 0, :], ps_d[:, 0, :], nh[:, 0, :].bitcast(F32), ALU.subtract).then_inc(S["split1"], 1)
                dve.wait_ge(S["nh1"], n * DC + 2)
                late = nl[:, 1, :].rearrange("p (s t) -> p s t", s=SEQS)
                dve.tensor_tensor(late[:, :, 1:2 * P], ps_d[:, 1, :].rearrange("p (s t) -> p s t", s=SEQS)[:, :, 0:2 * P - 1],
                                  nh[:, 1, :].bitcast(F32).rearrange("p (s t) -> p s t", s=SEQS)[:, :, 1:2 * P], ALU.subtract)
                dve.tensor_copy(late[:, :, 0:1], zer[:, :].rearrange("p (s t) -> p s t", s=SEQS)).then_inc(S["split1"], 1)

                def rotate(t):
                    m = n * GT + t
                    for i, full in enumerate(("sq_q", "sq_k")):
                        dve.wait_ge(S[full], m + 1)
                        dve.wait_ge(S["rn_done"], m + 1)
                        dve.tensor_reduce(ss[:, i, :], sq[:, i, :].rearrange("p (h d) -> p h d", d=HD), AX.X, ALU.add).then_inc(S["ss_done"], 1)
                        src = ps_q[:, i, :].rearrange("p (h d) -> p h d", d=HD)
                        src4 = ps_q[:, i, :].rearrange("p (h u d) -> p h u d", u=2, d=HD // 2)
                        cs = tab[:, 2 * i, t % 2, :].unsqueeze(1).broadcast_to([P, H, HD])
                        sn = tab[:, 2 * i + 1, t % 2, :].rearrange("p (u d) -> p u d", u=2)
                        if i == 0:
                            dve.wait_ge(S["s_full"], 2 * m + 1)
                        dve.tensor_tensor(m1[:, i, :].rearrange("p (h d) -> p h d", d=HD), src, cs, ALU.mult)
                        dst = m2[:, i, :].rearrange("p (h u d) -> p h u d", u=2, d=HD // 2)
                        for u in range(2):
                            ins = dve.tensor_tensor(dst[:, :, u, :], src4[:, :, 1 - u, :], sn[:, u, :].unsqueeze(1).broadcast_to([P, H, HD // 2]), ALU.mult)
                        ins.then_inc(S["qk_read"], 1)
                    dve.wait_ge(S["ss_done"], 2 * m + 3)
                    dve.tensor_scalar(sc[:, :, :], ss[:, :, :], 1e-24, None, ALU.max).then_inc(S["sc_done"], 1)

                def turned(t):
                    m = n * GT + t
                    dve.wait_ge(S["s_full"], 2 * m + 3)
                    dve.tensor_copy(kt[:, :, t * P:(t + 1) * P], ps_d[:, 1, :].rearrange("p (c t) -> p c t", t=P)).then_inc(S["kt_done"], 1)

                for t in range(GT):
                    rotate(t)
                    if t >= 1:
                        turned(t - 1)
                turned(GT - 1)

                def soft(s, h):
                    m = n * NH + s * H + h
                    reach(dve, S["d_full"], m + 1)
                    dve.wait_ge(S["p_done"], m + 1)
                    dve.tensor_tensor_reduce(sm[:, h % 2, 0:P], ps_d[:, h % 2, 0:P], mask[:, 0:P], -1.0, -NEG, ALU.add, ALU.min,
                                             mx[:, s * H + h, 0:1])
                    dve.tensor_tensor_reduce(sm[:, h % 2, P:SC], ps_d[:, h % 2, P:SC], mask[:, P:SC], -1.0, -NEG, ALU.add, ALU.min,
                                             mx[:, s * H + h, 1:2]).then_inc(S["sm_done"], 1)

                def turned_p(s, h):
                    m = n * NH + s * H + h
                    dve.wait_ge(S["p_full"], m + 3)
                    dve.tensor_copy(pt[:, h % 2, :], ps_p[:, 0, 0:SC]).then_inc(S["pt_done"], 1)

                for s in range(SEQS):
                    for h in range(H + 1):
                        if h < H:
                            soft(s, h)
                        if h >= 1:
                            if h >= 3 or s == 1:
                                dve.wait_ge(S["pv_done"], n * NH + s * H + h - 1 if h >= 2 else n * NH + s * H + 1)
                            turned_p(s, h - 1)
                    q = n * SEQS + s
                    dve.wait_ge(S["p_done"], n * NH + s * H + H + 2)
                    dve.reciprocal(rinv[:, :, :], rsum[:, :, :]).then_inc(S["ri"], 1)
                    dve.wait_ge(S["ri"], q + 2)
                    dve.wait_ge(S["pv_done"], n * NH + s * H + H + 1)
                    dve.wait_ge(S["ot_full"], 2 * q + 1)
                    for w in range(2):
                        dve.tensor_tensor(o[:, w, :].rearrange("p (h d) -> p h d", d=HD), ps_o[:, w, :].rearrange("p (h d) -> p h d", d=HD),
                                          rinv[:, w, :].unsqueeze(2).broadcast_to([P, H, HD]), ALU.mult).then_inc(S["o_done"], 1)
                    for w in range(2):
                        dve.wait_ge(S["ot_h"], 2 * q + w + 1)
                        dve.tensor_tensor(ot_lo[:, w, :, :].rearrange("p c t -> p (c t)"), ps_d[:, w, :],
                                          ot_hi[:, w, :, :].rearrange("p c t -> p (c t)").bitcast(F32), ALU.subtract).then_inc(S["ot_split"], 1)
                    dve.wait_ge(S["y_full"], q + 2)
                    dve.tensor_tensor(x2(g, s), ps_q[:, s, :], x2(g, s), ALU.add).then_inc(S["x_mid"], 1)

                reach(dve, S["x_mid"], n * SEQS + SEQS + 1)
                for t in range(GT):
                    dve.bn_stats(st[:, t, 0, :], xt(g, t)[:, 0:P])
                reach(dve, S["shifted"], n * 32 + 32)
                for t in range(GT):
                    ins = dve.bn_stats(st[:, t, 1, :], xs[:, t, :])
                ins.then_inc(S["st"], 1)
                reach(dve, S["st"], n + 1)
                for t in range(GT):
                    ins = dve.bn_aggr(mv[:, t, :], st[:, t, :, :].rearrange("p a b -> p (a b)"))
                ins.then_inc(S["mv"], 1)
                dve.wait_ge(S["mv"], n + 1)
                dve.tensor_scalar(ve[:, :], mv[:, :, 1], EPS, None, ALU.add).then_inc(S["ve"], 1)
                dve.wait_ge(S["rs"], n + 1)
                dve.wait_ge(S["t1_full"], n + 1)
                for t in range(GT):
                    dve.tensor_scalar(xn[:, t, 0:P], xt(g, t)[:, 0:P], mv[:, t, 0:1], rs[:, t:t + 1], ALU.subtract, ALU.mult)
                    ins = dve.tensor_scalar(xn[:, t, P:D], xs[:, t, :], mv[:, t, 0:1], rs[:, t:t + 1], ALU.subtract, ALU.mult)
                ins.then_inc(S["xn"], 1)
                for c in range(DC):
                    dve.wait_ge(S["nf_done"], n * DC + c + 1)
                    dve.tensor_tensor(nl[:, c, :], nf[:, c, :], nh[:, c, :].bitcast(F32), ALU.subtract).then_inc(S["split2"], 1)

                def gated(j):
                    m = n * FC + j
                    dve.wait_ge(S["a_full"], m + 1)
                    dve.wait_ge(S["gate_done"], m + 1)
                    dve.wait_ge(S["h_split"], m) if j >= 2 else dve.wait_ge(S["h_split"], n * FC + 1)
                    dve.scalar_tensor_tensor(hid[:, j % 2, :], val_bank[j % 2], b1_cur[:, 0, j:j + 1], gate[:, j % 2, :],
                                             ALU.add, ALU.mult).then_inc(S["gated"], 1)

                def lo_part(j):
                    m = n * FC + j
                    dve.wait_ge(S["h_hi"], m + 1)
                    dve.tensor_tensor(h_lo[:, j % 2, :], hid[:, j % 2, :], h_hi[:, j % 2, :].bitcast(F32), ALU.subtract).then_inc(S["h_split"], 1)

                for j in range(FC):
                    gated(j)
                    lo_part(j)
                dve.wait_ge(S["xb"], n + 1)
                dve.wait_ge(S["h_used"], n * FC + FC + 2)
                for s in range(SEQS):
                    ins = dve.tensor_tensor(x2(g, s), ps_o[:, s, :], x2(g, s), ALU.add)
                ins.then_inc(S["x_ready"], 1)

            dve.sem_inc(S["p_done"], 2)
            dve.memset(neghalf[:, :], -0.5).then_inc(S["padp"], 1)
            dve.memset(b1_all[:, :, :, :], 0.0).then_inc(S["pad"], 1)
            dve.memset(zer[:, :], 0.0)
            dve.memset(xs[0:1, :, :], 0.0)
            for w in (w1_hi, w1_lo):
                dve.memset(w[:, :, :, HID:HIDP].bitcast(F32), 0.0)
            for w in (w2_hi, w2_lo):
                dve.memset(w[:, FC - 1, :].bitcast(F32), 0.0)
            dve.memset(mx[:, :, :], 0.0).then_inc(S["fill"], 1)
            dve.wait_ge(S["fill"], 1)
            for g in range(NG):
                for t in range(GT):
                    ins = dve.bn_stats(st[:, t, 0, :], X[:, GT * g + t, :])
                ins.then_inc(S["x0_st"], 1)
                dve.wait_ge(S["x0_st"], g + 1)
                for t in range(GT):
                    ins = dve.bn_aggr(mv[:, t, :], st[:, t, 0, :])
                ins.then_inc(S["x0_mv"], 1)
                dve.wait_ge(S["x0_mv"], g + 1)
                dve.tensor_scalar(ve[:, :], mv[:, :, 1], EPS, None, ALU.add).then_inc(S["x0_ve"], 1)
                dve.wait_ge(S["x0_rs"], g + 1)
                dve.wait_ge(S["h_out"], 16 * NG)
                for t in range(GT):
                    xg = X[:, GT * g + t, :]
                    ins = dve.tensor_scalar(xg, xg, mv[:, t, 0:1], rs[:, t:t + 1], ALU.subtract, ALU.mult)
                ins.then_inc(S["x_ready"], 1)
                dve.wait_ge(S["x_ready"], g + 1)
            dve.wait_ge(S["vec"], ALLV)
            with dve.Fori(0, L) as l:
                dve.wait_ge(S["hi_a"], l + 1)
                dve.tensor_tensor(qkv_lo[:, :, :], raw_qkv, qkv_hi[:, :, :].bitcast(F32), ALU.subtract)
                dve.tensor_tensor(wo_lo[:, :, :], raw_o, wo_hi[:, :, :].bitcast(F32), ALU.subtract).then_inc(S["split_a"], 1)
                dve.wait_ge(S["qk_read"], l * NG * GT * 2 + 1)
                for i in range(2):
                    for u in range(2):
                        ins = dve.tensor_tensor(tab[:, 2 * i + u, :, :], rot[:, 2 * i + u, :, :],
                                                scl[:, i, u, ds(l * HD, HD)].unsqueeze(1).broadcast_to([P, 2, HD]), ALU.mult)
                ins.then_inc(S["tab"], 1)
                reach(dve, S["tab"], l + 1)
                with dve.Fori(0, NG) as g:
                    step(l, g)
            for g in range(NG):
                dve.wait_ge(S["h_in"], 16 * g + 16)
                xg = X[:, GT * g:GT * g + GT, :]
                dve.tensor_tensor(xg, xg, hres[:, :, :], ALU.add).then_inc(S["fin"], 1)

        @block.gpsimd
        def _(pool):
            def step(l, g):
                n = l * NG + g
                for t in range(GT):
                    m = n * GT + t
                    pool.wait_ge(S["sc_done"], m + 1)
                    pool.tensor_tensor(rn[:, :, :].rearrange("p a h -> p (a h)"), sc[:, :, :].rearrange("p a h -> p (a h)"), neghalf[:, :], ALU.pow).then_inc(S["rn_done"], 1)
                    for i in range(2):
                        pool.tensor_tensor(m1[:, i, :], m1[:, i, :], m2[:, i, :], ALU.add).then_inc(S["rota"], 1)
                    for i in range(2):
                        pool.wait_ge(S["rota"], 2 * m + 1 + i)
                        if i == 0:
                            pool.wait_ge(S["rn_done"], m + 2)
                        mm = m1[:, i, :].rearrange("p (h d) -> p h d", d=HD)
                        pool.tensor_tensor(mm, mm, rn[:, i, :].unsqueeze(2).broadcast_to([P, H, HD]), ALU.mult).then_inc(S["roted"], 1)
                pool.wait_ge(S["ve"], n + 1)
                pool.tensor_tensor(rs[:, :], ve[:, :], neghalf[:, 0:GT], ALU.pow).then_inc(S["rs"], 1)
                reach(pool, S["xn"], n + 2)
                for t in range(GT):
                    ins = pool.tensor_tensor(xt(g, t), xt(g, t), b2_all[:, ds(l * D, D)], ALU.add)
                ins.then_inc(S["xb"], 1)

            pool.memset(ident[:, :], 0.0).then_inc(S["ident"], 1)
            pool.memset(mask[:, :], 0.0).then_inc(S["maskz"], 1)
            pool.wait_ge(S["ident"], 1)
            pool.affine_select(out=ident[:, :], in_=ident[:, :], compare_op=ALU.not_equal, fill=1.0, base=0,
                               pattern=[[-1, P]], channel_multiplier=1).then_inc(S["ident"], 1)
            pool.wait_ge(S["maskz"], 1)
            for i, sign in ((0, 1), (1, -1), (2, 1)):
                m = mask[:, i * P:(i + 1) * P]
                ins = pool.affine_select(out=m, in_=m, compare_op=ALU.is_ge, fill=NEG, base=0, pattern=[[-sign, P]], channel_multiplier=sign)
            ins.then_inc(S["mask"], 1)
            pool.wait_ge(S["padp"], 1)
            for g in range(NG):
                pool.wait_ge(S["x0_ve"], g + 1)
                pool.tensor_tensor(rs[:, :], ve[:, :], neghalf[:, 0:GT], ALU.pow).then_inc(S["x0_rs"], 1)
            pool.wait_ge(S["vec"], ALLV)
            with pool.Fori(0, L) as l:
                pool.wait_ge(S["hi_b"], l + 1)
                pool.tensor_tensor(w1_lo[:, :, :, 0:HID].rearrange("p c u n -> p (c u) n"), raw_1[:, :, :, 0:HID].rearrange("p c u n -> p (c u) n"),
                                   w1_hi[:, :, :, 0:HID].rearrange("p c u n -> p (c u) n").bitcast(F32), ALU.subtract)
                pool.tensor_tensor(w2_lo[0:LAST, FC - 1, :], raw_2[0:LAST, FC - 1, :], w2_hi[0:LAST, FC - 1, :].bitcast(F32), ALU.subtract)
                pool.tensor_tensor(w2_lo[:, 0:FC - 1, :], raw_2[:, 0:FC - 1, :], w2_hi[:, 0:FC - 1, :].bitcast(F32), ALU.subtract).then_inc(S["split_b"], 1)
                with pool.Fori(0, NG) as g:
                    step(l, g)
            for g in range(NG):
                if g:
                    pool.wait_ge(S["fin"], g)
                else:
                    pool.wait_ge(S["x_ready"], NG + L * NG)
                pool.dma_start(hres[:, :, :], out_v[:, GT * g:GT * g + GT, :]).then_inc(S["h_in"], 16)
                pool.wait_ge(S["fin"], g + 1)
                pool.dma_start(out_v[:, GT * g:GT * g + GT, :], X[:, GT * g:GT * g + GT, :]).then_inc(S["stored"], 16)
            pool.wait_ge(S["stored"], 16 * NG)


def program(nc, dram, out, phases=3):
    def run(phase, *args):
        sems = []
        phase(nc, sems, X, dram, *args)
        nc.clear_and_free_semaphores(sems)
        nc.all_engine_barrier()

    with ExitStack() as ctx:
        ctx.enter_context(nc.allow_non_contiguous_dma(reason="short vectors, loaded once"))
        X = ctx.enter_context(nc.sbuf_tensor("X", [P, NT, D], F32))
        run(tower_phase)
        if phases >= 2:
            run(attention_phase)
        if phases >= 3:
            run(window_phase, out)
            return
        s_out = ctx.enter_context(nc.semaphore("s_out"))
        with nc.Block() as block:
            @block.sync
            def _(sp):
                sp.dma_start(out.rearrange("s (t p) d -> p (s t) d", p=P), X[:, :, :]).then_inc(s_out, 16)
                sp.wait_ge(s_out, 16)


_INS = ["x", "L0_tok_emb", "L0_tok_pos_emb", "L0_tok_A_diag", "L0_tok_B", "L0_tok_C", "L0_tok_D", "L0_tok_w1", "L0_tok_b1",
        "L0_tok_w2", "L0_tok_b2", "L0_tok_ln1_s", "L0_tok_ln1_b", "L0_tok_ln2_s", "L0_tok_ln2_b", "L0_tok_lnf_s", "L0_tok_lnf_b",
        "L0_attn_Wq", "L0_attn_Wk", "L0_attn_Wv", "L0_attn_Wo", "L0_attn_gamma", "L0_ffn_wqkv", "L0_ffn_q_scale", "L0_ffn_k_scale",
        "L0_ffn_wo", "L0_ffn_ln_g", "L0_ffn_ln_b", "L0_ffn_w1", "L0_ffn_b1", "L0_ffn_w2", "L0_ffn_b2"]


def kernel(**inputs):
    import concourse.bacc as bacc
    from concourse.bass_utils import run_bass_kernel_spmd

    nc = bacc.Bacc("TRN2", target_bir_lowering=False, num_devices=1)
    arrays, dram = {}, {}
    for name, a in {**{n: inputs[n] for n in _INS}, **constants()}.items():
        a = np.ascontiguousarray(a)
        arrays[f"in_{name}"] = a
        dram[name] = nc.dram_tensor(f"in_{name}", a.shape, mybir.dt.from_np(a.dtype), kind="ExternalInput").ap()
    out = nc.dram_tensor("out", (8, 2 * P, D), F32, kind="ExternalOutput").ap()
    program(nc, dram, out)
    return run_bass_kernel_spmd(nc, [arrays], core_ids=[0]).results[0]["out"]
```

```python
import concourse.bass as bass
from concourse import mybir
from contextlib import ExitStack
import numpy as np

F32 = mybir.dt.float32
F32R = mybir.dt.float32r
I32 = mybir.dt.int32
U32 = mybir.dt.uint32
ALU = mybir.AluOpType
ACT = mybir.ActivationFunctionType
AX = mybir.AxisListType
ds = bass.ds

P = 128
NT = 16
GT = 4
GTOK = GT * P
NG = NT // GT
D = 256
DC = D // P
EPS = 1e-5


def reach(eng, sem, value, sem2=None, value2=None):
    if not isinstance(value, int):
        value = eng.to_reg(value)
    if sem2 is not None and not isinstance(value2, int):
        value2 = eng.to_reg(value2)
    eng.wait_ge(sem, 1)
    eng.wait_ge(sem, value)
    if sem2 is not None:
        eng.wait_ge(sem2, value2)


def tower_phase(nc, sems, X, dram):
    L, S, F = 4, 64, 1024
    FC = F // P
    V = dram["L0_tok_emb"].shape[0]
    STEPS = NG
    VECS = 8

    with ExitStack() as ctx:
        def sb(name, shape, dt=F32):
            return ctx.enter_context(nc.sbuf_tensor("t_" + name, shape, dt))

        def sem(name):
            sems.append(nc.alloc_semaphore("t_" + name))
            return sems[-1]

        raw_b = sb("raw_b", [P, DC, S])
        raw_c = sb("raw_c", [P, D])
        raw_d = sb("raw_d", [P, DC, D])
        raw_1 = sb("raw_1", [P, DC, F])
        raw_2 = sb("raw_2", [P, FC, D])
        b_cat = sb("b_cat", [P, DC, 2 * S], F32R)
        b_hiz = sb("b_hiz", [P, DC, 2 * S], F32R)
        c_hi = sb("c_hi", [P, D], F32R)
        c_lo = sb("c_lo", [P, D], F32R)
        d_hi = sb("d_hi", [P, DC, D], F32R)
        d_lo = sb("d_lo", [P, DC, D], F32R)
        w1_hi = sb("w1_hi", [P, DC, F], F32R)
        w1_lo = sb("w1_lo", [P, DC, F], F32R)
        w2_hi = sb("w2_hi", [P, FC, D], F32R)
        w2_lo = sb("w2_lo", [P, FC, D], F32R)
        ln_all = sb("ln_all", [P, 4, L * DC])
        ln_cur = sb("ln_cur", [P, 4, DC])
        fb_all = sb("fb_all", [P, L * FC])
        fb_cur = sb("fb_cur", [P, FC])
        b2_all = sb("b2_all", [P, L * D])
        a_raw = sb("a_raw", [P, L])
        a_all = sb("a_all", [P, L])
        keep = sb("keep", [P, GTOK])
        decay = sb("decay", [P, GTOK])
        neghalf = sb("neghalf", [P, GT])
        ids = sb("ids", [P, NT], I32)
        idm = sb("idm", [P, NT])
        idf = sb("idf", [P, NT])
        idx = sb("idx", [P, NT], U32)
        pos = sb("pos", [P, 2, D])
        ident = sb("ident", [P, P])
        st = [sb(f"st{k}", [P, GT, 6]) for k in (1, 2)]
        mv = [sb(f"mv{k}", [P, GT, 2]) for k in (1, 2)]
        ve = [sb(f"ve{k}", [P, GT]) for k in (1, 2)]
        rs = [sb(f"rs{k}", [P, GT]) for k in (1, 2)]
        xn = [sb(f"xn{k}", [P, GT, D]) for k in (1, 2)]
        nf = [sb(f"nf{k}", [P, DC, GTOK]) for k in (1, 2)]
        nh = [sb(f"nh{k}", [P, DC, GTOK], F32R) for k in (1, 2)]
        nl = [sb(f"nl{k}", [P, DC, GTOK], F32R) for k in (1, 2)]
        hs = sb("hs", [P, GTOK])
        hs_hi = sb("hs_hi", [P, GTOK], F32R)
        hs_lo = sb("hs_lo", [P, GTOK], F32R)
        gf = sb("gf", [P, 2, GTOK])
        g_hi = sb("g_hi", [P, 4, GTOK], F32R)
        g_lo = sb("g_lo", [P, 4, GTOK], F32R)

        def bank(name, n=1):
            return ctx.enter_context(nc.psum_tensor("t_" + name, [P, n, 512], F32))

        ps_t = bank("ps_t", 2)
        ps_u = bank("ps_u")
        ps_f = bank("ps_f", 2)
        ps_o = bank("ps_o", 2)

        s_ids, s_idm, s_idf, s_idx = sem("ids"), sem("idm"), sem("idf"), sem("idx")
        s_vec, s_pos, s_gather = sem("vec"), sem("pos"), [sem(f"gather{g}") for g in range(NG)]
        s_ident, s_keep, s_decay, s_sig = sem("ident"), sem("keep"), sem("decay"), sem("sig")
        raw_front, raw_w1, raw_w2 = sem("raw_front"), sem("raw_w1"), sem("raw_w2")
        front_hi, front_split = sem("front_hi"), sem("front_split")
        w1_h, w1_split, w2_h, w2_split = sem("w1_h"), sem("w1_split"), sem("w2_h"), sem("w2_split")
        cur_ready = sem("cur_ready")
        x_ready, xb_ready, xy_ready = sem("x_ready"), sem("xb_ready"), sem("xy_ready")
        st_done = [sem(f"st_done{k}") for k in (1, 2)]
        mv_done = [sem(f"mv_done{k}") for k in (1, 2)]
        ve_done = [sem(f"ve_done{k}") for k in (1, 2)]
        rs_done = [sem(f"rs_done{k}") for k in (1, 2)]
        xn_ready = [sem(f"xn_ready{k}") for k in (1, 2)]
        t_full = [sem(f"t_full{k}") for k in (1, 2)]
        nf_done = [sem(f"nf_done{k}") for k in (1, 2)]
        n_split = [sem(f"n_split{k}") for k in (1, 2)]
        pf_free = sem("pf_free")
        u_full, scanned, hs_hi_done, hs_split = sem("u_full"), sem("scanned"), sem("hs_hi_done"), sem("hs_split")
        y_full, f_full = sem("y_full"), sem("f_full")
        g_hi_done, g_split, g_used = sem("g_hi_done"), sem("g_split"), sem("g_used")

        def tiles(g):
            return range(GT * g, GT * g + GT)

        block = ctx.enter_context(nc.Block())

        def num(l, g):
            return l * STEPS + g

        def after(l, g, k):
            return (l + (g + k) // STEPS, (g + k) % STEPS)

        @block.sync
        def _(sp):
            sp.dma_start(ids[:, :], dram["x"].rearrange("s (t p) -> p (s t)", p=P)).then_inc(s_ids, 16)
            sp.dma_start(pos[:, :, :], dram["L0_tok_pos_emb"][0:2 * P, :].rearrange("(t p) d -> p t d", p=P)).then_inc(s_pos, 16)
            for l in range(L):
                if l >= 1:
                    sp.wait_ge(front_split, l)
                sp.dma_start(raw_b[:, :, :], dram["L0_tok_B"][l].rearrange("(c p) s -> p c s", p=P)).then_inc(raw_front, 16)
                sp.dma_start(raw_c[0:S, :], dram["L0_tok_C"][l]).then_inc(raw_front, 16)
                sp.dma_start(raw_c[S:2 * S, :], dram["L0_tok_C"][l]).then_inc(raw_front, 16)
                sp.dma_start(raw_d[:, :, :], dram["L0_tok_D"][l].rearrange("(c p) s -> p c s", p=P)).then_inc(raw_front, 16)
                if l >= 1:
                    sp.wait_ge(w1_split, FC * l)
                sp.dma_start(raw_1[:, :, :], dram["L0_tok_w1"][l].rearrange("(c p) s -> p c s", p=P)).then_inc(raw_w1, 16)
                if l >= 1:
                    sp.wait_ge(w2_split, FC * l)
                sp.dma_start(raw_2[:, :, :], dram["L0_tok_w2"][l].rearrange("(c p) s -> p c s", p=P)).then_inc(raw_w2, 16)

        @block.tensor
        def _(pe):
            def transposes(k, l, g):
                n = num(l, g)
                pe.wait_ge(xn_ready[k], n + 1)
                if k == 0:
                    pe.wait_ge(nf_done[1], n * DC + 1)
                for c in range(DC):
                    for t in range(GT):
                        mm = pe.transpose(ps_t[:, c, t * P:(t + 1) * P], xn[k][:, t, c * P:(c + 1) * P], ident[:, :])
                mm.then_inc(t_full[k], 1)

            def state_in(l, g):
                n = num(l, g)
                if g == 0:
                    pe.wait_ge(front_split, l + 1)
                pe.wait_ge(n_split[0], n * 2 + 2)
                pe.wait_ge(scanned, n + 1)
                for c in range(DC):
                    pe.matmul(ps_u[:, 0, :], b_cat[:, c, :], nh[0][:, c, :], start=(c == 0), stop=False)
                    mm = pe.matmul(ps_u[:, 0, :], b_hiz[:, c, :], nl[0][:, c, :], start=False, stop=(c == DC - 1))
                mm.then_inc(u_full, 1)

            def state_out(l, g):
                n = num(l, g)
                pe.wait_ge(hs_split, n + 1)
                for t in range(GT):
                    tok = slice(t * P, (t + 1) * P)
                    out = ps_t[:, t // 2, (t % 2) * D:(t % 2 + 1) * D]
                    passes = [(nh[0][:, c, tok], w[:, c, :]) for c in range(DC) for w in (d_hi, d_lo)]
                    passes += [(nl[0][:, c, tok], d_hi[:, c, :]) for c in range(DC)]
                    passes += [(hs_hi[:, tok], c_hi[:, :]), (hs_hi[:, tok], c_lo[:, :]), (hs_lo[:, tok], c_hi[:, :])]
                    for i, (a, w) in enumerate(passes):
                        mm = pe.matmul(out, a, w, start=(t % 2 == 0 and i == 0),
                                       stop=(t % 2 == 1 and i == len(passes) - 1), skip_group_check=True)
                mm.then_inc(y_full, 1)

            def hidden(l, g, j):
                n = num(l, g)
                if g == 0:
                    pe.wait_ge(w1_split, l * FC + j + 1)
                if j == 0:
                    pe.wait_ge(n_split[1], n * 2 + 2)
                pe.wait_ge(pf_free, n * FC + j + 1)
                col = slice(j * P, (j + 1) * P)
                for c in range(DC):
                    pe.matmul(ps_f[:, j % 2, :], w1_hi[:, c, col], nh[1][:, c, :], start=(c == 0), stop=False)
                    pe.matmul(ps_f[:, j % 2, :], w1_lo[:, c, col], nh[1][:, c, :], start=False, stop=False)
                    mm = pe.matmul(ps_f[:, j % 2, :], w1_hi[:, c, col], nl[1][:, c, :], start=False, stop=(c == DC - 1))
                mm.then_inc(f_full, 1)

            def output(l, g, j):
                n = num(l, g)
                if g == 0:
                    pe.wait_ge(w2_split, l * FC + j + 1)
                if j == 0:
                    pe.wait_ge(x_ready, n + NG)
                pe.wait_ge(g_split, n * FC + j + 3)
                for t in range(GT):
                    tok = slice(t * P, (t + 1) * P)
                    out = ps_o[:, t // 2, (t % 2) * D:(t % 2 + 1) * D]
                    pe.matmul(out, g_hi[:, j % 4, tok], w2_hi[:, j, :], start=(j == 0 and t % 2 == 0), stop=False, skip_group_check=True)
                    pe.matmul(out, g_hi[:, j % 4, tok], w2_lo[:, j, :], start=False, stop=False, skip_group_check=True)
                    mm = pe.matmul(out, g_lo[:, j % 4, tok], w2_hi[:, j, :], start=False,
                                   stop=(j == FC - 1 and t % 2 == 1), skip_group_check=True)
                mm.then_inc(g_used, 1)

            def step(l, g, front):
                nx = after(l, g, 1)
                hidden(l, g, 0)
                hidden(l, g, 1)
                if front:
                    transposes(0, *nx)
                output(l, g, 0)
                hidden(l, g, 2)
                if front:
                    state_in(*nx)
                output(l, g, 1)
                hidden(l, g, 3)
                output(l, g, 2)
                if front:
                    state_out(*nx)
                for j in range(4, FC):
                    hidden(l, g, j)
                    if j < FC - 1:
                        output(l, g, j - 1)
                if front:
                    transposes(1, *nx)
                output(l, g, FC - 2)
                output(l, g, FC - 1)

            for s in (t_full[0], t_full[1], nf_done[0], nf_done[1], scanned):
                pe.sem_inc(s, 1)
            pe.sem_inc(pf_free, 2)
            pe.wait_ge(s_ident, 2)
            transposes(0, 0, 0)
            state_in(0, 0)
            state_out(0, 0)
            transposes(1, 0, 0)
            with pe.Fori(0, L - 1) as l:
                for g in range(STEPS):
                    step(l, g, True)
            for g in range(STEPS):
                step(L - 1, g, g < STEPS - 1)

        @block.scalar
        def _(act):
            def spread(k, l, g):
                n = num(l, g)
                act.wait_ge(t_full[k], n + 2)
                for c in range(DC):
                    s = ln_cur[:, 2 * k, c:c + 1]
                    b = ln_cur[:, 2 * k + 1, c:c + 1]
                    act.activation(nf[k][:, c, :], ps_t[:, c, :], ACT.Identity, bias=b, scale=s)
                    ins = act.activation(nh[k][:, c, :], ps_t[:, c, :], ACT.Identity, bias=b, scale=s)
                    ins.then_inc(nf_done[k], 1)

            def state_hi(l, g):
                act.wait_ge(scanned, num(l, g) + 2)
                act.activation(hs_hi[:, :], hs[:, :], ACT.Copy).then_inc(hs_hi_done, 1)

            def gelu(l, g, j):
                n = num(l, g) * FC + j
                act.wait_ge(f_full, n + 1)
                act.wait_ge(g_used, n + 1)
                act.wait_ge(g_split, n + 1)
                act.activation(gf[:, j % 2, :], ps_f[:, j % 2, :], ACT.Gelu, bias=fb_cur[:, j:j + 1]).then_inc(pf_free, 1)
                act.wait_ge(pf_free, n + 3)
                act.activation(g_hi[:, j % 4, :], gf[:, j % 2, :], ACT.Copy).then_inc(g_hi_done, 1)

            def take_ln(l, count):
                act.activation(ln_cur[:, :, :], ln_all[:, :, ds(l * DC, DC)], ACT.Copy).then_inc(cur_ready, 1)
                act.wait_ge(cur_ready, count)

            def take_fb(l, count):
                act.activation(fb_cur[:, :], fb_all[:, ds(l * FC, FC)], ACT.Copy).then_inc(cur_ready, 1)
                act.wait_ge(cur_ready, count)

            def w1_hi_part(l, j, used):
                act.wait_ge(raw_w1, l * 16 + 16)
                if used is not None:
                    act.wait_ge(f_full, used)
                act.activation(w1_hi[:, :, j * P:(j + 1) * P], raw_1[:, :, j * P:(j + 1) * P], ACT.Copy).then_inc(w1_h, 1)

            def w2_hi_part(l, j, used):
                act.wait_ge(raw_w2, l * 16 + 16)
                if used is not None:
                    act.wait_ge(g_used, used)
                act.activation(w2_hi[:, j, :], raw_2[:, j, :], ACT.Copy).then_inc(w2_h, 1)

            def step(l, g, front):
                nx = after(l, g, 1)
                n = num(l, g) * FC
                prep = front and g == STEPS - 1
                if g == 0:
                    act.wait_ge(pf_free, n + 2)
                    take_fb(l, l * 2 + 2)
                if prep:
                    act.wait_ge(nf_done[1], num(l, g) * DC + DC + 1)
                    take_ln(l + 1, l * 2 + 3)
                for j in range(FC):
                    gelu(l, g, j)
                    if front and j == 1:
                        spread(0, *nx)
                    if front and j == 3:
                        state_hi(*nx)
                    if prep:
                        w1_hi_part(l + 1, j, n + j + 1)
                        if j >= 3:
                            w2_hi_part(l + 1, j - 3, n + 4 + j - 2)
                if front:
                    spread(1, *nx)
                if prep:
                    for j in range(FC - 3, FC):
                        w2_hi_part(l + 1, j, n + 4 + j + 1)

            act.sem_inc(g_used, 4)
            act.sem_inc(g_split, 2)
            act.wait_ge(s_vec, 16 * VECS)
            act.activation(a_all[:, :], a_raw[:, :], ACT.Sigmoid).then_inc(s_sig, 1)
            take_ln(0, 1)
            spread(0, 0, 0)
            for j in range(FC):
                w1_hi_part(0, j, None)
            state_hi(0, 0)
            spread(1, 0, 0)
            for j in range(FC):
                w2_hi_part(0, j, None)
            with act.Fori(0, L - 1) as l:
                for g in range(STEPS):
                    step(l, g, True)
            for g in range(STEPS):
                step(L - 1, g, g < STEPS - 1)


        @block.vector
        def _(dve):
            def grp(g):
                return X[:, GT * g:GT * g + GT, :]

            def stats(k, l, g):
                n = num(l, g)
                if k == 0:
                    reach(dve, x_ready, n + 1)
                else:
                    reach(dve, xy_ready, n + 1)
                for t in range(GT):
                    ins = dve.bn_stats(st[k][:, t, :], X[:, GT * g + t, :])
                ins.then_inc(st_done[k], 1)
                reach(dve, st_done[k], n + 1)
                for t in range(GT):
                    ins = dve.bn_aggr(mv[k][:, t, :], st[k][:, t, :])
                ins.then_inc(mv_done[k], 1)
                dve.wait_ge(mv_done[k], n + 1)
                dve.tensor_scalar(ve[k][:, :], mv[k][:, :, 1], EPS, None, ALU.add).then_inc(ve_done[k], 1)

            def norm(k, l, g):
                n = num(l, g)
                dve.wait_ge(rs_done[k], n + 1)
                dve.wait_ge(t_full[k], n + 1)
                for t in range(GT):
                    ins = dve.tensor_scalar(xn[k][:, t, :], X[:, GT * g + t, :], mv[k][:, t, 0:1], rs[k][:, t:t + 1],
                                            ALU.subtract, ALU.mult)
                ins.then_inc(xn_ready[k], 1)

            def spread_lo(k, l, g):
                n = num(l, g)
                for c in range(DC):
                    dve.wait_ge(nf_done[k], n * DC + c + 2)
                    dve.tensor_tensor(nl[k][:, c, :], nf[k][:, c, :], nh[k][:, c, :].bitcast(F32),
                                      ALU.subtract).then_inc(n_split[k], 1)

            def scan(l, g):
                n = num(l, g)
                dve.wait_ge(u_full, n + 1)
                dve.tensor_tensor_scan(hs[:, :], decay[:, :], ps_u[:, 0, :], 0.0, ALU.mult, ALU.add).then_inc(scanned, 1)

            def state_lo(l, g):
                n = num(l, g)
                dve.wait_ge(hs_hi_done, n + 1)
                dve.tensor_tensor(hs_lo[:, :], hs[:, :], hs_hi[:, :].bitcast(F32), ALU.subtract).then_inc(hs_split, 1)

            def add_state(l, g):
                n = num(l, g)
                dve.wait_ge(y_full, n + 1)
                for h in range(2):
                    x2 = X[:, GT * g + 2 * h:GT * g + 2 * h + 2, :].rearrange("p t d -> p (t d)")
                    ins = dve.tensor_tensor(x2, ps_t[:, h, :], x2, ALU.add)
                ins.then_inc(xy_ready, 1)

            def gelu_lo(l, g, j):
                n = num(l, g) * FC + j
                dve.wait_ge(g_hi_done, n + 1)
                dve.tensor_tensor(g_lo[:, j % 4, :], gf[:, j % 2, :], g_hi[:, j % 4, :].bitcast(F32),
                                  ALU.subtract).then_inc(g_split, 1)

            def add_output(l, g):
                n = num(l, g)
                dve.wait_ge(xb_ready, n + 1)
                dve.wait_ge(g_used, n * FC + FC + 4)
                for h in range(2):
                    x2 = X[:, GT * g + 2 * h:GT * g + 2 * h + 2, :].rearrange("p t d -> p (t d)")
                    ins = dve.tensor_tensor(x2, ps_o[:, h, :], x2, ALU.add)
                ins.then_inc(x_ready, 1)

            def set_decay(l, count):
                dve.tensor_scalar(decay[:, :], keep[:, :], a_all[:, ds(l, 1)], None, ALU.mult).then_inc(s_decay, 1)
                dve.wait_ge(s_decay, count)

            def step(l, g, front, ahead):
                nx, n2 = after(l, g, 1), after(l, g, 2)
                if front and g == STEPS - 1:
                    set_decay(l + 1, l + 2)
                gelu_lo(l, g, 0)
                gelu_lo(l, g, 1)
                if front:
                    spread_lo(0, *nx)
                gelu_lo(l, g, 2)
                if front:
                    scan(*nx)
                gelu_lo(l, g, 3)
                if front:
                    state_lo(*nx)
                gelu_lo(l, g, 4)
                if front:
                    add_state(*nx)
                    stats(1, *nx)
                gelu_lo(l, g, 5)
                if front:
                    norm(1, *nx)
                if ahead:
                    stats(0, *n2)
                gelu_lo(l, g, 6)
                if ahead:
                    norm(0, *n2)
                gelu_lo(l, g, 7)
                if front:
                    spread_lo(1, *nx)
                add_output(l, g)

            dve.wait_ge(s_ids, 16)
            dve.tensor_scalar(idm[:, :], ids[:, :], 0.0, float(V), ALU.is_lt, ALU.mult).then_inc(s_idm, 1)
            dve.wait_ge(s_idm, 1)
            dve.tensor_tensor(idf[:, :], ids[:, :], idm[:, :], ALU.add).then_inc(s_idf, 1)
            dve.wait_ge(s_idf, 1)
            dve.tensor_scalar(idx[:, :], idf[:, :], 0.0, float(V - 1), ALU.max, ALU.min).then_inc(s_idx, 1)
            dve.memset(keep[:, :], 1.0).then_inc(s_keep, 1)
            dve.wait_ge(s_keep, 1)
            dve.memset(keep[:, :].rearrange("p (s t) -> p s t", t=2 * P)[:, :, 0:1], 0.0).then_inc(s_keep, 1)
            dve.memset(neghalf[:, :], -0.5).then_inc(s_keep, 1)
            dve.memset(b_hiz[:, :, :].bitcast(F32), 0.0).then_inc(s_keep, 1)
            dve.wait_ge(s_sig, 1)
            dve.wait_ge(s_keep, 4)
            set_decay(0, 1)
            dve.wait_ge(s_pos, 16)
            for g in range(NG):
                dve.wait_ge(s_gather[g], 16 * GT)
                for h in range(2):
                    x2 = X[:, GT * g + 2 * h:GT * g + 2 * h + 2, :]
                    ins = dve.tensor_tensor(x2, x2, pos[:, :, :], ALU.add)
                ins.then_inc(x_ready, 1)
                if g == 0:
                    stats(0, 0, 0)
                    norm(0, 0, 0)
                    spread_lo(0, 0, 0)
            scan(0, 0)
            state_lo(0, 0)
            add_state(0, 0)
            stats(1, 0, 0)
            norm(1, 0, 0)
            stats(0, 0, 1)
            norm(0, 0, 1)
            spread_lo(1, 0, 0)
            with dve.Fori(0, L - 1) as l:
                for g in range(STEPS):
                    step(l, g, True, True)
            for g in range(STEPS):
                step(L - 1, g, g < STEPS - 1, g < STEPS - 2)

        @block.gpsimd
        def _(pool):
            def rstd(k, l, g):
                pool.wait_ge(ve_done[k], num(l, g) + 1)
                pool.tensor_tensor(rs[k][:, :], ve[k][:, :], neghalf[:, :], ALU.pow).then_inc(rs_done[k], 1)

            def add_bias(l, g):
                reach(pool, xn_ready[1], num(l, g) + 1)
                for t in tiles(g):
                    ins = pool.tensor_tensor(X[:, t, :], X[:, t, :], b2_all[:, ds(l * D, D)], ALU.add)
                ins.then_inc(xb_ready, 1)

            def split_front(l, first):
                pool.wait_ge(raw_front, l * 64 + 64)
                if not first:
                    reach(pool, y_full, l * STEPS)
                pool.tensor_copy(b_cat[:, :, 0:S], raw_b[:, :, :])
                pool.tensor_copy(b_hiz[:, :, 0:S], raw_b[:, :, :])
                pool.tensor_copy(c_hi[:, :], raw_c[:, :])
                pool.tensor_copy(d_hi[:, :, :], raw_d[:, :, :]).then_inc(front_hi, 1)
                pool.wait_ge(front_hi, l + 1)
                pool.tensor_tensor(b_cat[:, :, S:2 * S], raw_b[:, :, :], b_cat[:, :, 0:S].bitcast(F32), ALU.subtract)
                pool.tensor_tensor(c_lo[:, :], raw_c[:, :], c_hi[:, :].bitcast(F32), ALU.subtract)
                pool.tensor_tensor(d_lo[:, :, :], raw_d[:, :, :], d_hi[:, :, :].bitcast(F32), ALU.subtract).then_inc(front_split, 1)

            def w1_lo_part(l, j):
                pool.wait_ge(w1_h, l * FC + j + 1)
                col = slice(j * P, (j + 1) * P)
                pool.tensor_tensor(w1_lo[:, :, col], raw_1[:, :, col], w1_hi[:, :, col].bitcast(F32), ALU.subtract).then_inc(w1_split, 1)

            def w2_lo_part(l, j):
                pool.wait_ge(w2_h, l * FC + j + 1)
                pool.tensor_tensor(w2_lo[:, j, :], raw_2[:, j, :], w2_hi[:, j, :].bitcast(F32), ALU.subtract).then_inc(w2_split, 1)

            def step(l, g, front, ahead):
                nx, n2 = after(l, g, 1), after(l, g, 2)
                prep = front and g == STEPS - 1
                if prep:
                    for j in range(4):
                        w1_lo_part(l + 1, j)
                if front and g == STEPS - 2 and ahead:
                    split_front(l + 1, False)
                if front:
                    rstd(1, *nx)
                    add_bias(*nx)
                if ahead:
                    rstd(0, *n2)
                if prep:
                    for j in range(4, FC):
                        w1_lo_part(l + 1, j)
                    for j in range(FC):
                        w2_lo_part(l + 1, j)

            pool.memset(ident[:, :], 0.0).then_inc(s_ident, 1)
            pool.wait_ge(s_idx, 1)
            for t in range(NT):
                pool.indirect_dma_start(X[:, t, :], None, dram["L0_tok_emb"][:, :],
                                        bass.IndirectOffsetOnAxis(ap=idx[:, t:t + 1], axis=0)).then_inc(s_gather[t // GT], 16)
            pool.wait_ge(s_ident, 1)
            pool.affine_select(out=ident[:, :], in_=ident[:, :], compare_op=ALU.not_equal, fill=1.0, base=0,
                               pattern=[[-1, P]], channel_multiplier=1).then_inc(s_ident, 1)
            for k, name in enumerate(("L0_tok_ln1_s", "L0_tok_ln1_b", "L0_tok_ln2_s", "L0_tok_ln2_b")):
                pool.dma_start(ln_all[:, k, :], dram[name].rearrange("l (c p) -> p (l c)", p=P)).then_inc(s_vec, 16)
            pool.dma_start(fb_all[:, :], dram["L0_tok_b1"].rearrange("l (c p) -> p (l c)", p=P)).then_inc(s_vec, 16)
            pool.dma_start(b2_all[:, :], dram["L0_tok_b2"].rearrange("(a l) d -> a (l d)", a=1).broadcast_to([P, L * D])).then_inc(s_vec, 16)
            pool.dma_start(a_raw[0:S, :], dram["L0_tok_A_diag"].rearrange("l s -> s l")).then_inc(s_vec, 16)
            pool.dma_start(a_raw[S:2 * S, :], dram["L0_tok_A_diag"].rearrange("l s -> s l")).then_inc(s_vec, 16)
            pool.wait_ge(s_keep, 4)
            rstd(0, 0, 0)
            split_front(0, True)
            rstd(1, 0, 0)
            pool.wait_ge(s_vec, 16 * VECS)
            add_bias(0, 0)
            rstd(0, 0, 1)
            for j in range(FC):
                w1_lo_part(0, j)
            for j in range(FC):
                w2_lo_part(0, j)
            with pool.Fori(0, L - 1) as l:
                for g in range(STEPS):
                    step(l, g, True, True)
            for g in range(STEPS):
                step(L - 1, g, g < STEPS - 1, g < STEPS - 2)


def attention_phase(nc, sems, X, dram):
    H, HD = 16, 16
    ROW = 64
    HP = H // 2
    QUAD, HQ = 4, H // 4
    SCALE = HD ** -0.5
    SEQS = 2
    SCORES = 3 * P
    AHEAD = 4
    LAG = 3
    VECS = 3
    NS = SEQS * H

    with ExitStack() as ctx:
        def sb(name, shape, dt=F32):
            return ctx.enter_context(nc.sbuf_tensor("a_" + name, shape, dt))

        def sem(name):
            sems.append(nc.alloc_semaphore("a_" + name))
            return sems[-1]

        def bank(name, n=1):
            return ctx.enter_context(nc.psum_tensor("a_" + name, [P, n, 512], F32))

        raw_w = sb("raw_w", [P, DC, 3 * D])
        w_hi = sb("w_hi", [P, DC, 3 * D], F32R)
        w_lo = sb("w_lo", [P, DC, 3 * D], F32R)
        raw_o = sb("raw_o", [P, HQ, D])
        wo_hi = sb("wo_hi", [P, HQ, D], F32R)
        wo_lo = sb("wo_lo", [P, HQ, D], F32R)
        fs = sb("fs", [P, D])
        fb = sb("fb", [P, D])
        gam = sb("gam", [P, H])
        gsc = sb("gsc", [P, H])
        neghalf = sb("neghalf", [P, GT])
        ident = sb("ident", [P, P])
        st = sb("st", [P, GT, 6])
        mv = sb("mv", [P, GT, 2])
        ve = sb("ve", [P, GT])
        rs = sb("rs", [P, GT])
        xn = sb("xn", [P, GT, D])
        nh = sb("nh", [P, DC, GTOK], F32R)
        nl = sb("nl", [P, DC, GTOK], F32R)
        sq = sb("sq", [P, 2 * D])
        nrm = sb("nrm", [P, 2 * H])
        qs = [sb(f"qs{i}", [P, H, ROW], F32R) for i in range(2)]
        ks = [sb(f"ks{i}", [P, H, ROW], F32R) for i in range(2)]
        v = sb("v", [P, GT, H, 2 * HD])
        qt = sb("qt", [P, HP, GTOK], F32R)
        kt = sb("kt", [P, HP, GTOK], F32R)
        dist = sb("dist", [P, 2, SCORES])
        e = sb("e", [P, 4, SCORES])
        ot_hi = sb("ot_hi", [P, HQ, 2 * P], F32R)
        ot_lo = sb("ot_lo", [P, HQ, 2 * P], F32R)

        ps_t = bank("ps_t", 2)
        ps_p = bank("ps_p", 2)
        ps_qk, ps_v = ps_p[:, 0:1, :], ps_p[:, 1:2, :]
        ps_d = bank("ps_d", 2)
        ps_o = bank("ps_o", 2)
        ps_s = (ps_o, ps_p)

        s_w, s_wo, s_vec, s_zero, s_ident, s_gsc = (sem(x) for x in ("w", "wo", "vec", "zero", "ident", "gsc"))
        w_h, w_split, s_pad = sem("w_h"), sem("w_split"), sem("pad")
        st_done, mv_done, ve_done, rs_done, xn_ready = (sem(x) for x in ("st", "mv", "ve", "rs", "xn"))
        h_mul, h_ready = sem("h_mul"), sem("h_ready")
        t_full, nh_done, n_split = sem("t_full"), sem("nh_done"), sem("n_split")
        qk_full, v_full, sq_done, qk_hi, qk_read, v_done = (sem(x) for x in ("qk_full", "v_full", "sq_done", "qk_hi", "qk_read", "v_done"))
        nrm_done, nrm_hi, stacked, s_full, qt_done, kt_done = (sem(x) for x in ("nrm", "nrm_hi", "stacked", "s_full", "qt_done", "kt_done"))
        d_full, relu_done, exp_done, masked, pv_done = (sem(x) for x in ("d_full", "relu", "exp", "masked", "pv"))
        ot_h, ot_split, y_full, y_added = sem("ot_h"), sem("ot_split"), sem("y_full"), sem("y_added")

        block = ctx.enter_context(nc.Block())

        @block.sync
        def _(sp):
            for i, name in enumerate(("L0_attn_Wq", "L0_attn_Wk", "L0_attn_Wv")):
                sp.dma_start(raw_w[:, :, D * i:D * i + D], dram[name].rearrange("(c p) n -> p c n", p=P)).then_inc(s_w, 16)
            sp.dma_start(fs[:, :], dram["L0_tok_lnf_s"].rearrange("(a d) -> a d", a=1).broadcast_to([P, D])).then_inc(s_vec, 16)
            sp.dma_start(fb[:, :], dram["L0_tok_lnf_b"].rearrange("(a d) -> a d", a=1).broadcast_to([P, D])).then_inc(s_vec, 16)
            sp.dma_start(gam[:, :], dram["L0_attn_gamma"].rearrange("(a d) -> a d", a=1).broadcast_to([P, H])).then_inc(s_vec, 16)
            sp.wait_ge(s_zero, 1)
            wo = dram["L0_attn_Wo"].rearrange("(q j d) n -> j d q n", j=QUAD, d=HD)
            for j in range(QUAD):
                sp.dma_start(raw_o[32 * j:32 * j + HD, :, :], wo[j]).then_inc(s_wo, 16)

        @block.tensor
        def _(pe):
            def turn_x(g):
                pe.wait_ge(xn_ready, g * 2 + 2)
                for c in range(DC):
                    for t in range(GT):
                        mm = pe.transpose(ps_t[:, c, t * P:(t + 1) * P], xn[:, t, c * P:(c + 1) * P], ident[:, :])
                mm.then_inc(t_full, 1)

            def group(g, ahead):
                def project(t):
                    tok = slice(t * P, (t + 1) * P)
                    pe.wait_ge(qk_read, g * GT + t + 1)
                    for out, lo, hi, full in ((ps_qk[:, 0, :], 0, 2 * D, qk_full), (ps_v[:, 0, 0:D], 2 * D, 3 * D, v_full)):
                        if lo:
                            pe.wait_ge(v_done, g * GT + t + 1)
                        for c in range(DC):
                            pe.matmul(out, nh[:, c, tok], w_hi[:, c, lo:hi], start=(c == 0), stop=False)
                            pe.matmul(out, nh[:, c, tok], w_lo[:, c, lo:hi], start=False, stop=False)
                            mm = pe.matmul(out, nl[:, c, tok], w_hi[:, c, lo:hi], start=False, stop=(c == DC - 1))
                        mm.then_inc(full, 1)

                def turn(t):
                    pe.wait_ge(stacked, g * GT + t + 2)
                    pe.wait_ge(qt_done, g * GT + t + 1)
                    pe.wait_ge(kt_done, g * GT + t + 1)
                    for dst, src in ((ps_t, qs[t % 2]), (ps_d, ks[t % 2])):
                        for hp in range(HP):
                            mm = pe.transpose(dst[:, hp // 4, (hp % 4) * P:(hp % 4 + 1) * P],
                                              src[:, 2 * hp:2 * hp + 2, :].rearrange("p h r -> p (h r)").bitcast(F32), ident[:, :])
                        mm.then_inc(s_full, 1)

                def distances(i):
                    h = i % H
                    s = i // H
                    n = g * NS + i
                    if i == 0:
                        pe.wait_ge(qt_done, g * GT + GT + 1)
                        pe.wait_ge(kt_done, g * GT + GT + 1)
                    pe.wait_ge(relu_done, n + 1)
                    rows = slice(ROW * (h % 2), ROW * (h % 2) + ROW)
                    t0, t1 = 2 * s * P, (2 * s + 1) * P
                    pe.matmul(ps_d[:, h % 2, 0:2 * P], kt[rows, h // 2, t1:t1 + P], qt[rows, h // 2, t0:t0 + 2 * P], start=True, stop=True)
                    pe.matmul(ps_d[:, h % 2, 2 * P:3 * P], kt[rows, h // 2, t0:t0 + P], qt[rows, h // 2, t0:t0 + P],
                              start=True, stop=True).then_inc(d_full, 1)

                def values(i):
                    s, h = divmod(i, H)
                    if i == 0:
                        pe.wait_ge(y_added, g * SEQS + 1)
                    if i == H:
                        pe.wait_ge(qk_read, g * GT + GT + 1)
                        pe.wait_ge(v_done, g * GT + GT + 1)
                    pe.wait_ge(masked, g * NS + i + 1)
                    j, q = h % QUAD, h // QUAD
                    out = ps_s[s][32 * j:32 * j + 32, q // 2, (q % 2) * 2 * P:(q % 2 + 1) * 2 * P]
                    pe.matmul(out, v[:, 2 * s + 1, h, :], e[:, h % 4, 0:2 * P], start=True, stop=False, skip_group_check=True)
                    pe.matmul(out[:, 0:P], v[:, 2 * s, h, :], e[:, h % 4, 2 * P:3 * P], start=False, stop=True,
                              skip_group_check=True).then_inc(pv_done, 1)

                def project_out(s):
                    pe.wait_ge(ot_split, g * SEQS + s + 2)
                    for t in range(2):
                        out = ps_o[:, s, t * D:(t + 1) * D]
                        for q in range(HQ):
                            tok = slice(t * P, (t + 1) * P)
                            pe.matmul(out, ot_hi[:, q, tok], wo_hi[:, q, :], start=(t == 0 and q == 0), stop=False, skip_group_check=True)
                            pe.matmul(out, ot_hi[:, q, tok], wo_lo[:, q, :], start=False, stop=False, skip_group_check=True)
                            mm = pe.matmul(out, ot_lo[:, q, tok], wo_hi[:, q, :], start=False, stop=(t == 1 and q == HQ - 1), skip_group_check=True)
                    mm.then_inc(y_full, 1)

                pe.wait_ge(w_split, 2)
                pe.wait_ge(n_split, g * DC + DC)
                for t in range(GT):
                    project(t)
                    if t >= 1:
                        turn(t - 1)
                turn(GT - 1)
                for i in range(NS + AHEAD):
                    if i < NS:
                        distances(i)
                    if i >= AHEAD:
                        values(i - AHEAD)
                    if i == H + LAG + AHEAD:
                        project_out(0)
                if ahead:
                    turn_x(g + 1)
                project_out(1)

            for s in (y_added, qk_read, v_done, qt_done, kt_done, ot_split, nrm_done, s_full, y_full, t_full, stacked):
                pe.sem_inc(s, 1)
            pe.sem_inc(relu_done, 2)
            pe.wait_ge(s_ident, 2)
            pe.wait_ge(s_pad, 5)
            turn_x(0)
            with pe.Fori(0, NG - 1) as g:
                group(g, True)
            group(NG - 1, False)

        @block.scalar
        def _(act):
            def spread(g):
                act.wait_ge(t_full, g + 2)
                for c in range(DC):
                    act.activation(nh[:, c, :], ps_t[:, c, :], ACT.Copy).then_inc(nh_done, 1)

            def group(g, ahead):
                def stack(t):
                    n = g * GT + t
                    q = ps_qk[:, 0, 0:D].rearrange("p (h d) -> p h d", h=H)
                    k = ps_qk[:, 0, D:2 * D].rearrange("p (h d) -> p h d", h=H)
                    act.wait_ge(qk_full, n + 1)
                    act.wait_ge(nrm_done, n + 1)
                    act.activation(sq[:, :], ps_qk[:, 0, :], ACT.Square).then_inc(sq_done, 1)
                    act.wait_ge(s_full, (g * GT + max(t - 1, 0)) * 2 + 1)
                    act.activation(qs[t % 2][:, :, 0:HD], q, ACT.Copy)
                    act.activation(qs[t % 2][:, :, HD:2 * HD], q, ACT.Copy).then_inc(qk_hi, 1)
                    act.activation(ks[t % 2][:, :, 0:HD], k, ACT.Copy, scale=-2.0)
                    act.activation(ks[t % 2][:, :, 2 * HD:3 * HD], k, ACT.Copy, scale=-2.0).then_inc(qk_hi, 1)
                    act.wait_ge(v_full, n + 1)
                    act.wait_ge(pv_done, g * NS + 4)
                    act.activation(v[:, t, :, 0:HD], ps_v[:, 0, 0:D].rearrange("p (h d) -> p h d", h=H), ACT.Copy).then_inc(v_done, 1)

                def turned(t):
                    n = g * GT + t
                    act.wait_ge(s_full, n * 2 + 2)
                    act.activation(qt[:, :, t * P:(t + 1) * P], ps_t[:, :, :].rearrange("p b (h t) -> p (b h) t", t=P), ACT.Copy).then_inc(qt_done, 1)

                for t in range(GT):
                    stack(t)
                    if t >= 1:
                        turned(t - 1)
                turned(GT - 1)
                def output_hi(s):
                    act.wait_ge(pv_done, g * NS + (s + 1) * H + 4)
                    act.wait_ge(y_full, g * SEQS + s + 1)
                    for b in range(2):
                        act.activation(ot_hi[:, 2 * b:2 * b + 2, :].rearrange("p q t -> p (q t)"), ps_s[s][:, b, :], ACT.Copy).then_inc(ot_h, 1)

                for i in range(NS):
                    n = g * NS + i
                    act.wait_ge(relu_done, n + 3)
                    act.wait_ge(pv_done, n + 1)
                    act.activation(e[:, i % 4, :], dist[:, i % 2, :], ACT.Exp, scale=gsc[:, i % H:i % H + 1]).then_inc(exp_done, 1)
                    if i == H + LAG + 1:
                        output_hi(0)
                output_hi(1)
                if ahead:
                    spread(g + 1)

            act.sem_inc(pv_done, 4)
            act.wait_ge(s_w, 48)
            act.activation(w_hi[:, :, :], raw_w[:, :, :], ACT.Copy).then_inc(w_h, 1)
            act.wait_ge(s_wo, 64)
            act.activation(wo_hi[:, :, :], raw_o[:, :, :], ACT.Copy).then_inc(w_h, 1)
            act.wait_ge(s_gsc, 1)
            act.wait_ge(s_pad, 5)
            spread(0)
            with act.Fori(0, NG - 1) as g:
                group(g, True)
            group(NG - 1, False)

        @block.vector
        def _(dve):
            def norm_stats(g, k):
                if k:
                    reach(dve, h_ready, g + 1)
                else:
                    dve.wait_ge(s_pad, 5)
                for t in range(GT):
                    ins = dve.bn_stats(st[:, t, :], X[:, ds(g * GT + t, 1), :].rearrange("p a d -> p (a d)"))
                ins.then_inc(st_done, 1)

            def norm_variance(g, k):
                n = g * 2 + k
                reach(dve, st_done, n + 1)
                for t in range(GT):
                    ins = dve.bn_aggr(mv[:, t, :], st[:, t, :])
                ins.then_inc(mv_done, 1)
                dve.wait_ge(mv_done, n + 1)
                dve.tensor_scalar(ve[:, :], mv[:, :, 1], EPS, None, ALU.add).then_inc(ve_done, 1)

            def norm_apply(g, k, tiles):
                n = g * 2 + k
                dve.wait_ge(rs_done, n + 1)
                if k == 0:
                    dve.wait_ge(t_full, g + 1)
                for t in tiles:
                    ins = dve.tensor_scalar(xn[:, t, :], X[:, ds(g * GT + t, 1), :].rearrange("p a d -> p (a d)"), mv[:, t, 0:1], rs[:, t:t + 1],
                                            ALU.subtract, ALU.mult)
                if tiles[-1] == GT - 1:
                    ins.then_inc(xn_ready, 1)

            def split_x(g):
                for c in range(DC):
                    dve.wait_ge(nh_done, g * DC + c + 1)
                    dve.tensor_tensor(nl[:, c, :], ps_t[:, c, :], nh[:, c, :].bitcast(F32), ALU.subtract).then_inc(n_split, 1)

            def group(g, ahead):
                def stack(t):
                    n = g * GT + t
                    q = ps_qk[:, 0, 0:D].rearrange("p (h d) -> p h d", h=H)
                    k = ps_qk[:, 0, D:2 * D].rearrange("p (h d) -> p h d", h=H)
                    dve.wait_ge(sq_done, n + 1)
                    dve.wait_ge(stacked, n + 1)
                    dve.tensor_reduce(nrm[:, :], sq[:, :].rearrange("p (h d) -> p h d", d=HD), AX.X, ALU.add).then_inc(nrm_done, 1)
                    dve.wait_ge(qk_hi, n * 2 + 2)
                    dve.tensor_tensor(qs[t % 2][:, :, 2 * HD:3 * HD], q, qs[t % 2][:, :, 0:HD].bitcast(F32), ALU.subtract)
                    dve.wait_ge(nrm_done, n + 2)
                    dve.tensor_copy(qs[t % 2][:, :, 3 * HD:3 * HD + 1], nrm[:, 0:H].unsqueeze(2))
                    dve.tensor_copy(ks[t % 2][:, :, 3 * HD + 2:3 * HD + 3], nrm[:, H:2 * H].unsqueeze(2)).then_inc(nrm_hi, 1)
                    dve.scalar_tensor_tensor(ks[t % 2][:, :, HD:2 * HD], k, -2.0, ks[t % 2][:, :, 0:HD].bitcast(F32),
                                             ALU.mult, ALU.subtract).then_inc(qk_read, 1)
                    dve.wait_ge(nrm_hi, n + 1)
                    dve.tensor_tensor(qs[t % 2][:, :, 3 * HD + 1:3 * HD + 2], nrm[:, 0:H].unsqueeze(2),
                                      qs[t % 2][:, :, 3 * HD:3 * HD + 1].bitcast(F32), ALU.subtract)
                    dve.tensor_tensor(ks[t % 2][:, :, 3 * HD + 3:3 * HD + 4], nrm[:, H:2 * H].unsqueeze(2),
                                      ks[t % 2][:, :, 3 * HD + 2:3 * HD + 3].bitcast(F32), ALU.subtract).then_inc(stacked, 1)

                def turned(t):
                    n = g * GT + t
                    dve.wait_ge(s_full, n * 2 + 3)
                    dve.tensor_copy(kt[:, :, t * P:(t + 1) * P], ps_d[:, :, :].rearrange("p b (h t) -> p (b h) t", t=P)).then_inc(kt_done, 1)

                for t in range(GT):
                    stack(t)
                    if t >= 1:
                        turned(t - 1)
                turned(GT - 1)
                def output_lo(s):
                    for b in range(2):
                        dve.wait_ge(ot_h, (g * SEQS + s) * 2 + b + 1)
                        ins = dve.tensor_tensor(ot_lo[:, 2 * b:2 * b + 2, :].rearrange("p q t -> p (q t)"), ps_s[s][:, b, :],
                                                ot_hi[:, 2 * b:2 * b + 2, :].rearrange("p q t -> p (q t)").bitcast(F32), ALU.subtract)
                    ins.then_inc(ot_split, 1)

                def add_output(s):
                    dve.wait_ge(y_full, g * SEQS + s + 2)
                    x2 = X[:, ds(g * GT + 2 * s, 2), :].rearrange("p t d -> p (t d)")
                    dve.tensor_tensor(x2, ps_o[:, s, :], x2, ALU.add).then_inc(y_added, 1)

                for i in range(NS):
                    s, h = divmod(i, H)
                    dve.wait_ge(d_full, g * NS + i + 1)
                    dve.wait_ge(exp_done, g * NS + i + 1)
                    dve.tensor_scalar(dist[:, h % 2, :], ps_d[:, h % 2, 0:SCORES], 0.0, None, ALU.max).then_inc(relu_done, 1)
                    if ahead and h == 1:
                        norm_stats(g + 1, s)
                    if ahead and h == 2:
                        norm_variance(g + 1, s)
                    first = 6 + 4 * s
                    if ahead and h in (first, first + 1):
                        norm_apply(g + 1, s, (2 * (h - first), 2 * (h - first) + 1))
                    if i == H + LAG + 2:
                        output_lo(0)
                    if i == H + LAG + 6:
                        add_output(0)
                output_lo(1)
                if ahead:
                    split_x(g + 1)
                add_output(1)

            dve.sem_inc(exp_done, 2)
            dve.memset(neghalf[:, :], -0.5).then_inc(s_pad, 1)
            for i in range(2):
                dve.memset(qs[i][:, :, 3 * HD + 2:3 * HD + 4].bitcast(F32), 1.0)
                dve.memset(qs[i][:, :, 3 * HD + 4:ROW].bitcast(F32), 0.0)
                dve.memset(ks[i][:, :, 3 * HD:3 * HD + 2].bitcast(F32), 1.0)
                dve.memset(ks[i][:, :, 3 * HD + 4:ROW].bitcast(F32), 0.0).then_inc(s_pad, 1)
            dve.memset(v[:, :, :, HD:2 * HD], 0.0).then_inc(s_pad, 1)
            dve.wait_ge(s_vec, 16 * VECS)
            dve.tensor_scalar(gsc[:, :], gam[:, :], -SCALE, None, ALU.mult).then_inc(s_gsc, 1)
            dve.memset(ve[:, :], 1.0).then_inc(s_pad, 1)
            dve.wait_ge(s_pad, 5)
            for k in range(2):
                norm_stats(0, k)
                norm_variance(0, k)
                norm_apply(0, k, range(GT))
            split_x(0)
            with dve.Fori(0, NG - 1) as g:
                group(g, True)
            group(NG - 1, False)

        @block.gpsimd
        def _(pool):
            def rstd(g, k):
                pool.wait_ge(ve_done, g * 2 + k + 1)
                pool.tensor_tensor(rs[:, :], ve[:, :], neghalf[:, :], ALU.pow).then_inc(rs_done, 1)

            def scale_h(g, t):
                if t == 0:
                    reach(pool, xn_ready, g * 2 + 1)
                ins = pool.tensor_tensor(X[:, ds(g * GT + t, 1), :].rearrange("p a d -> p (a d)"), xn[:, t, :], fs[:, :], ALU.mult)
                if t == GT - 1:
                    ins.then_inc(h_mul, 1)

            def bias_h(g, t):
                if t == 0:
                    reach(pool, h_mul, g + 1)
                xt = X[:, ds(g * GT + t, 1), :].rearrange("p a d -> p (a d)")
                ins = pool.tensor_tensor(xt, xt, fb[:, :], ALU.add)
                if t == GT - 1:
                    ins.then_inc(h_ready, 1)

            def group(g, ahead):
                for s in range(SEQS):
                    for h in range(H):
                        n = g * NS + s * H + h
                        reach(pool, exp_done, n + 3)
                        diag = e[:, h % 4, P:3 * P]
                        pool.affine_select(out=diag, in_=diag, compare_op=ALU.is_gt, fill=zero, base=0,
                                           pattern=[[0, 2], [-1, P]], channel_multiplier=1).then_inc(masked, 1)
                        if ahead and h == 2:
                            rstd(g + 1, s)
                        if ahead and s == 0 and 8 <= h < 12:
                            scale_h(g + 1, h - 8)
                        if ahead and s == 0 and h >= 12:
                            bias_h(g + 1, h - 12)

            pool.memset(ident[:, :], 0.0).then_inc(s_ident, 1)
            pool.memset(raw_o[:, :, :], 0.0).then_inc(s_zero, 1)
            pool.wait_ge(s_ident, 1)
            pool.affine_select(out=ident[:, :], in_=ident[:, :], compare_op=ALU.not_equal, fill=1.0, base=0,
                               pattern=[[-1, P]], channel_multiplier=1).then_inc(s_ident, 1)
            pool.wait_ge(w_h, 1)
            pool.tensor_tensor(w_lo[:, :, :], raw_w[:, :, :], w_hi[:, :, :].bitcast(F32), ALU.subtract).then_inc(w_split, 1)
            pool.wait_ge(w_h, 2)
            pool.tensor_tensor(wo_lo[:, :, :], raw_o[:, :, :], wo_hi[:, :, :].bitcast(F32), ALU.subtract).then_inc(w_split, 1)
            pool.wait_ge(s_vec, 16 * VECS)
            pool.wait_ge(s_pad, 5)
            zero = pool.to_reg(0.0)
            rstd(0, 0)
            for t in range(GT):
                scale_h(0, t)
            for t in range(GT):
                bias_h(0, t)
            rstd(0, 1)
            with pool.Fori(0, NG - 1) as g:
                group(g, True)
            group(NG - 1, False)


WINDOW, HEADS3, HD3 = 128, 8, 64


def constants():
    n, f = 2 * P, np.float32
    half = np.arange(0, HD3, 2).astype(f)
    inv_freq = (f(1.0) / np.power(f(10000.0), half / f(HD3))).astype(f)
    t = np.arange(n).astype(f)
    freqs = np.concatenate([t[:, None] * inv_freq[None, :]] * 2, axis=-1).astype(f)
    base = ((half + f(0.4 * HD3)) / f(1.4 * HD3)).astype(f)
    power = ((t - f(n // 2)) / f(WINDOW // 2)).astype(f)
    scale = np.power(base[None, :].astype(np.float64), power[:, None])
    scale = np.concatenate([scale, scale], axis=-1)
    cos, sin = np.cos(freqs.astype(np.float64)), np.sin(freqs.astype(np.float64))
    sin = sin * np.where(np.arange(HD3) < HD3 // 2, -1.0, 1.0)[None, :]
    return {"rotary": np.stack([-8 * cos * scale, -8 * sin * scale, cos / scale, sin / scale]).astype(f)}


def window_phase(nc, sems, X, dram, out):
    L, H, HD, INNER, HID = 2, HEADS3, HD3, HEADS3 * HD3, 682
    FC = -(-HID // P)
    HIDP = FC * P
    LAST = HID - (FC - 1) * P
    IC = INNER // P
    SEQS = 2
    NH = SEQS * H
    QUAD = 4
    NQ = NH // QUAD
    SC = 3 * P
    FAR = float(np.finfo(np.float32).max)
    STEPS = L * NG
    NLOAD = 4 + 2 * (1 + 2 * L) + 4 * L
    TURN_AT = 3
    SPLIT_AT = 4
    PIECES = [("G", 0), ("G", 1), ("A", 0), ("A", 1), ("G", 2), ("G", 3), ("O", 0), ("O", 1), ("A", 2), ("A", 3),
              ("G", 4), ("G", 5), ("O", 2), ("O", 3), ("A", 4), ("A", 5), ("O", 4), ("O", 5)]

    def past(v):
        return max(v, 0) if isinstance(v, int) else v

    with ExitStack() as ctx:
        def sb(name, shape, dt=F32):
            return ctx.enter_context(nc.sbuf_tensor("w_" + name, shape, dt))

        def sem(name):
            sems.append(nc.alloc_semaphore("w_" + name))
            return sems[-1]

        def bank(name, n=1):
            return ctx.enter_context(nc.psum_tensor("w_" + name, [P, n, 512], F32))

        raw = sb("raw", [P, DC * 2 * HIDP])
        raw_qkv = raw[:, :].rearrange("p (c n) -> p c n", c=DC)
        raw_1 = raw[:, :].rearrange("p (c u n) -> p c u n", c=DC, u=2)
        raw_o = raw[:, 0:IC * D].rearrange("p (c n) -> p c n", c=IC)
        raw_2 = raw[:, IC * D:(IC + FC) * D].rearrange("p (c n) -> p c n", c=FC)
        qkv_hi = sb("qkv_hi", [P, DC, 3 * INNER], F32R)
        qkv_lo = sb("qkv_lo", [P, DC, 3 * INNER], F32R)
        wo_hi = sb("wo_hi", [P, IC, D], F32R)
        wo_lo = sb("wo_lo", [P, IC, D], F32R)
        w1_hi = sb("w1_hi", [P, DC, 2, HIDP], F32R)
        w1_lo = sb("w1_lo", [P, DC, 2, HIDP], F32R)
        w2_hi = sb("w2_hi", [P, FC, D], F32R)
        w2_lo = sb("w2_lo", [P, FC, D], F32R)
        ln_all = sb("ln_all", [P, 2, L * DC])
        b1_all = sb("b1_all", [P, L, 2, FC])
        b2_all = sb("b2_all", [P, L * D])
        scl = sb("scl", [P, 2, 2, L * HD])
        tab = sb("tab", [P, L, 4, 2, HD])
        neghalf = sb("neghalf", [P, GT])
        ident = sb("ident", [P, P])
        mask = sb("mask", [P, SC])
        st = sb("st", [P, GT, 2, 6])
        mv = sb("mv", [P, GT, 2])
        ve = sb("ve", [P, GT])
        rs = sb("rs", [P, GT])
        xn = sb("xn", [P, GT, D])
        xs = sb("xs", [P, GT, P])
        ah = sb("ah", [P, DC, GTOK], F32R)
        al = sb("al", [P, DC, GTOK], F32R)
        nh = sb("nh", [P, DC, GTOK], F32R)
        nl = sb("nl", [P, DC, GTOK], F32R)
        ss = sb("ss", [P, 2, H])
        sc = sb("sc", [P, 2, H])
        iv = sb("iv", [P, 2, H])
        y0 = sb("y0", [P, 2, H])
        ya = sb("ya", [P, 2, H])
        yb = sb("yb", [P, 2, H])
        rn = sb("rn", [P, GT, 2, H])
        m1 = sb("m1", [P, 2, 2, INNER])
        m2 = sb("m2", [P, 2, INNER])
        qt = sb("qt", [P, IC, GTOK])
        kt = sb("kt", [P, IC, GTOK])
        v = sb("v", [P, GT, INNER])
        sm = sb("sm", [P, 2, SC])
        mx = sb("mx", [P, NH, 2])
        rsum = sb("rsum", [P, 2, 2, QUAD])
        rinv = sb("rinv", [P, 2, QUAD])
        pr = sb("pr", [P, 2, SC])
        pt = sb("pt", [P, 2, SC])
        o = sb("o", [P, GT, INNER])
        ot_hi = sb("ot_hi", [P, 2, IC, P], F32R)
        ot_lo = sb("ot_lo", [P, 2, IC, P], F32R)
        gate = sb("gate", [P, 2, GTOK])
        nf = gate
        hid = sb("hid", [P, 2, GTOK])
        h_hi = sb("h_hi", [P, 2, GTOK], F32R)
        h_lo = sb("h_lo", [P, 2, GTOK], F32R)
        hres = xn

        ps_d = bank("ps_d", 2)
        ps_x = bank("ps_x", 2)
        ps_p = ps_x[:, 0:1, :]
        ps_a = ps_x[:, 1:2, :]
        ps_f = bank("ps_f", 2)
        ps_o = bank("ps_o", 2)

        names = ("h_out h_in stored vec ident maskz mask pad fill raw_qkv raw_ow raw_1 hi_qkv hi_o hi_2 hi_1 split_qkv split_o split_2 "
                 "split_1 tab x_ready x0_st x0_mv x0_ve x0_rs staged t1_full ah_done split1 q_full k_full v_full sq v_done "
                 "qk_read ss_done sc_done iv_done y0_done ya_done yb_done rn_done rota kscaled s_full qt_done kt_done d_full sm_done "
                 "p_done p_full pt_done pv_done ri o_done ot_full ot_h ot_split y_tile x_mid shifted st mv ve rs xn t2_full nf_done "
                 "split2 g_full a_full gelu_done gated h_hi h_split h_used xb padp fin")
        S = {x: sem(x) for x in names.split()}
        block = ctx.enter_context(nc.Block())

        def xt(g, t):
            return X[:, ds(g * GT + t, 1), :].rearrange("p a d -> p (a d)")

        def x2(g, s):
            return X[:, ds(g * GT + 2 * s, 2), :].rearrange("p t d -> p (t d)")

        def steps(eng, step):
            step(0, 0, None)
            with eng.Fori(1, NG - 1) as n:
                step(n, 0, 0)
            step(NG - 1, 0, 0)
            step(NG, 1, 0)
            with eng.Fori(NG + 1, STEPS - 1) as n:
                step(n, 1, 1)
            step(STEPS - 1, 1, 1)
            step(STEPS, None, 1)

        def at(n, k):
            return isinstance(n, int) and n == k

        def group_rows(n, la):
            return X[:, ds((n - NG * la) * GT, GT), :]

        out_v = out.rearrange("s (t p) d -> p (s t) d", p=P)

        @block.sync
        def _(sp):
            def load_ow(l):
                sp.dma_start(raw_o, dram["L0_ffn_wo"][l].rearrange("(c p) n -> p c n", p=P)).then_inc(S["raw_ow"], 16)
                w2 = dram["L0_ffn_w2"][l]
                sp.dma_start(raw_2[:, 0:FC - 1, :], w2[0:(FC - 1) * P, :].rearrange("(c p) n -> p c n", p=P)).then_inc(S["raw_ow"], 16)
                sp.dma_start(raw_2[0:LAST, FC - 1, :], w2[(FC - 1) * P:HID, :]).then_inc(S["raw_ow"], 16)

            def load_qkv(l):
                sp.dma_start(raw_qkv, dram["L0_ffn_wqkv"][l].rearrange("(c p) n -> p c n", p=P)).then_inc(S["raw_qkv"], 16)

            def load_1(l):
                w1 = dram["L0_ffn_w1"][l].rearrange("(c p) (u n) -> p c u n", p=P, u=2)
                for u in range(2):
                    sp.dma_start(raw_1[:, :, u, 0:HID], w1[:, :, u, :]).then_inc(S["raw_1"], 16)

            def step(n, la, lf):
                if at(n, NG - 1):
                    sp.wait_ge(S["split_qkv"], 2)
                    load_ow(1)
                if at(n, NG):
                    sp.wait_ge(S["split_o"], 2)
                    sp.wait_ge(S["split_2"], 2)
                    load_1(1)
                if la is not None:
                    sp.wait_ge(S["x_mid"], n * SEQS + SEQS)
                    sp.wait_ge(S["xn"], n)
                    xg = group_rows(n, la)
                    sp.dma_start(xs[1:P, :, :], xg[0:P - 1, :, P:D]).then_inc(S["shifted"], 16)
                    sp.dma_start(xs[0:1, :, :].rearrange("p (s t) d -> p s t d", s=SEQS)[:, :, 1, :],
                                 xg[P - 1:P, :, P:D].rearrange("p (s t) d -> p s t d", s=SEQS)[:, :, 0, :]).then_inc(S["shifted"], 16)

            load_qkv(0)
            for g in range(NG):
                sp.dma_start(out_v[:, GT * g:GT * g + GT, :], X[:, GT * g:GT * g + GT, :]).then_inc(S["h_out"], 16)
            for k, name in enumerate(("L0_ffn_ln_g", "L0_ffn_ln_b")):
                sp.dma_start(ln_all[:, k, :], dram[name].rearrange("l (c p) -> p (l c)", p=P)).then_inc(S["vec"], 16)
            sp.dma_start(tab[:, 0, :, :, :].rearrange("p k t d -> p (k t) d"),
                         dram["rotary"].rearrange("k (t p) d -> p (k t) d", p=P)).then_inc(S["vec"], 16)
            sp.dma_start(b2_all[:, :], dram["L0_ffn_b2"].rearrange("(a l) d -> a (l d)", a=1).broadcast_to([P, L * D])).then_inc(S["vec"], 16)
            for k, name in enumerate(("L0_ffn_q_scale", "L0_ffn_k_scale")):
                src = dram[name].rearrange("(a l) (u d) -> a l u d", a=1, u=2)
                sp.dma_start(scl[:, k, 0, :], dram[name].rearrange("(a l) d -> a (l d)", a=1).broadcast_to([P, L * HD])).then_inc(S["vec"], 16)
                for i in range(L):
                    for u in range(2):
                        sp.dma_start(scl[:, k, 1, i * HD + u * (HD // 2):i * HD + (u + 1) * (HD // 2)],
                                     src[:, i, 1 - u, :].broadcast_to([P, HD // 2])).then_inc(S["vec"], 16)
            sp.wait_ge(S["pad"], 1)
            for i in range(L):
                for u in range(2):
                    b1 = dram["L0_ffn_b1"][i, u * HID:(u + 1) * HID]
                    sp.dma_start(b1_all[:, i, u, 0:FC - 1], b1[0:(FC - 1) * P].rearrange("(c p) -> p c", p=P)).then_inc(S["vec"], 16)
                    sp.dma_start(b1_all[0:LAST, i, u, FC - 1:FC], b1[(FC - 1) * P:HID].rearrange("(p c) -> p c", c=1)).then_inc(S["vec"], 16)
            sp.wait_ge(S["split_qkv"], 1)
            load_ow(0)
            sp.wait_ge(S["split_o"], 1)
            sp.wait_ge(S["split_2"], 1)
            load_1(0)
            sp.wait_ge(S["split_1"], 1)
            load_qkv(1)
            steps(sp, step)

        @block.tensor
        def _(pe):
            def turn_x(dst):
                for c in range(DC):
                    for t in range(GT):
                        mm = pe.transpose(dst[:, c, t * P:(t + 1) * P], xn[:, t, c * P:(c + 1) * P], ident[:, :])
                return mm

            def turn_in(n):
                pe.wait_ge(S["staged"], n + 1)
                turn_x(ps_x).then_inc(S["t1_full"], 1)

            def step(n, la, lf):
                def project(t):
                    m = n * GT + t
                    tok = slice(t * P, (t + 1) * P)
                    for i, (dst, full) in enumerate(((ps_f[:, 0, :], "q_full"), (ps_f[:, 1, :], "k_full"), (ps_p[:, 0, :], "v_full"))):
                        pe.wait_ge(S["v_done" if i == 2 else "qk_read"], m if i == 2 else past(2 * m + i - 1))
                        cols = slice(i * INNER, (i + 1) * INNER)
                        for c in range(DC):
                            pe.matmul(dst, ah[:, c, tok], qkv_hi[:, c, cols], start=(c == 0), stop=False)
                            pe.matmul(dst, ah[:, c, tok], qkv_lo[:, c, cols], start=False, stop=False)
                            mm = pe.matmul(dst, al[:, c, tok], qkv_hi[:, c, cols], start=False, stop=(c == DC - 1))
                        mm.then_inc(S[full], 1)

                def turn(t):
                    m = n * GT + t
                    for i, (ready, free) in enumerate((("rota", "qt_done"), ("kscaled", "kt_done"))):
                        pe.wait_ge(S[ready], 2 * m + 1 if i == 0 else m + 1)
                        pe.wait_ge(S[free], m)
                        for c in range(IC):
                            mm = pe.transpose(ps_d[:, i, c * P:(c + 1) * P], m1[:, t % 2, i, c * P:(c + 1) * P], ident[:, :])
                        mm.then_inc(S["s_full"], 1)

                def scores(i):
                    s, h = divmod(i, H)
                    m = n * NH + i
                    if i == 0:
                        pe.wait_ge(S["qt_done"], n * GT + GT)
                        pe.wait_ge(S["kt_done"], n * GT + GT)
                    pe.wait_ge(S["sm_done"], past(m - 1))
                    rows = slice(HD * (h % 2), HD * (h % 2) + HD)
                    t0, t1, t2 = 2 * s * P, (2 * s + 1) * P, (2 * s + 2) * P
                    b = ps_d[:, i % 2, :]
                    pe.matmul(b[:, 0:P], qt[rows, h // 2, t0:t1], kt[rows, h // 2, t0:t1], start=True, stop=True)
                    pe.matmul(b[:, P:SC], qt[rows, h // 2, t1:t2], kt[rows, h // 2, t0:t2], start=True, stop=True).then_inc(S["d_full"], 1)

                def turn_p(i):
                    m = n * NH + i
                    if i == 0:
                        pe.wait_ge(S["v_done"], n * GT + GT)
                    pe.wait_ge(S["p_done"], m + 1)
                    pe.wait_ge(S["pt_done"], m)
                    for b in range(3):
                        mm = pe.transpose(ps_p[:, 0, b * P:(b + 1) * P], pr[:, i % 2, b * P:(b + 1) * P], ident[:, :])
                    mm.then_inc(S["p_full"], 1)

                def values(i):
                    s, h = divmod(i, H)
                    if i % QUAD == 0:
                        pe.wait_ge(S["o_done"], n * NQ + i // QUAD)
                    pe.wait_ge(S["pt_done"], n * NH + i + 1)
                    vs = slice(h * HD, (h + 1) * HD)
                    o0 = ps_a[:, 0, (i % QUAD) * HD:(i % QUAD + 1) * HD]
                    o1 = ps_a[:, 0, (QUAD + i % QUAD) * HD:(QUAD + i % QUAD + 1) * HD]
                    pe.matmul(o0, pt[:, i % 2, 0:P], v[:, 2 * s, vs], start=True, stop=True)
                    pe.matmul(o1, pt[:, i % 2, P:2 * P], v[:, 2 * s, vs], start=True, stop=False)
                    pe.matmul(o1, pt[:, i % 2, 2 * P:3 * P], v[:, 2 * s + 1, vs], start=False, stop=True).then_inc(S["pv_done"], 1)

                def turn_o(k):
                    pe.wait_ge(S["ot_split"], past(n * GT + k - 1))
                    for c in range(IC):
                        mm = pe.transpose(ps_d[:, k % 2, c * P:(c + 1) * P], o[:, k, c * P:(c + 1) * P], ident[:, :])
                    mm.then_inc(S["ot_full"], 1)

                def project_out(k):
                    pe.wait_ge(S["ot_split"], n * GT + k + 1)
                    dst = ps_f[:, k // 2, (k % 2) * D:(k % 2 + 1) * D]
                    for c in range(IC):
                        pe.matmul(dst, ot_hi[:, k % 2, c, :], wo_hi[:, c, :], start=(k % 2 == 0 and c == 0), stop=False, skip_group_check=True)
                        pe.matmul(dst, ot_hi[:, k % 2, c, :], wo_lo[:, c, :], start=False, stop=False, skip_group_check=True)
                        mm = pe.matmul(dst, ot_lo[:, k % 2, c, :], wo_hi[:, c, :], start=False, stop=(k % 2 == 1 and c == IC - 1), skip_group_check=True)
                    mm.then_inc(S["y_tile"], 1)

                def piece(i):
                    what, j = PIECES[i]
                    m = (n - 1) * FC + j
                    if what == "O":
                        pe.wait_ge(S["h_split"], m + 3)
                        for t in range(GT):
                            tok = slice(t * P, (t + 1) * P)
                            dst = ps_o[:, t // 2, (t % 2) * D:(t % 2 + 1) * D]
                            pe.matmul(dst, h_hi[:, j % 2, tok], w2_hi[:, j, :], start=(j == 0 and t % 2 == 0), stop=False, skip_group_check=True)
                            pe.matmul(dst, h_hi[:, j % 2, tok], w2_lo[:, j, :], start=False, stop=False, skip_group_check=True)
                            mm = pe.matmul(dst, h_lo[:, j % 2, tok], w2_hi[:, j, :], start=False, stop=(j == FC - 1 and t % 2 == 1), skip_group_check=True)
                        mm.then_inc(S["h_used"], 1)
                        return
                    if i == 0:
                        pe.wait_ge(S["split_1"], lf + 1)
                        pe.wait_ge(S["split_2"], lf + 1)
                        pe.wait_ge(S["split2"], n * DC)
                    if what == "A":
                        pe.wait_ge(S["gelu_done"], m + 1)
                    elif j < 2:
                        pe.wait_ge(S["qk_read"], n * GT * 2 if la is None else (n * GT + GT) * 2)
                        pe.wait_ge(S["x_mid"], n * SEQS)
                    else:
                        pe.wait_ge(S["gated"], m + 1)
                    u = 1 if what == "G" else 0
                    cols = slice(j * P, (j + 1) * P)
                    for c in range(DC):
                        pe.matmul(ps_f[:, j % 2, :], w1_hi[:, c, u, cols], nh[:, c, :], start=(c == 0), stop=False)
                        pe.matmul(ps_f[:, j % 2, :], w1_lo[:, c, u, cols], nh[:, c, :], start=False, stop=False)
                        mm = pe.matmul(ps_f[:, j % 2, :], w1_hi[:, c, u, cols], nl[:, c, :], start=False, stop=(c == DC - 1))
                    mm.then_inc(S["g_full" if u else "a_full"], 1)

                def turn_normed():
                    pe.wait_ge(S["xn"], n)
                    pe.wait_ge(S["x_ready"], n - 1 + NG)
                    turn_x(ps_o).then_inc(S["t2_full"], 1)

                if la is not None:
                    pe.wait_ge(S["split_qkv"], la + 1)
                    pe.wait_ge(S["split1"], n * DC + DC)
                    pe.wait_ge(S["x_mid"], n * SEQS)
                    for t in range(GT):
                        project(t)
                        if t >= 1:
                            turn(t - 1)
                        if t == TURN_AT and lf is not None:
                            turn_normed()
                    turn(GT - 1)
                else:
                    turn_normed()
                for i in range(NH + 2):
                    if la is not None and i < NH:
                        scores(i)
                    if la is not None and 1 <= i <= NH:
                        turn_p(i - 1)
                    if lf is not None:
                        piece(i)
                    if la is not None and i >= 2:
                        values(i - 2)
                if la is not None:
                    pe.wait_ge(S["o_done"], n * NQ + NQ)
                    pe.wait_ge(S["split_o"], la + 1)
                    if lf is not None:
                        pe.wait_ge(S["gated"], n * FC + 2)
                    turn_o(0)
                    for k in range(GT):
                        if k < GT - 1:
                            turn_o(k + 1)
                        if k == 0 and not at(n, STEPS - 1):
                            turn_in(n + 1)
                        project_out(k)

            for x in ("gated", "h_used", "h_split"):
                pe.sem_inc(S[x], 2)
            pe.wait_ge(S["ident"], 2)
            pe.wait_ge(S["fill"], 1)
            turn_in(0)
            steps(pe, step)

        @block.scalar
        def _(act):
            def split_qkv(l):
                act.wait_ge(S["raw_qkv"], 16 * l + 16)
                act.wait_ge(S["v_full"], l * NG * GT)
                act.activation(qkv_hi[:, :, :], raw_qkv, ACT.Copy).then_inc(S["hi_qkv"], 1)

            def split_o(l):
                act.wait_ge(S["raw_ow"], 48 * l + 48)
                act.wait_ge(S["y_tile"], l * NG * GT)
                act.activation(wo_hi[:, :, :], raw_o, ACT.Copy).then_inc(S["hi_o"], 1)

            def split_2(l):
                act.wait_ge(S["raw_ow"], 48 * l + 48)
                act.wait_ge(S["h_used"], l * NG * FC + 2)
                act.activation(w2_hi[0:LAST, FC - 1, :], raw_2[0:LAST, FC - 1, :], ACT.Copy)
                act.activation(w2_hi[:, 0:FC - 1, :], raw_2[:, 0:FC - 1, :], ACT.Copy).then_inc(S["hi_2"], 1)

            def split_1(l):
                act.wait_ge(S["raw_1"], 32 * l + 32)
                act.activation(w1_hi[:, :, :, 0:HID].rearrange("p c u n -> p (c u) n"),
                               raw_1[:, :, :, 0:HID].rearrange("p c u n -> p (c u) n"), ACT.Copy).then_inc(S["hi_1"], 1)

            def spread(n):
                act.wait_ge(S["t1_full"], n + 1)
                act.activation(ah[:, 0, :], ps_x[:, 0, :], ACT.Copy).then_inc(S["ah_done"], 1)
                act.activation(ah[:, 1, :].rearrange("p (s t) -> p s t", s=SEQS)[:, :, 1:2 * P],
                               ps_x[:, 1, :].rearrange("p (s t) -> p s t", s=SEQS)[:, :, 0:2 * P - 1], ACT.Copy).then_inc(S["ah_done"], 1)

            def step(n, la, lf):
                def squares(t):
                    m = n * GT + t
                    for i, full in enumerate(("q_full", "k_full")):
                        act.wait_ge(S["rota"], past(2 * m + i - 1))
                        act.wait_ge(S[full], m + 1)
                        act.activation(m2[:, i, :], ps_f[:, i, :], ACT.Square).then_inc(S["sq"], 1)
                    act.wait_ge(S["v_full"], m + 1)
                    act.wait_ge(S["pv_done"], n * NH)
                    act.activation(v[:, t, :], ps_p[:, 0, :], ACT.Copy).then_inc(S["v_done"], 1)

                def root(t):
                    act.wait_ge(S["iv_done"], n * GT + t + 1)
                    act.activation(y0[:, :, :], iv[:, :, :], ACT.Sqrt).then_inc(S["y0_done"], 1)

                def turned(t):
                    act.wait_ge(S["s_full"], 2 * (n * GT + t) + 1)
                    act.activation(qt[:, :, t * P:(t + 1) * P], ps_d[:, 0, :].rearrange("p (c t) -> p c t", t=P), ACT.Copy).then_inc(S["qt_done"], 1)
                    act.wait_ge(S["s_full"], 2 * (n * GT + t) + 2)
                    act.activation(kt[:, :, t * P:(t + 1) * P], ps_d[:, 1, :].rearrange("p (c t) -> p c t", t=P), ACT.Copy).then_inc(S["kt_done"], 1)

                if la is not None:
                    for t in range(GT):
                        squares(t)
                        if t >= 1:
                            turned(t - 1)
                        root(t)
                    turned(GT - 1)
                if lf is not None:
                    act.wait_ge(S["t2_full"], n)
                    act.wait_ge(S["gated"], (n - 1) * FC + 2)
                    for c in range(DC):
                        s, b = (ln_all[:, k, lf * DC + c:lf * DC + c + 1] for k in range(2))
                        act.activation(nf[:, c, :], ps_o[:, c, :], ACT.Identity, bias=b, scale=s)
                        act.activation(nh[:, c, :], ps_o[:, c, :], ACT.Identity, bias=b, scale=s).then_inc(S["nf_done"], 1)

                def probabilities(i):
                    m = n * NH + i
                    q = n * NQ + i // QUAD
                    if i % QUAD == 0:
                        act.wait_ge(S["ri"], past(q - 1))
                    act.wait_ge(S["sm_done"], m + 1)
                    act.wait_ge(S["p_full"], past(m - 1))
                    act.activation(pr[:, i % 2, 0:P], sm[:, i % 2, 0:P], ACT.Exp, scale=-1.0,
                                   bias=mx[:, i, 0:1], accum_out=rsum[:, i // QUAD % 2, 0, i % QUAD:i % QUAD + 1])
                    act.activation(pr[:, i % 2, P:SC], sm[:, i % 2, P:SC], ACT.Exp, scale=-1.0,
                                   bias=mx[:, i, 1:2], accum_out=rsum[:, i // QUAD % 2, 1, i % QUAD:i % QUAD + 1]).then_inc(S["p_done"], 1)

                def gelu(j):
                    m = (n - 1) * FC + j
                    act.wait_ge(S["g_full"], m + 1)
                    act.wait_ge(S["gated"], m + 1)
                    if j < 2:
                        act.wait_ge(S["split2"], n * DC)
                    act.activation(gate[:, j % 2, :], ps_f[:, j % 2, :], ACT.Gelu, bias=b1_all[:, lf, 1, j:j + 1]).then_inc(S["gelu_done"], 1)

                def hidden_hi(j):
                    m = (n - 1) * FC + j
                    act.wait_ge(S["gated"], m + 3)
                    act.wait_ge(S["h_used"], m + 1)
                    act.activation(h_hi[:, j % 2, :], hid[:, j % 2, :], ACT.Copy).then_inc(S["h_hi"], 1)

                for i in range(NH + 2):
                    if la is not None and i < NH:
                        probabilities(i)
                    if lf is not None:
                        what, j = PIECES[i]
                        if what == "G" and j % 2 == 1:
                            gelu(j - 1)
                            gelu(j)
                        if i >= 1 and PIECES[i - 1][0] == "A":
                            hidden_hi(PIECES[i - 1][1])
                    if i == SPLIT_AT and at(n, NG - 1):
                        split_qkv(1)
                    if i == SPLIT_AT and at(n, NG):
                        split_o(1)
                if at(n, NG):
                    split_2(1)
                if la is not None:
                    for k in range(GT):
                        act.wait_ge(S["ot_full"], n * GT + k + 1)
                        act.wait_ge(S["y_tile"], past(n * GT + k - 1))
                        act.activation(ot_hi[:, k % 2, :, :].rearrange("p c t -> p (c t)"), ps_d[:, k % 2, :], ACT.Copy).then_inc(S["ot_h"], 1)
                        if k == 1 and not at(n, STEPS - 1):
                            spread(n + 1)
                if at(n, NG):
                    split_1(1)

            act.wait_ge(S["fill"], 1)
            spread(0)
            split_qkv(0)
            split_o(0)
            split_2(0)
            act.wait_ge(S["vec"], 16 * NLOAD)
            split_1(0)
            steps(act, step)

        @block.vector
        def _(dve):
            def split_in(n):
                dve.wait_ge(S["ah_done"], n * DC + 1)
                dve.tensor_tensor(al[:, 0, :], ps_x[:, 0, :], ah[:, 0, :].bitcast(F32), ALU.subtract).then_inc(S["split1"], 1)
                dve.wait_ge(S["ah_done"], n * DC + 2)
                dve.tensor_tensor(al[:, 1, :].rearrange("p (s t) -> p s t", s=SEQS)[:, :, 1:2 * P],
                                  ps_x[:, 1, :].rearrange("p (s t) -> p s t", s=SEQS)[:, :, 0:2 * P - 1],
                                  ah[:, 1, :].bitcast(F32).rearrange("p (s t) -> p s t", s=SEQS)[:, :, 1:2 * P], ALU.subtract).then_inc(S["split1"], 1)

            def step(n, la, lf):
                def rotate(t):
                    m = n * GT + t
                    for i in range(2):
                        dve.wait_ge(S["sq"], 2 * m + i + 1)
                        dve.tensor_reduce(ss[:, i, :], m2[:, i, :].rearrange("p (h d) -> p h d", d=HD), AX.X, ALU.add).then_inc(S["ss_done"], 1)
                        src = ps_f[:, i, :].rearrange("p (h d) -> p h d", d=HD)
                        src4 = ps_f[:, i, :].rearrange("p (h u d) -> p h u d", u=2, d=HD // 2)
                        cs = tab[:, la, 2 * i, t % 2, :].unsqueeze(1).broadcast_to([P, H, HD])
                        sn = tab[:, la, 2 * i + 1, t % 2, :].rearrange("p (u d) -> p u d", u=2)
                        dve.wait_ge(S["s_full"], past(2 * (m - 2) + i + 1))
                        dve.tensor_tensor(m1[:, t % 2, i, :].rearrange("p (h d) -> p h d", d=HD), src, cs, ALU.mult)
                        dst = m2[:, i, :].rearrange("p (h u d) -> p h u d", u=2, d=HD // 2)
                        dve.wait_ge(S["ss_done"], 2 * m + i + 1)
                        for u in range(2):
                            ins = dve.tensor_tensor(dst[:, :, u, :], src4[:, :, 1 - u, :], sn[:, u, :].unsqueeze(1).broadcast_to([P, H, HD // 2]), ALU.mult)
                        ins.then_inc(S["qk_read"], 1)
                    dve.tensor_scalar(sc[:, :, :], ss[:, :, :], 1e-24, None, ALU.max).then_inc(S["sc_done"], 1)
                    dve.wait_ge(S["sc_done"], m + 1)
                    dve.reciprocal(iv[:, :, :], sc[:, :, :]).then_inc(S["iv_done"], 1)

                def inverse_root(t):
                    m = n * GT + t
                    dve.wait_ge(S["y0_done"], m + 1)
                    dve.tensor_tensor(ya[:, :, :], y0[:, :, :], y0[:, :, :], ALU.mult).then_inc(S["ya_done"], 1)
                    dve.wait_ge(S["ya_done"], m + 1)
                    dve.scalar_tensor_tensor(yb[:, :, :], ya[:, :, :], -0.5, sc[:, :, :], ALU.mult, ALU.mult).then_inc(S["yb_done"], 1)
                    dve.wait_ge(S["yb_done"], m + 1)
                    dve.scalar_tensor_tensor(rn[:, t, :, :], yb[:, :, :], 1.5, y0[:, :, :], ALU.add, ALU.mult).then_inc(S["rn_done"], 1)

                def norm_stats():
                    g = n - 1 - NG * lf
                    reach(dve, S["x_mid"], n * SEQS)
                    for t in range(GT):
                        dve.bn_stats(st[:, t, 0, :], xt(g, t)[:, 0:P])
                    reach(dve, S["shifted"], n * 32)
                    for t in range(GT):
                        ins = dve.bn_stats(st[:, t, 1, :], xs[:, t, :])
                    ins.then_inc(S["st"], 1)
                    reach(dve, S["st"], n)
                    for t in range(GT):
                        ins = dve.bn_aggr(mv[:, t, :], st[:, t, :, :].rearrange("p a b -> p (a b)"))
                    ins.then_inc(S["mv"], 1)
                    dve.wait_ge(S["mv"], n)
                    dve.tensor_scalar(ve[:, :], mv[:, :, 1], EPS, None, ALU.add).then_inc(S["ve"], 1)

                def norm():
                    g = n - 1 - NG * lf
                    dve.wait_ge(S["rs"], n)
                    dve.wait_ge(S["t1_full"], n if la is None else n + 1)
                    for t in range(GT):
                        dve.tensor_scalar(xn[:, t, 0:P], xt(g, t)[:, 0:P], mv[:, t, 0:1], rs[:, t:t + 1], ALU.subtract, ALU.mult)
                        ins = dve.tensor_scalar(xn[:, t, P:D], xs[:, t, :], mv[:, t, 0:1], rs[:, t:t + 1], ALU.subtract, ALU.mult)
                    ins.then_inc(S["xn"], 1)

                if la is not None:
                    for t in range(GT):
                        rotate(t)
                        if lf is not None and t == 1:
                            norm_stats()
                        if lf is not None and t == 2:
                            norm()
                        inverse_root(t)
                else:
                    norm_stats()
                    norm()
                if lf is not None:
                    for c in range(DC):
                        dve.wait_ge(S["nf_done"], (n - 1) * DC + c + 1)
                        dve.tensor_tensor(nl[:, c, :], nf[:, c, :], nh[:, c, :].bitcast(F32), ALU.subtract).then_inc(S["split2"], 1)

                def soft(i):
                    s, h = divmod(i, H)
                    m = n * NH + i
                    reach(dve, S["d_full"], m + 1, S["p_done"], past(m - 1))
                    dve.tensor_tensor_reduce(sm[:, i % 2, 0:P], ps_d[:, i % 2, 0:P], mask[:, 0:P], rn[:, 2 * s, 0, h:h + 1], FAR, ALU.add, ALU.min,
                                             mx[:, i, 0:1])
                    dve.tensor_tensor_reduce(sm[:, i % 2, P:SC], ps_d[:, i % 2, P:SC], mask[:, P:SC], rn[:, 2 * s + 1, 0, h:h + 1], FAR, ALU.add, ALU.min,
                                             mx[:, i, 1:2]).then_inc(S["sm_done"], 1)

                def turned_p(i):
                    m = n * NH + i
                    dve.wait_ge(S["pv_done"], past(m - 1))
                    dve.wait_ge(S["p_full"], m + 1)
                    dve.tensor_copy(pt[:, i % 2, :], ps_p[:, 0, 0:SC]).then_inc(S["pt_done"], 1)

                def normalise(i):
                    s, h = divmod(i + 1 - QUAD, H)
                    q = n * NQ + i // QUAD
                    dve.wait_ge(S["p_done"], n * NH + i + 1)
                    dve.wait_ge(S["o_done"], q)
                    dve.reciprocal(rinv[:, :, :], rsum[:, i // QUAD % 2, :, :]).then_inc(S["ri"], 1)
                    dve.wait_ge(S["ri"], q + 1)
                    dve.wait_ge(S["pv_done"], n * NH + i + 1)
                    dve.wait_ge(S["ot_full"], n * GT)
                    dve.tensor_tensor(o[:, 2 * s:2 * s + 2, h * HD:(h + QUAD) * HD].rearrange("p w (h d) -> p w h d", d=HD),
                                      ps_a[:, 0, :].rearrange("p (w h d) -> p w h d", w=2, d=HD),
                                      rinv[:, :, :].unsqueeze(3).broadcast_to([P, 2, QUAD, HD]), ALU.mult).then_inc(S["o_done"], 1)

                def gated(j):
                    m = (n - 1) * FC + j
                    dve.wait_ge(S["a_full"], m + 1)
                    dve.wait_ge(S["h_split"], m + 1)
                    dve.scalar_tensor_tensor(hid[:, j % 2, :], ps_f[:, j % 2, :], b1_all[:, lf, 0, j:j + 1], gate[:, j % 2, :],
                                             ALU.add, ALU.mult).then_inc(S["gated"], 1)

                def hidden_lo(j):
                    m = (n - 1) * FC + j
                    dve.wait_ge(S["h_hi"], m + 1)
                    dve.tensor_tensor(h_lo[:, j % 2, :], hid[:, j % 2, :], h_hi[:, j % 2, :].bitcast(F32), ALU.subtract).then_inc(S["h_split"], 1)

                def add_output():
                    g = n - 1 - NG * lf
                    dve.wait_ge(S["xb"], n)
                    dve.wait_ge(S["h_used"], n * FC + 2)
                    for s in range(SEQS):
                        ins = dve.tensor_tensor(x2(g, s), ps_o[:, s, :], x2(g, s), ALU.add)
                    ins.then_inc(S["x_ready"], 1)

                def add_attention(s):
                    dve.wait_ge(S["y_tile"], n * GT + 2 * s + 2)
                    g = n - NG * la
                    dve.tensor_tensor(x2(g, s), ps_f[:, s, :], x2(g, s), ALU.add).then_inc(S["x_mid"], 1)

                for i in range(NH + 3):
                    if la is not None:
                        if i >= 3 and (i - 2) % QUAD == 0:
                            normalise(i - 3)
                        if i < NH:
                            soft(i)
                        if 1 <= i <= NH:
                            turned_p(i - 1)
                    if lf is not None:
                        if i >= 2 and PIECES[i - 2][0] == "A":
                            hidden_lo(PIECES[i - 2][1])
                        if 1 <= i <= NH + 2 and PIECES[i - 1][0] == "A":
                            gated(PIECES[i - 1][1])
                if la is not None:
                    for k in range(GT):
                        dve.wait_ge(S["ot_h"], n * GT + k + 1)
                        dve.tensor_tensor(ot_lo[:, k % 2, :, :].rearrange("p c t -> p (c t)"), ps_d[:, k % 2, :],
                                          ot_hi[:, k % 2, :, :].rearrange("p c t -> p (c t)").bitcast(F32), ALU.subtract).then_inc(S["ot_split"], 1)
                        if k == 0 and lf is not None:
                            add_output()
                        if k == 1 and not at(n, STEPS - 1):
                            split_in(n + 1)
                        if k == 2:
                            add_attention(0)
                    add_attention(1)
                else:
                    add_output()

            dve.memset(neghalf[:, :], -0.5).then_inc(S["padp"], 1)
            dve.memset(b1_all[:, :, :, :], 0.0).then_inc(S["pad"], 1)
            dve.memset(xs[0:1, :, :], 0.0)
            for a in (ah, al):
                dve.memset(a[:, 1, :].rearrange("p (s t) -> p s t", s=SEQS)[:, :, 0:1].bitcast(F32), 0.0)
            for w in (w1_hi, w1_lo):
                dve.memset(w[:, :, :, HID:HIDP].bitcast(F32), 0.0)
            for w in (w2_hi, w2_lo):
                dve.memset(w[:, FC - 1, :].bitcast(F32), 0.0)
            dve.memset(mx[:, :, :], 0.0).then_inc(S["fill"], 1)
            dve.wait_ge(S["fill"], 1)
            for g in range(NG):
                for t in range(GT):
                    ins = dve.bn_stats(st[:, t, 0, :], X[:, GT * g + t, :])
                ins.then_inc(S["x0_st"], 1)
                dve.wait_ge(S["x0_st"], g + 1)
                for t in range(GT):
                    ins = dve.bn_aggr(mv[:, t, :], st[:, t, 0, :])
                ins.then_inc(S["x0_mv"], 1)
                dve.wait_ge(S["x0_mv"], g + 1)
                dve.tensor_scalar(ve[:, :], mv[:, :, 1], EPS, None, ALU.add).then_inc(S["x0_ve"], 1)
                dve.wait_ge(S["x0_rs"], g + 1)
                dve.wait_ge(S["h_out"], 16 * NG)
                for t in range(GT):
                    xg = X[:, GT * g + t, :]
                    ins = dve.tensor_scalar(xg, xg, mv[:, t, 0:1], rs[:, t:t + 1], ALU.subtract, ALU.mult)
                ins.then_inc(S["x_ready"], 1)
                dve.wait_ge(S["x_ready"], g + 1)
            split_in(0)
            dve.wait_ge(S["vec"], 16 * NLOAD)
            for l in reversed(range(L)):
                for i in range(2):
                    for u in range(2):
                        ins = dve.tensor_tensor(tab[:, l, 2 * i + u, :, :], tab[:, 0, 2 * i + u, :, :],
                                                scl[:, i, u, l * HD:(l + 1) * HD].unsqueeze(1).broadcast_to([P, 2, HD]), ALU.mult)
            ins.then_inc(S["tab"], 1)
            dve.wait_ge(S["tab"], 1)
            steps(dve, step)
            for g in range(NG):
                dve.wait_ge(S["h_in"], 16 * g + 16)
                xg = X[:, GT * g:GT * g + GT, :]
                dve.tensor_tensor(xg, xg, hres[:, :, :], ALU.add).then_inc(S["fin"], 1)

        @block.gpsimd
        def _(pool):
            def lo_qkv(l):
                pool.wait_ge(S["hi_qkv"], l + 1)
                pool.tensor_tensor(qkv_lo[:, :, :], raw_qkv, qkv_hi[:, :, :].bitcast(F32), ALU.subtract).then_inc(S["split_qkv"], 1)

            def lo_o(l):
                pool.wait_ge(S["hi_o"], l + 1)
                pool.tensor_tensor(wo_lo[:, :, :], raw_o, wo_hi[:, :, :].bitcast(F32), ALU.subtract).then_inc(S["split_o"], 1)

            def lo_2(l):
                pool.wait_ge(S["hi_2"], l + 1)
                pool.tensor_tensor(w2_lo[0:LAST, FC - 1, :], raw_2[0:LAST, FC - 1, :], w2_hi[0:LAST, FC - 1, :].bitcast(F32), ALU.subtract)
                pool.tensor_tensor(w2_lo[:, 0:FC - 1, :], raw_2[:, 0:FC - 1, :], w2_hi[:, 0:FC - 1, :].bitcast(F32), ALU.subtract).then_inc(S["split_2"], 1)

            def lo_1(l):
                pool.wait_ge(S["hi_1"], l + 1)
                pool.tensor_tensor(w1_lo[:, :, :, 0:HID].rearrange("p c u n -> p (c u) n"), raw_1[:, :, :, 0:HID].rearrange("p c u n -> p (c u) n"),
                                   w1_hi[:, :, :, 0:HID].rearrange("p c u n -> p (c u) n").bitcast(F32), ALU.subtract).then_inc(S["split_1"], 1)

            def stage(n, l):
                reach(pool, S["x_ready"], n + 1)
                pool.tensor_copy(xn[:, :, :], X[:, ds((n - NG * l) * GT, GT), :]).then_inc(S["staged"], 1)

            def step(n, la, lf):
                if la is not None:
                    for t in range(GT):
                        m = n * GT + t
                        for i in range(2):
                            pool.wait_ge(S["qk_read"], 2 * m + i + 1)
                            pool.tensor_tensor(m1[:, t % 2, i, :], m1[:, t % 2, i, :], m2[:, i, :], ALU.add).then_inc(S["rota"], 1)
                        pool.wait_ge(S["rota"], 2 * m + 2)
                        pool.wait_ge(S["rn_done"], m + 1)
                        mk = m1[:, t % 2, 1, :].rearrange("p (h d) -> p h d", d=HD)
                        pool.tensor_tensor(mk, mk, rn[:, t, 1, :].unsqueeze(2).broadcast_to([P, H, HD]), ALU.mult).then_inc(S["kscaled"], 1)
                        if t == 1 and lf is not None:
                            pool.wait_ge(S["ve"], n)
                            pool.tensor_tensor(rs[:, :], ve[:, :], neghalf[:, :], ALU.pow).then_inc(S["rs"], 1)
                else:
                    pool.wait_ge(S["ve"], n)
                    pool.tensor_tensor(rs[:, :], ve[:, :], neghalf[:, :], ALU.pow).then_inc(S["rs"], 1)
                if lf is not None:
                    g = n - 1 - NG * lf
                    reach(pool, S["xn"], n)
                    for t in range(GT):
                        ins = pool.tensor_tensor(xt(g, t), xt(g, t), b2_all[:, lf * D:(lf + 1) * D], ALU.add)
                    ins.then_inc(S["xb"], 1)

            def between(n, la, lf):
                step(n, la, lf)
                if lf is None:
                    pool.wait_ge(S["t1_full"], n + 1)
                else:
                    pool.wait_ge(S["t2_full"], n)
                if la is not None and not at(n, STEPS - 1):
                    stage(n + 1, 1 if isinstance(n, int) and n + 1 >= NG else la)
                if at(n, NG - 1):
                    lo_qkv(1)
                if at(n, NG):
                    lo_o(1)
                    lo_2(1)
                    lo_1(1)

            pool.memset(ident[:, :], 0.0).then_inc(S["ident"], 1)
            pool.memset(mask[:, :], 0.0).then_inc(S["maskz"], 1)
            pool.wait_ge(S["ident"], 1)
            pool.affine_select(out=ident[:, :], in_=ident[:, :], compare_op=ALU.not_equal, fill=1.0, base=0,
                               pattern=[[-1, P]], channel_multiplier=1).then_inc(S["ident"], 1)
            pool.wait_ge(S["maskz"], 1)
            for i, sign in ((0, 1), (1, -1), (2, 1)):
                m = mask[:, i * P:(i + 1) * P]
                ins = pool.affine_select(out=m, in_=m, compare_op=ALU.is_ge, fill=FAR, base=0, pattern=[[-sign, P]], channel_multiplier=sign)
            ins.then_inc(S["mask"], 1)
            pool.wait_ge(S["padp"], 1)
            for g in range(NG):
                pool.wait_ge(S["x0_ve"], g + 1)
                pool.tensor_tensor(rs[:, :], ve[:, :], neghalf[:, :], ALU.pow).then_inc(S["x0_rs"], 1)
                if g == 0:
                    stage(0, 0)
            lo_qkv(0)
            lo_o(0)
            lo_2(0)
            lo_1(0)

            steps(pool, between)
            for g in range(NG):
                if g:
                    pool.wait_ge(S["fin"], g)
                else:
                    pool.wait_ge(S["x_ready"], NG + STEPS)
                pool.dma_start(hres[:, :, :], out_v[:, GT * g:GT * g + GT, :]).then_inc(S["h_in"], 16)
                pool.wait_ge(S["fin"], g + 1)
                pool.dma_start(out_v[:, GT * g:GT * g + GT, :], X[:, GT * g:GT * g + GT, :]).then_inc(S["stored"], 16)
            pool.wait_ge(S["stored"], 16 * NG)


def program(nc, dram, out, phases=3):
    def run(phase, *args):
        sems = []
        phase(nc, sems, X, dram, *args)
        nc.clear_and_free_semaphores(sems)
        nc.all_engine_barrier()

    with ExitStack() as ctx:
        ctx.enter_context(nc.allow_non_contiguous_dma(reason="short vectors, loaded once"))
        X = ctx.enter_context(nc.sbuf_tensor("X", [P, NT, D], F32))
        run(tower_phase)
        if phases >= 2:
            run(attention_phase)
        if phases >= 3:
            run(window_phase, out)
            return
        s_out = ctx.enter_context(nc.semaphore("s_out"))
        with nc.Block() as block:
            @block.sync
            def _(sp):
                sp.dma_start(out.rearrange("s (t p) d -> p (s t) d", p=P), X[:, :, :]).then_inc(s_out, 16)
                sp.wait_ge(s_out, 16)


_INS = ["x", "L0_tok_emb", "L0_tok_pos_emb", "L0_tok_A_diag", "L0_tok_B", "L0_tok_C", "L0_tok_D", "L0_tok_w1", "L0_tok_b1",
        "L0_tok_w2", "L0_tok_b2", "L0_tok_ln1_s", "L0_tok_ln1_b", "L0_tok_ln2_s", "L0_tok_ln2_b", "L0_tok_lnf_s", "L0_tok_lnf_b",
        "L0_attn_Wq", "L0_attn_Wk", "L0_attn_Wv", "L0_attn_Wo", "L0_attn_gamma", "L0_ffn_wqkv", "L0_ffn_q_scale", "L0_ffn_k_scale",
        "L0_ffn_wo", "L0_ffn_ln_g", "L0_ffn_ln_b", "L0_ffn_w1", "L0_ffn_b1", "L0_ffn_w2", "L0_ffn_b2"]


def kernel(**inputs):
    import concourse.bacc as bacc
    from concourse.bass_utils import run_bass_kernel_spmd

    nc = bacc.Bacc("TRN2", target_bir_lowering=False, num_devices=1)
    arrays, dram = {}, {}
    for name, a in {**{n: inputs[n] for n in _INS}, **constants()}.items():
        a = np.ascontiguousarray(a)
        arrays[f"in_{name}"] = a
        dram[name] = nc.dram_tensor(f"in_{name}", a.shape, mybir.dt.from_np(a.dtype), kind="ExternalInput").ap()
    out = nc.dram_tensor("out", (8, 2 * P, D), F32, kind="ExternalOutput").ap()
    program(nc, dram, out)
    return run_bass_kernel_spmd(nc, [arrays], core_ids=[0]).results[0]["out"]
```

```python
import concourse.bass as bass
from concourse import mybir
from contextlib import ExitStack
import numpy as np

F32 = mybir.dt.float32
F32R = mybir.dt.float32r
I32 = mybir.dt.int32
U32 = mybir.dt.uint32
ALU = mybir.AluOpType
ACT = mybir.ActivationFunctionType
AX = mybir.AxisListType
ds = bass.ds

P = 128
NT = 16
GT = 4
GTOK = GT * P
NG = NT // GT
D = 256
DC = D // P
EPS = 1e-5


def reach(eng, sem, value, sem2=None, value2=None):
    if not isinstance(value, int):
        value = eng.to_reg(value)
    if sem2 is not None and not isinstance(value2, int):
        value2 = eng.to_reg(value2)
    eng.wait_ge(sem, 1)
    eng.wait_ge(sem, value)
    if sem2 is not None:
        eng.wait_ge(sem2, value2)


def attention_raw(raw):
    return (raw[:, 0:DC * 3 * D].rearrange("p (c n) -> p c n", c=DC),
            raw[:, DC * 3 * D:DC * 3 * D + 4 * D].rearrange("p (q n) -> p q n", q=4))


def tower_phase(nc, sems, X, dram, raw, wa):
    L, S, F = 4, 64, 1024
    FC = F // P
    V = dram["L0_tok_emb"].shape[0]
    STEPS = NG
    VECS = 8

    with ExitStack() as ctx:
        def sb(name, shape, dt=F32):
            return ctx.enter_context(nc.sbuf_tensor("t_" + name, shape, dt))

        def sem(name):
            sems.append(nc.alloc_semaphore("t_" + name))
            return sems[-1]

        raw_b = sb("raw_b", [P, DC, S])
        raw_c = sb("raw_c", [P, D])
        raw_d = sb("raw_d", [P, DC, D])
        raw_1 = sb("raw_1", [P, DC, F])
        raw_2 = sb("raw_2", [P, FC, D])
        b_cat = sb("b_cat", [P, DC, 2 * S], F32R)
        b_hiz = sb("b_hiz", [P, DC, 2 * S], F32R)
        c_hi = sb("c_hi", [P, D], F32R)
        c_lo = sb("c_lo", [P, D], F32R)
        d_hi = sb("d_hi", [P, DC, D], F32R)
        d_lo = sb("d_lo", [P, DC, D], F32R)
        w1_hi = sb("w1_hi", [P, DC, F], F32R)
        w1_lo = sb("w1_lo", [P, DC, F], F32R)
        w2_hi = sb("w2_hi", [P, FC, D], F32R)
        w2_lo = sb("w2_lo", [P, FC, D], F32R)
        ln_all = sb("ln_all", [P, 4, L * DC])
        ln_cur = sb("ln_cur", [P, 4, DC])
        fb_all = sb("fb_all", [P, L * FC])
        fb_cur = sb("fb_cur", [P, FC])
        b2_all = sb("b2_all", [P, L * D])
        a_raw = sb("a_raw", [P, L])
        a_all = sb("a_all", [P, L])
        keep = sb("keep", [P, GTOK])
        decay = sb("decay", [P, GTOK])
        neghalf = sb("neghalf", [P, GT])
        ids = sb("ids", [P, NT], I32)
        idm = sb("idm", [P, NT])
        idf = sb("idf", [P, NT])
        idx = sb("idx", [P, NT], U32)
        pos = sb("pos", [P, 2, D])
        ident = sb("ident", [P, P])
        st = [sb(f"st{k}", [P, GT, 6]) for k in (1, 2)]
        mv = [sb(f"mv{k}", [P, GT, 2]) for k in (1, 2)]
        ve = [sb(f"ve{k}", [P, GT]) for k in (1, 2)]
        rs = [sb(f"rs{k}", [P, GT]) for k in (1, 2)]
        xn = [sb(f"xn{k}", [P, GT, D]) for k in (1, 2)]
        nf = [sb(f"nf{k}", [P, DC, GTOK]) for k in (1, 2)]
        nh = [sb(f"nh{k}", [P, DC, GTOK], F32R) for k in (1, 2)]
        nl = [sb(f"nl{k}", [P, DC, GTOK], F32R) for k in (1, 2)]
        hs = sb("hs", [P, GTOK])
        hs_hi = sb("hs_hi", [P, GTOK], F32R)
        hs_lo = sb("hs_lo", [P, GTOK], F32R)
        gf = sb("gf", [P, 2, GTOK])
        g_hi = sb("g_hi", [P, 4, GTOK], F32R)
        g_lo = sb("g_lo", [P, 4, GTOK], F32R)

        def bank(name, n=1):
            return ctx.enter_context(nc.psum_tensor("t_" + name, [P, n, 512], F32))

        ps_t = bank("ps_t", 2)
        ps_u = bank("ps_u")
        ps_f = bank("ps_f", 2)
        ps_o = bank("ps_o", 2)

        s_ids, s_idm, s_idf, s_idx = sem("ids"), sem("idm"), sem("idf"), sem("idx")
        s_vec, s_pos, s_gather = sem("vec"), sem("pos"), [sem(f"gather{g}") for g in range(NG)]
        s_ident, s_keep, s_decay, s_sig = sem("ident"), sem("keep"), sem("decay"), sem("sig")
        raw_front, raw_w1, raw_w2 = sem("raw_front"), sem("raw_w1"), sem("raw_w2")
        front_hi, front_split = sem("front_hi"), sem("front_split")
        w1_h, w1_split, w2_h, w2_split = sem("w1_h"), sem("w1_split"), sem("w2_h"), sem("w2_split")
        cur_ready = sem("cur_ready")
        x_ready, xb_ready, xy_ready = sem("x_ready"), sem("xb_ready"), sem("xy_ready")
        st_done = [sem(f"st_done{k}") for k in (1, 2)]
        mv_done = [sem(f"mv_done{k}") for k in (1, 2)]
        ve_done = [sem(f"ve_done{k}") for k in (1, 2)]
        rs_done = [sem(f"rs_done{k}") for k in (1, 2)]
        xn_ready = [sem(f"xn_ready{k}") for k in (1, 2)]
        t_full = [sem(f"t_full{k}") for k in (1, 2)]
        nf_done = [sem(f"nf_done{k}") for k in (1, 2)]
        n_split = [sem(f"n_split{k}") for k in (1, 2)]
        pf_free = sem("pf_free")
        u_full, scanned, hs_hi_done, hs_split = sem("u_full"), sem("scanned"), sem("hs_hi_done"), sem("hs_split")
        y_full, f_full = sem("y_full"), sem("f_full")
        g_hi_done, g_split, g_used = sem("g_hi_done"), sem("g_split"), sem("g_used")

        raw_w, raw_o = attention_raw(raw)
        wa_raw, wa_zero, wa_h, wa_l = sem("wa_raw"), sem("wa_zero"), sem("wa_h"), sem("wa_l")
        wa_parts = [(wa[0][:, c, :], wa[1][:, c, :], raw_w[:, c, :]) for c in range(DC)]
        wa_parts += [(wa[2][:, 2 * c:2 * c + 2, :], wa[3][:, 2 * c:2 * c + 2, :], raw_o[:, 2 * c:2 * c + 2, :]) for c in range(2)]

        def tiles(g):
            return range(GT * g, GT * g + GT)

        block = ctx.enter_context(nc.Block())

        def front_parts(eng, l):
            eng.tensor_copy(b_cat[:, :, 0:S], raw_b[:, :, :])
            eng.tensor_copy(b_hiz[:, :, 0:S], raw_b[:, :, :])
            eng.tensor_copy(c_hi[:, :], raw_c[:, :])
            eng.tensor_copy(d_hi[:, :, :], raw_d[:, :, :]).then_inc(front_hi, 1)
            eng.wait_ge(front_hi, l + 1)
            eng.tensor_tensor(b_cat[:, :, S:2 * S], raw_b[:, :, :], b_cat[:, :, 0:S].bitcast(F32), ALU.subtract)
            eng.tensor_tensor(c_lo[:, :], raw_c[:, :], c_hi[:, :].bitcast(F32), ALU.subtract)
            eng.tensor_tensor(d_lo[:, :, :], raw_d[:, :, :], d_hi[:, :, :].bitcast(F32), ALU.subtract).then_inc(front_split, 1)

        def num(l, g):
            return l * STEPS + g

        def after(l, g, k):
            return (l + (g + k) // STEPS, (g + k) % STEPS)

        @block.sync
        def _(sp):
            sp.dma_start(ids[:, :], dram["x"].rearrange("s (t p) -> p (s t)", p=P)).then_inc(s_ids, 16)
            sp.dma_start(pos[:, :, :], dram["L0_tok_pos_emb"][0:2 * P, :].rearrange("(t p) d -> p t d", p=P)).then_inc(s_pos, 16)
            for l in range(L):
                if l >= 1:
                    sp.wait_ge(front_split, l)
                sp.dma_start(raw_b[:, :, :], dram["L0_tok_B"][l].rearrange("(c p) s -> p c s", p=P)).then_inc(raw_front, 16)
                sp.dma_start(raw_c[0:S, :], dram["L0_tok_C"][l]).then_inc(raw_front, 16)
                sp.dma_start(raw_c[S:2 * S, :], dram["L0_tok_C"][l]).then_inc(raw_front, 16)
                sp.dma_start(raw_d[:, :, :], dram["L0_tok_D"][l].rearrange("(c p) s -> p c s", p=P)).then_inc(raw_front, 16)
                if l >= 1:
                    sp.wait_ge(w1_split, FC * l)
                sp.dma_start(raw_1[:, :, :], dram["L0_tok_w1"][l].rearrange("(c p) s -> p c s", p=P)).then_inc(raw_w1, 16)
                if l >= 1:
                    sp.wait_ge(w2_split, FC * l)
                sp.dma_start(raw_2[:, :, :], dram["L0_tok_w2"][l].rearrange("(c p) s -> p c s", p=P)).then_inc(raw_w2, 16)
                if l == 0:
                    for i, name in enumerate(("L0_attn_Wq", "L0_attn_Wk", "L0_attn_Wv")):
                        sp.dma_start(raw_w[:, :, D * i:D * i + D], dram[name].rearrange("(c p) n -> p c n", p=P)).then_inc(wa_raw, 16)
                    sp.wait_ge(wa_zero, 1)
                    wo = dram["L0_attn_Wo"].rearrange("(q j d) n -> j d q n", j=4, d=16)
                    for j in range(4):
                        sp.dma_start(raw_o[32 * j:32 * j + 16, :, :], wo[j]).then_inc(wa_raw, 16)

        @block.tensor
        def _(pe):
            def transposes(k, l, g):
                n = num(l, g)
                pe.wait_ge(xn_ready[k], n + 1)
                if k == 0:
                    pe.wait_ge(nf_done[1], n * DC + 1)
                for c in range(DC):
                    for t in range(GT):
                        mm = pe.transpose(ps_t[:, c, t * P:(t + 1) * P], xn[k][:, t, c * P:(c + 1) * P], ident[:, :])
                mm.then_inc(t_full[k], 1)

            def state_in(l, g):
                n = num(l, g)
                if g == 0:
                    pe.wait_ge(front_split, l + 1)
                pe.wait_ge(n_split[0], n * 2 + 2)
                pe.wait_ge(scanned, n + 1)
                for c in range(DC):
                    pe.matmul(ps_u[:, 0, :], b_cat[:, c, :], nh[0][:, c, :], start=(c == 0), stop=False)
                    mm = pe.matmul(ps_u[:, 0, :], b_hiz[:, c, :], nl[0][:, c, :], start=False, stop=(c == DC - 1))
                mm.then_inc(u_full, 1)

            def state_out(l, g):
                n = num(l, g)
                pe.wait_ge(hs_split, n + 1)
                for t in range(GT):
                    tok = slice(t * P, (t + 1) * P)
                    out = ps_t[:, t // 2, (t % 2) * D:(t % 2 + 1) * D]
                    passes = [(nh[0][:, c, tok], w[:, c, :]) for c in range(DC) for w in (d_hi, d_lo)]
                    passes += [(nl[0][:, c, tok], d_hi[:, c, :]) for c in range(DC)]
                    passes += [(hs_hi[:, tok], c_hi[:, :]), (hs_hi[:, tok], c_lo[:, :]), (hs_lo[:, tok], c_hi[:, :])]
                    for i, (a, w) in enumerate(passes):
                        mm = pe.matmul(out, a, w, start=(t % 2 == 0 and i == 0),
                                       stop=(t % 2 == 1 and i == len(passes) - 1), skip_group_check=True)
                mm.then_inc(y_full, 1)

            def hidden(l, g, j):
                n = num(l, g)
                if g == 0:
                    pe.wait_ge(w1_split, l * FC + j + 1)
                if j == 0:
                    pe.wait_ge(n_split[1], n * 2 + 2)
                pe.wait_ge(pf_free, n * FC + j + 1)
                col = slice(j * P, (j + 1) * P)
                for c in range(DC):
                    pe.matmul(ps_f[:, j % 2, :], w1_hi[:, c, col], nh[1][:, c, :], start=(c == 0), stop=False)
                    pe.matmul(ps_f[:, j % 2, :], w1_lo[:, c, col], nh[1][:, c, :], start=False, stop=False)
                    mm = pe.matmul(ps_f[:, j % 2, :], w1_hi[:, c, col], nl[1][:, c, :], start=False, stop=(c == DC - 1))
                mm.then_inc(f_full, 1)

            def output(l, g, j):
                n = num(l, g)
                if g == 0:
                    pe.wait_ge(w2_split, l * FC + j + 1)
                if j == 0:
                    pe.wait_ge(x_ready, n + NG)
                pe.wait_ge(g_split, n * FC + j + 3)
                for t in range(GT):
                    tok = slice(t * P, (t + 1) * P)
                    out = ps_o[:, t // 2, (t % 2) * D:(t % 2 + 1) * D]
                    pe.matmul(out, g_hi[:, j % 4, tok], w2_hi[:, j, :], start=(j == 0 and t % 2 == 0), stop=False, skip_group_check=True)
                    pe.matmul(out, g_hi[:, j % 4, tok], w2_lo[:, j, :], start=False, stop=False, skip_group_check=True)
                    mm = pe.matmul(out, g_lo[:, j % 4, tok], w2_hi[:, j, :], start=False,
                                   stop=(j == FC - 1 and t % 2 == 1), skip_group_check=True)
                mm.then_inc(g_used, 1)

            def step(l, g, front):
                nx = after(l, g, 1)
                hidden(l, g, 0)
                hidden(l, g, 1)
                if front:
                    transposes(0, *nx)
                for j in range(2, FC):
                    hidden(l, g, j)
                    if front and j == 3:
                        state_in(*nx)
                    if front and j == 4:
                        state_out(*nx)
                    if front and j == FC - 1:
                        transposes(1, *nx)
                    output(l, g, j - 2)
                output(l, g, FC - 2)
                output(l, g, FC - 1)

            for s in (t_full[0], t_full[1], nf_done[0], nf_done[1], scanned):
                pe.sem_inc(s, 1)
            pe.sem_inc(pf_free, 2)
            pe.wait_ge(s_ident, 2)
            transposes(0, 0, 0)
            state_in(0, 0)
            state_out(0, 0)
            transposes(1, 0, 0)
            with pe.Fori(0, L - 1) as l:
                for g in range(STEPS):
                    step(l, g, True)
            for g in range(STEPS):
                step(L - 1, g, g < STEPS - 1)

        @block.scalar
        def _(act):
            def spread(k, l, g):
                n = num(l, g)
                act.wait_ge(t_full[k], n + 2)
                for c in range(DC):
                    s = ln_cur[:, 2 * k, c:c + 1]
                    b = ln_cur[:, 2 * k + 1, c:c + 1]
                    act.activation(nf[k][:, c, :], ps_t[:, c, :], ACT.Identity, bias=b, scale=s)
                    ins = act.activation(nh[k][:, c, :], ps_t[:, c, :], ACT.Identity, bias=b, scale=s)
                    ins.then_inc(nf_done[k], 1)

            def state_hi(l, g):
                act.wait_ge(scanned, num(l, g) + 2)
                act.activation(hs_hi[:, :], hs[:, :], ACT.Copy).then_inc(hs_hi_done, 1)

            def gelu(l, g, j):
                n = num(l, g) * FC + j
                act.wait_ge(f_full, n + 1)
                act.wait_ge(g_used, n + 1)
                act.wait_ge(g_split, n + 1)
                act.activation(gf[:, j % 2, :], ps_f[:, j % 2, :], ACT.Gelu, bias=fb_cur[:, j:j + 1]).then_inc(pf_free, 1)
                act.wait_ge(pf_free, n + 3)
                act.activation(g_hi[:, j % 4, :], gf[:, j % 2, :], ACT.Copy).then_inc(g_hi_done, 1)

            def take_ln(l, count):
                act.activation(ln_cur[:, :, :], ln_all[:, :, ds(l * DC, DC)], ACT.Copy).then_inc(cur_ready, 1)
                act.wait_ge(cur_ready, count)

            def take_fb(l, count):
                act.activation(fb_cur[:, :], fb_all[:, ds(l * FC, FC)], ACT.Copy).then_inc(cur_ready, 1)
                act.wait_ge(cur_ready, count)

            def w1_hi_part(l, j, used):
                act.wait_ge(raw_w1, l * 16 + 16)
                if used is not None:
                    act.wait_ge(f_full, used)
                act.activation(w1_hi[:, :, j * P:(j + 1) * P], raw_1[:, :, j * P:(j + 1) * P], ACT.Copy).then_inc(w1_h, 1)

            def w2_hi_part(l, j, used):
                act.wait_ge(raw_w2, l * 16 + 16)
                if used is not None:
                    act.wait_ge(g_used, used)
                act.activation(w2_hi[:, j, :], raw_2[:, j, :], ACT.Copy).then_inc(w2_h, 1)

            def step(l, g, front):
                nx = after(l, g, 1)
                n = num(l, g) * FC
                prep = front and g == STEPS - 1
                if g == 0:
                    act.wait_ge(pf_free, n + 2)
                    take_fb(l, l * 2 + 2)
                if prep:
                    act.wait_ge(nf_done[1], num(l, g) * DC + DC + 1)
                    take_ln(l + 1, l * 2 + 3)
                for j in range(FC):
                    gelu(l, g, j)
                    if front and j == 1:
                        spread(0, *nx)
                    if front and j == 3:
                        state_hi(*nx)
                    if prep:
                        w1_hi_part(l + 1, j, n + j + 1)
                        if j >= 3:
                            w2_hi_part(l + 1, j - 3, n + 4 + j - 2)
                if front:
                    spread(1, *nx)
                if prep:
                    for j in range(FC - 3, FC):
                        w2_hi_part(l + 1, j, n + 4 + j + 1)
                if isinstance(l, int):
                    act.wait_ge(wa_raw, 16 * 7)
                    act.activation(wa_parts[g][0], wa_parts[g][2], ACT.Copy).then_inc(wa_h, 1)

            for k, name in enumerate(("L0_tok_ln1_s", "L0_tok_ln1_b", "L0_tok_ln2_s", "L0_tok_ln2_b")):
                act.dma_start(ln_all[:, k, :], dram[name].rearrange("l (c p) -> p (l c)", p=P)).then_inc(s_vec, 16)
            act.dma_start(a_raw[0:S, :], dram["L0_tok_A_diag"].rearrange("l s -> s l")).then_inc(s_vec, 16)
            act.dma_start(a_raw[S:2 * S, :], dram["L0_tok_A_diag"].rearrange("l s -> s l")).then_inc(s_vec, 16)
            act.dma_start(fb_all[:, :], dram["L0_tok_b1"].rearrange("l (c p) -> p (l c)", p=P)).then_inc(s_vec, 16)
            act.dma_start(b2_all[:, :], dram["L0_tok_b2"].rearrange("(a l) d -> a (l d)", a=1).broadcast_to([P, L * D])).then_inc(s_vec, 16)
            act.sem_inc(g_used, 4)
            act.sem_inc(g_split, 2)
            act.wait_ge(s_vec, 16 * VECS)
            act.activation(a_all[:, :], a_raw[:, :], ACT.Sigmoid).then_inc(s_sig, 1)
            take_ln(0, 1)
            spread(0, 0, 0)
            for j in range(FC):
                w1_hi_part(0, j, None)
            state_hi(0, 0)
            spread(1, 0, 0)
            for j in range(FC):
                w2_hi_part(0, j, None)
            with act.Fori(0, L - 1) as l:
                for g in range(STEPS):
                    step(l, g, True)
            for g in range(STEPS):
                step(L - 1, g, g < STEPS - 1)


        @block.vector
        def _(dve):
            def grp(g):
                return X[:, GT * g:GT * g + GT, :]

            def stats(k, l, g):
                n = num(l, g)
                if k == 0:
                    reach(dve, x_ready, n + 1)
                else:
                    reach(dve, xy_ready, n + 1)
                for t in range(GT):
                    ins = dve.bn_stats(st[k][:, t, :], X[:, GT * g + t, :])
                ins.then_inc(st_done[k], 1)
                reach(dve, st_done[k], n + 1)
                for t in range(GT):
                    ins = dve.bn_aggr(mv[k][:, t, :], st[k][:, t, :])
                ins.then_inc(mv_done[k], 1)
                dve.wait_ge(mv_done[k], n + 1)
                dve.tensor_scalar(ve[k][:, :], mv[k][:, :, 1], EPS, None, ALU.add).then_inc(ve_done[k], 1)

            def norm(k, l, g):
                n = num(l, g)
                dve.wait_ge(rs_done[k], n + 1)
                dve.wait_ge(t_full[k], n + 1)
                for t in range(GT):
                    ins = dve.tensor_scalar(xn[k][:, t, :], X[:, GT * g + t, :], mv[k][:, t, 0:1], rs[k][:, t:t + 1],
                                            ALU.subtract, ALU.mult)
                ins.then_inc(xn_ready[k], 1)

            def spread_lo(k, l, g):
                n = num(l, g)
                for c in range(DC):
                    dve.wait_ge(nf_done[k], n * DC + c + 2)
                    dve.tensor_tensor(nl[k][:, c, :], nf[k][:, c, :], nh[k][:, c, :].bitcast(F32),
                                      ALU.subtract).then_inc(n_split[k], 1)

            def scan(l, g):
                n = num(l, g)
                dve.wait_ge(u_full, n + 1)
                dve.tensor_tensor_scan(hs[:, :], decay[:, :], ps_u[:, 0, :], 0.0, ALU.mult, ALU.add).then_inc(scanned, 1)

            def state_lo(l, g):
                n = num(l, g)
                dve.wait_ge(hs_hi_done, n + 1)
                dve.tensor_tensor(hs_lo[:, :], hs[:, :], hs_hi[:, :].bitcast(F32), ALU.subtract).then_inc(hs_split, 1)

            def add_state(l, g):
                n = num(l, g)
                dve.wait_ge(y_full, n + 1)
                for h in range(2):
                    x2 = X[:, GT * g + 2 * h:GT * g + 2 * h + 2, :].rearrange("p t d -> p (t d)")
                    ins = dve.tensor_tensor(x2, ps_t[:, h, :], x2, ALU.add)
                ins.then_inc(xy_ready, 1)

            def gelu_lo(l, g, j):
                n = num(l, g) * FC + j
                dve.wait_ge(g_hi_done, n + 1)
                dve.tensor_tensor(g_lo[:, j % 4, :], gf[:, j % 2, :], g_hi[:, j % 4, :].bitcast(F32),
                                  ALU.subtract).then_inc(g_split, 1)

            def add_output(l, g):
                n = num(l, g)
                dve.wait_ge(xb_ready, n + 1)
                dve.wait_ge(g_used, n * FC + FC + 4)
                for h in range(2):
                    x2 = X[:, GT * g + 2 * h:GT * g + 2 * h + 2, :].rearrange("p t d -> p (t d)")
                    ins = dve.tensor_tensor(x2, ps_o[:, h, :], x2, ALU.add)
                ins.then_inc(x_ready, 1)

            def set_decay(l, count):
                dve.tensor_scalar(decay[:, :], keep[:, :], a_all[:, ds(l, 1)], None, ALU.mult).then_inc(s_decay, 1)
                dve.wait_ge(s_decay, count)

            def step(l, g, front, ahead):
                nx, n2 = after(l, g, 1), after(l, g, 2)
                if front and g == STEPS - 1:
                    set_decay(l + 1, l + 2)
                gelu_lo(l, g, 0)
                gelu_lo(l, g, 1)
                if front:
                    spread_lo(0, *nx)
                gelu_lo(l, g, 2)
                if front:
                    scan(*nx)
                gelu_lo(l, g, 3)
                if front:
                    state_lo(*nx)
                gelu_lo(l, g, 4)
                if front:
                    add_state(*nx)
                    stats(1, *nx)
                gelu_lo(l, g, 5)
                if front:
                    norm(1, *nx)
                gelu_lo(l, g, 6)
                if ahead:
                    stats(0, *n2)
                gelu_lo(l, g, 7)
                if front:
                    spread_lo(1, *nx)
                if ahead:
                    norm(0, *n2)
                add_output(l, g)

            dve.wait_ge(s_ids, 16)
            dve.tensor_scalar(idm[:, :], ids[:, :], 0.0, float(V), ALU.is_lt, ALU.mult).then_inc(s_idm, 1)
            dve.wait_ge(s_idm, 1)
            dve.tensor_tensor(idf[:, :], ids[:, :], idm[:, :], ALU.add).then_inc(s_idf, 1)
            dve.wait_ge(s_idf, 1)
            dve.tensor_scalar(idx[:, :], idf[:, :], 0.0, float(V - 1), ALU.max, ALU.min).then_inc(s_idx, 1)
            dve.memset(keep[:, :], 1.0).then_inc(s_keep, 1)
            dve.wait_ge(s_keep, 1)
            dve.memset(keep[:, :].rearrange("p (s t) -> p s t", t=2 * P)[:, :, 0:1], 0.0).then_inc(s_keep, 1)
            dve.memset(neghalf[:, :], -0.5).then_inc(s_keep, 1)
            dve.memset(b_hiz[:, :, :].bitcast(F32), 0.0).then_inc(s_keep, 1)
            dve.wait_ge(s_keep, 4)
            dve.wait_ge(raw_front, 64)
            front_parts(dve, 0)
            dve.wait_ge(s_pos, 16)

            def add_positions(g):
                dve.wait_ge(s_gather[g], 16 * GT)
                for h in range(2):
                    x2 = X[:, GT * g + 2 * h:GT * g + 2 * h + 2, :]
                    ins = dve.tensor_tensor(x2, x2, pos[:, :, :], ALU.add)
                ins.then_inc(x_ready, 1)

            add_positions(0)
            stats(0, 0, 0)
            norm(0, 0, 0)
            dve.wait_ge(s_sig, 1)
            set_decay(0, 1)
            spread_lo(0, 0, 0)
            add_positions(1)
            scan(0, 0)
            state_lo(0, 0)
            add_positions(2)
            add_positions(3)
            add_state(0, 0)
            stats(1, 0, 0)
            norm(1, 0, 0)
            stats(0, 0, 1)
            norm(0, 0, 1)
            spread_lo(1, 0, 0)
            with dve.Fori(0, L - 1) as l:
                for g in range(STEPS):
                    step(l, g, True, True)
            for g in range(STEPS):
                step(L - 1, g, g < STEPS - 1, g < STEPS - 2)

        @block.gpsimd
        def _(pool):
            def rstd(k, l, g):
                pool.wait_ge(ve_done[k], num(l, g) + 1)
                pool.tensor_tensor(rs[k][:, :], ve[k][:, :], neghalf[:, :], ALU.pow).then_inc(rs_done[k], 1)

            def add_bias(l, g):
                reach(pool, xn_ready[1], num(l, g) + 1)
                for t in tiles(g):
                    ins = pool.tensor_tensor(X[:, t, :], X[:, t, :], b2_all[:, ds(l * D, D)], ALU.add)
                ins.then_inc(xb_ready, 1)

            def split_front(l):
                pool.wait_ge(raw_front, l * 64 + 64)
                reach(pool, y_full, l * STEPS)
                front_parts(pool, l)

            def w1_lo_part(l, j):
                pool.wait_ge(w1_h, l * FC + j + 1)
                col = slice(j * P, (j + 1) * P)
                pool.tensor_tensor(w1_lo[:, :, col], raw_1[:, :, col], w1_hi[:, :, col].bitcast(F32), ALU.subtract).then_inc(w1_split, 1)

            def w2_lo_part(l, j):
                pool.wait_ge(w2_h, l * FC + j + 1)
                pool.tensor_tensor(w2_lo[:, j, :], raw_2[:, j, :], w2_hi[:, j, :].bitcast(F32), ALU.subtract).then_inc(w2_split, 1)

            def step(l, g, front, ahead):
                nx, n2 = after(l, g, 1), after(l, g, 2)
                prep = front and g == STEPS - 1
                if prep:
                    for j in range(4):
                        w1_lo_part(l + 1, j)
                if front and g == STEPS - 2 and ahead:
                    split_front(l + 1)
                if front:
                    rstd(1, *nx)
                    add_bias(*nx)
                if ahead:
                    rstd(0, *n2)
                if prep:
                    for j in range(4, FC):
                        w1_lo_part(l + 1, j)
                    for j in range(FC):
                        w2_lo_part(l + 1, j)
                if isinstance(l, int):
                    pool.wait_ge(wa_h, g + 1)
                    hi, lo, whole = wa_parts[g]
                    pool.tensor_tensor(lo, whole, hi.bitcast(F32), ALU.subtract).then_inc(wa_l, 1)

            pool.memset(ident[:, :], 0.0).then_inc(s_ident, 1)
            pool.memset(raw_o[:, :, :], 0.0).then_inc(wa_zero, 1)

            def gather(t):
                pool.indirect_dma_start(X[:, t, :], None, dram["L0_tok_emb"][:, :],
                                        bass.IndirectOffsetOnAxis(ap=idx[:, t:t + 1], axis=0)).then_inc(s_gather[t // GT], 16)

            pool.wait_ge(s_idx, 1)
            for t in range(2 * GT):
                gather(t)
            pool.wait_ge(s_ident, 1)
            pool.affine_select(out=ident[:, :], in_=ident[:, :], compare_op=ALU.not_equal, fill=1.0, base=0,
                               pattern=[[-1, P]], channel_multiplier=1).then_inc(s_ident, 1)
            pool.wait_ge(s_keep, 4)
            rstd(0, 0, 0)
            for t in range(2 * GT, NT):
                gather(t)
            for j in range(FC):
                w1_lo_part(0, j)
            rstd(1, 0, 0)
            pool.wait_ge(s_vec, 16 * VECS)
            add_bias(0, 0)
            rstd(0, 0, 1)
            for j in range(FC):
                w2_lo_part(0, j)
            with pool.Fori(0, L - 1) as l:
                for g in range(STEPS):
                    step(l, g, True, True)
            for g in range(STEPS):
                step(L - 1, g, g < STEPS - 1, g < STEPS - 2)


def attention_phase(nc, sems, X, dram, wa, out, raw, qkv):
    H, HD = 16, 16
    ROW = 64
    HP = H // 2
    QUAD, HQ = 4, H // 4
    SCALE = HD ** -0.5
    SEQS = 2
    SCORES = 3 * P
    BANKS = 4
    SLOTS = 8
    AHEAD = 6
    LAG = 3
    OUT = H + AHEAD
    VECS = 3
    NS = SEQS * H

    with ExitStack() as ctx:
        def sb(name, shape, dt=F32):
            return ctx.enter_context(nc.sbuf_tensor("a_" + name, shape, dt))

        def sem(name):
            sems.append(nc.alloc_semaphore("a_" + name))
            return sems[-1]

        def bank(name, n=1):
            return ctx.enter_context(nc.psum_tensor("a_" + name, [P, n, 512], F32))

        w_hi, w_lo, wo_hi, wo_lo = wa
        fs = sb("fs", [P, D])
        fb = sb("fb", [P, D])
        gam = sb("gam", [P, H])
        gsc = sb("gsc", [P, H])
        neghalf = sb("neghalf", [P, GT])
        ident = sb("ident", [P, P])
        st = sb("st", [P, GT, 6])
        mv = sb("mv", [P, GT, 2])
        ve = sb("ve", [P, GT])
        rs = sb("rs", [P, GT])
        xn = sb("xn", [P, GT, D])
        nh = sb("nh", [P, DC, GTOK], F32R)
        nl = sb("nl", [P, DC, GTOK], F32R)
        sq = sb("sq", [P, 2 * D])
        nrm = sb("nrm", [P, 2 * H])
        qs = [sb(f"qs{i}", [P, H, ROW], F32R) for i in range(2)]
        ks = [sb(f"ks{i}", [P, H, ROW], F32R) for i in range(2)]
        v = sb("v", [P, GT, H, 2 * HD])
        qt = sb("qt", [P, HP, GTOK], F32R)
        kt = sb("kt", [P, HP, GTOK], F32R)
        dist = sb("dist", [P, BANKS, SCORES])
        e = sb("e", [P, SLOTS, SCORES])
        ot_hi = sb("ot_hi", [P, HQ, 2 * P], F32R)
        ot_lo = sb("ot_lo", [P, HQ, 2 * P], F32R)

        ps_w = bank("ps_w", BANKS)
        ps_t, ps_d = ps_w[:, 0:2, :], ps_w[:, 2:4, :]
        ps_p = bank("ps_p", 2)
        ps_qk, ps_v = ps_p[:, 0:1, :], ps_p[:, 1:2, :]
        ps_o = bank("ps_o", 2)
        ps_s = (ps_o, ps_p)

        s_vec, s_ident, s_gsc, s_pad, s_stored = (sem(x) for x in ("vec", "ident", "gsc", "pad", "stored"))
        s_qkv, qkv_h, qkv_l = sem("qkv"), sem("qkv_h"), sem("qkv_l")
        st_done, mv_done, ve_done, rs_done, xn_ready = (sem(x) for x in ("st", "mv", "ve", "rs", "xn"))
        h_mul, h_ready = sem("h_mul"), sem("h_ready")
        t_full, nh_done, n_split = sem("t_full"), sem("nh_done"), sem("n_split")
        qk_full, v_full, sq_done, qk_hi, qk_read, v_done = (sem(x) for x in ("qk_full", "v_full", "sq_done", "qk_hi", "qk_read", "v_done"))
        nrm_done, nrm_hi, stacked, s_full, qt_done, kt_done = (sem(x) for x in ("nrm", "nrm_hi", "stacked", "s_full", "qt_done", "kt_done"))
        d_full, relu_done, exp_done, masked, pv_done = (sem(x) for x in ("d_full", "relu", "exp", "masked", "pv"))
        ot_h, ot_split, y_full, y_added = sem("ot_h"), sem("ot_split"), sem("y_full"), sem("y_added")

        PART = 3072 // (NS // 4)

        def qkv_part(w, k):
            return w[:, :, :].rearrange("p c n -> p (c n)")[:, k * PART:(k + 1) * PART]

        def qkv_raw(k):
            return raw[:, k * PART:(k + 1) * PART]

        block = ctx.enter_context(nc.Block())

        @block.sync
        def _(sp):
            sp.dma_start(fs[:, :], dram["L0_tok_lnf_s"].rearrange("(a d) -> a d", a=1).broadcast_to([P, D])).then_inc(s_vec, 16)
            sp.dma_start(fb[:, :], dram["L0_tok_lnf_b"].rearrange("(a d) -> a d", a=1).broadcast_to([P, D])).then_inc(s_vec, 16)
            sp.dma_start(gam[:, :], dram["L0_attn_gamma"].rearrange("(a d) -> a d", a=1).broadcast_to([P, H])).then_inc(s_vec, 16)
            sp.dma_start(raw[:, :].rearrange("p (c n) -> p c n", c=DC), dram["L0_ffn_wqkv"][0].rearrange("(c p) n -> p c n", p=P)).then_inc(s_qkv, 16)
            for g in range(NG - 1):
                sp.wait_ge(y_added, g * SEQS + SEQS + 1)
                sp.dma_start(out.rearrange("s (t p) d -> p (s t) d", p=P)[:, GT * g:GT * g + GT, :], X[:, GT * g:GT * g + GT, :]).then_inc(s_stored, 16)
            sp.wait_ge(s_stored, 16 * (NG - 1))

        @block.tensor
        def _(pe):
            def turn_x(g):
                pe.wait_ge(xn_ready, g * 2 + 2)
                for c in range(DC):
                    for t in range(GT):
                        mm = pe.transpose(ps_t[:, c, t * P:(t + 1) * P], xn[:, t, c * P:(c + 1) * P], ident[:, :])
                mm.then_inc(t_full, 1)

            def group(g, ahead):
                def project(t):
                    tok = slice(t * P, (t + 1) * P)
                    pe.wait_ge(qk_read, g * GT + t + 1)
                    for out, lo, hi, full in ((ps_qk[:, 0, :], 0, 2 * D, qk_full), (ps_v[:, 0, 0:D], 2 * D, 3 * D, v_full)):
                        if lo:
                            pe.wait_ge(v_done, g * GT + t + 1)
                        for c in range(DC):
                            pe.matmul(out, nh[:, c, tok], w_hi[:, c, lo:hi], start=(c == 0), stop=False)
                            pe.matmul(out, nh[:, c, tok], w_lo[:, c, lo:hi], start=False, stop=False)
                            mm = pe.matmul(out, nl[:, c, tok], w_hi[:, c, lo:hi], start=False, stop=(c == DC - 1))
                        mm.then_inc(full, 1)

                def turn(t):
                    pe.wait_ge(stacked, g * GT + t + 2)
                    pe.wait_ge(qt_done, g * GT + t + 1)
                    pe.wait_ge(kt_done, g * GT + t + 1)
                    for dst, src in ((ps_t, qs[t % 2]), (ps_d, ks[t % 2])):
                        for hp in range(HP):
                            mm = pe.transpose(dst[:, hp // 4, (hp % 4) * P:(hp % 4 + 1) * P],
                                              src[:, 2 * hp:2 * hp + 2, :].rearrange("p h r -> p (h r)").bitcast(F32), ident[:, :])
                        mm.then_inc(s_full, 1)

                def distances(i):
                    h = i % H
                    s = i // H
                    n = g * NS + i
                    if i == 0:
                        pe.wait_ge(qt_done, g * GT + GT + 1)
                        pe.wait_ge(kt_done, g * GT + GT + 1)
                    pe.wait_ge(relu_done, n + 1)
                    rows = slice(ROW * (h % 2), ROW * (h % 2) + ROW)
                    t0, t1 = 2 * s * P, (2 * s + 1) * P
                    pe.matmul(ps_w[:, h % BANKS, 0:2 * P], kt[rows, h // 2, t1:t1 + P], qt[rows, h // 2, t0:t0 + 2 * P], start=True, stop=True)
                    pe.matmul(ps_w[:, h % BANKS, 2 * P:3 * P], kt[rows, h // 2, t0:t0 + P], qt[rows, h // 2, t0:t0 + P],
                              start=True, stop=True).then_inc(d_full, 1)

                def values(i):
                    s, h = divmod(i, H)
                    if i == 0:
                        pe.wait_ge(y_added, g * SEQS + 1)
                    if i == H:
                        pe.wait_ge(qk_read, g * GT + GT + 1)
                        pe.wait_ge(v_done, g * GT + GT + 1)
                    pe.wait_ge(masked, g * NS + i + 1)
                    j, q = h % QUAD, h // QUAD
                    out = ps_s[s][32 * j:32 * j + 32, q // 2, (q % 2) * 2 * P:(q % 2 + 1) * 2 * P]
                    pe.matmul(out, v[:, 2 * s + 1, h, :], e[:, h % SLOTS, 0:2 * P], start=True, stop=False, skip_group_check=True)
                    pe.matmul(out[:, 0:P], v[:, 2 * s, h, :], e[:, h % SLOTS, 2 * P:3 * P], start=False, stop=True,
                              skip_group_check=True).then_inc(pv_done, 1)

                def project_out(s, k):
                    t, q = divmod(k, HQ)
                    if k == 0:
                        pe.wait_ge(ot_split, g * SEQS + s + 2)
                    out = ps_o[:, s, t * D:(t + 1) * D]
                    tok = slice(t * P, (t + 1) * P)
                    pe.matmul(out, ot_hi[:, q, tok], wo_hi[:, q, :], start=(k == 0), stop=False, skip_group_check=True)
                    pe.matmul(out, ot_hi[:, q, tok], wo_lo[:, q, :], start=False, stop=False, skip_group_check=True)
                    mm = pe.matmul(out, ot_lo[:, q, tok], wo_hi[:, q, :], start=False, stop=(k == 2 * HQ - 1), skip_group_check=True)
                    if k == 2 * HQ - 1:
                        mm.then_inc(y_full, 1)

                pe.wait_ge(n_split, g * DC + DC)
                for t in range(GT):
                    project(t)
                    if t >= 1:
                        turn(t - 1)
                turn(GT - 1)
                for i in range(NS + AHEAD):
                    if i < NS:
                        distances(i)
                    if i >= AHEAD:
                        values(i - AHEAD)
                    if OUT + LAG < i <= OUT + LAG + 2 * HQ:
                        project_out(0, i - OUT - LAG - 1)
                    if ahead and i == NS + 1:
                        pe.wait_ge(relu_done, g * NS + NS - 2 + BANKS)
                        turn_x(g + 1)
                for k in range(2 * HQ):
                    project_out(1, k)

            for s in (y_added, qk_read, v_done, qt_done, kt_done, ot_split, nrm_done, s_full, y_full, t_full, stacked):
                pe.sem_inc(s, 1)
            pe.sem_inc(relu_done, BANKS)
            pe.wait_ge(s_ident, 2)
            pe.wait_ge(s_pad, 4)
            turn_x(0)
            with pe.Fori(0, NG - 1) as g:
                group(g, True)
            group(NG - 1, False)

        @block.scalar
        def _(act):
            def spread(g):
                act.wait_ge(t_full, g + 2)
                for c in range(DC):
                    act.activation(nh[:, c, :], ps_t[:, c, :], ACT.Copy).then_inc(nh_done, 1)

            def group(g, ahead):
                def stack(t):
                    n = g * GT + t
                    q = ps_qk[:, 0, 0:D].rearrange("p (h d) -> p h d", h=H)
                    k = ps_qk[:, 0, D:2 * D].rearrange("p (h d) -> p h d", h=H)
                    act.wait_ge(qk_full, n + 1)
                    act.wait_ge(nrm_done, n + 1)
                    act.activation(sq[:, :], ps_qk[:, 0, :], ACT.Square).then_inc(sq_done, 1)
                    act.wait_ge(s_full, (g * GT + max(t - 1, 0)) * 2 + 1)
                    act.activation(qs[t % 2][:, :, 0:HD], q, ACT.Copy)
                    act.activation(qs[t % 2][:, :, HD:2 * HD], q, ACT.Copy).then_inc(qk_hi, 1)
                    act.activation(ks[t % 2][:, :, 0:HD], k, ACT.Copy, scale=-2.0)
                    act.activation(ks[t % 2][:, :, 2 * HD:3 * HD], k, ACT.Copy, scale=-2.0).then_inc(qk_hi, 1)
                    act.wait_ge(v_full, n + 1)
                    act.wait_ge(pv_done, g * NS + SLOTS)
                    act.activation(v[:, t, :, 0:HD], ps_v[:, 0, 0:D].rearrange("p (h d) -> p h d", h=H), ACT.Copy).then_inc(v_done, 1)

                def turned(t):
                    n = g * GT + t
                    act.wait_ge(s_full, n * 2 + 2)
                    act.activation(qt[:, :, t * P:(t + 1) * P], ps_t[:, :, :].rearrange("p b (h t) -> p (b h) t", t=P), ACT.Copy).then_inc(qt_done, 1)

                for t in range(GT):
                    stack(t)
                    if t >= 1:
                        turned(t - 1)
                turned(GT - 1)
                def output_hi(s):
                    act.wait_ge(pv_done, g * NS + (s + 1) * H + SLOTS)
                    act.wait_ge(y_full, g * SEQS + s + 1)
                    for b in range(2):
                        act.activation(ot_hi[:, 2 * b:2 * b + 2, :].rearrange("p q t -> p (q t)"), ps_s[s][:, b, :], ACT.Copy).then_inc(ot_h, 1)

                for i in range(NS):
                    n = g * NS + i
                    act.wait_ge(relu_done, n + BANKS + 1)
                    act.wait_ge(pv_done, n + 1)
                    act.activation(e[:, i % SLOTS, :], dist[:, i % BANKS, :], ACT.Exp, scale=gsc[:, i % H:i % H + 1]).then_inc(exp_done, 1)
                    if i == OUT - 1:
                        output_hi(0)
                    if not ahead and i % 4 == 3:
                        act.wait_ge(s_qkv, 16)
                        act.activation(qkv_part(qkv[0], i // 4), qkv_raw(i // 4), ACT.Copy).then_inc(qkv_h, 1)
                if ahead:
                    spread(g + 1)
                output_hi(1)

            act.sem_inc(pv_done, SLOTS)
            act.wait_ge(s_gsc, 1)
            act.wait_ge(s_pad, 4)
            spread(0)
            with act.Fori(0, NG - 1) as g:
                group(g, True)
            group(NG - 1, False)

        @block.vector
        def _(dve):
            def norm_stats(g, k):
                if k:
                    reach(dve, h_ready, g + 1)
                for t in range(GT):
                    ins = dve.bn_stats(st[:, t, :], X[:, ds(g * GT + t, 1), :].rearrange("p a d -> p (a d)"))
                ins.then_inc(st_done, 1)

            def norm_variance(g, k):
                n = g * 2 + k
                reach(dve, st_done, n + 1)
                for t in range(GT):
                    ins = dve.bn_aggr(mv[:, t, :], st[:, t, :])
                ins.then_inc(mv_done, 1)
                dve.wait_ge(mv_done, n + 1)
                dve.tensor_scalar(ve[:, :], mv[:, :, 1], EPS, None, ALU.add).then_inc(ve_done, 1)

            def norm_apply(g, k, tiles):
                n = g * 2 + k
                dve.wait_ge(rs_done, n + 1)
                if k == 0:
                    dve.wait_ge(t_full, g + 1)
                for t in tiles:
                    ins = dve.tensor_scalar(xn[:, t, :], X[:, ds(g * GT + t, 1), :].rearrange("p a d -> p (a d)"), mv[:, t, 0:1], rs[:, t:t + 1],
                                            ALU.subtract, ALU.mult)
                if tiles[-1] == GT - 1:
                    ins.then_inc(xn_ready, 1)

            def split_x(g):
                for c in range(DC):
                    dve.wait_ge(nh_done, g * DC + c + 1)
                    dve.tensor_tensor(nl[:, c, :], ps_t[:, c, :], nh[:, c, :].bitcast(F32), ALU.subtract).then_inc(n_split, 1)

            def qkv_rest(k):
                dve.wait_ge(qkv_h, k + 1)
                dve.tensor_tensor(qkv_part(qkv[1], k), qkv_raw(k), qkv_part(qkv[0], k).bitcast(F32), ALU.subtract).then_inc(qkv_l, 1)

            def group(g, ahead):
                def stack(t):
                    n = g * GT + t
                    q = ps_qk[:, 0, 0:D].rearrange("p (h d) -> p h d", h=H)
                    k = ps_qk[:, 0, D:2 * D].rearrange("p (h d) -> p h d", h=H)
                    dve.wait_ge(sq_done, n + 1)
                    dve.wait_ge(stacked, n + 1)
                    dve.tensor_reduce(nrm[:, :], sq[:, :].rearrange("p (h d) -> p h d", d=HD), AX.X, ALU.add).then_inc(nrm_done, 1)
                    dve.wait_ge(qk_hi, n * 2 + 2)
                    dve.tensor_tensor(qs[t % 2][:, :, 2 * HD:3 * HD], q, qs[t % 2][:, :, 0:HD].bitcast(F32), ALU.subtract)
                    dve.wait_ge(nrm_done, n + 2)
                    dve.tensor_copy(qs[t % 2][:, :, 3 * HD:3 * HD + 1], nrm[:, 0:H].unsqueeze(2))
                    dve.tensor_copy(ks[t % 2][:, :, 3 * HD + 2:3 * HD + 3], nrm[:, H:2 * H].unsqueeze(2)).then_inc(nrm_hi, 1)
                    dve.scalar_tensor_tensor(ks[t % 2][:, :, HD:2 * HD], k, -2.0, ks[t % 2][:, :, 0:HD].bitcast(F32),
                                             ALU.mult, ALU.subtract).then_inc(qk_read, 1)
                    dve.wait_ge(nrm_hi, n + 1)
                    dve.tensor_tensor(qs[t % 2][:, :, 3 * HD + 1:3 * HD + 2], nrm[:, 0:H].unsqueeze(2),
                                      qs[t % 2][:, :, 3 * HD:3 * HD + 1].bitcast(F32), ALU.subtract)
                    dve.tensor_tensor(ks[t % 2][:, :, 3 * HD + 3:3 * HD + 4], nrm[:, H:2 * H].unsqueeze(2),
                                      ks[t % 2][:, :, 3 * HD + 2:3 * HD + 3].bitcast(F32), ALU.subtract).then_inc(stacked, 1)

                def turned(t):
                    n = g * GT + t
                    dve.wait_ge(s_full, n * 2 + 3)
                    dve.tensor_copy(kt[:, :, t * P:(t + 1) * P], ps_d[:, :, :].rearrange("p b (h t) -> p (b h) t", t=P)).then_inc(kt_done, 1)

                for t in range(GT):
                    stack(t)
                    if t >= 1:
                        turned(t - 1)
                turned(GT - 1)
                def output_lo(s):
                    for b in range(2):
                        dve.wait_ge(ot_h, (g * SEQS + s) * 2 + b + 1)
                        ins = dve.tensor_tensor(ot_lo[:, 2 * b:2 * b + 2, :].rearrange("p q t -> p (q t)"), ps_s[s][:, b, :],
                                                ot_hi[:, 2 * b:2 * b + 2, :].rearrange("p q t -> p (q t)").bitcast(F32), ALU.subtract)
                    ins.then_inc(ot_split, 1)

                def add_output(s):
                    dve.wait_ge(y_full, g * SEQS + s + 2)
                    x2 = X[:, ds(g * GT + 2 * s, 2), :].rearrange("p t d -> p (t d)")
                    dve.tensor_tensor(x2, ps_o[:, s, :], x2, ALU.add).then_inc(y_added, 1)

                for i in range(NS):
                    s, h = divmod(i, H)
                    dve.wait_ge(d_full, g * NS + i + 1)
                    dve.wait_ge(exp_done, g * NS + i + 1)
                    dve.tensor_scalar(dist[:, h % BANKS, :], ps_w[:, h % BANKS, 0:SCORES], 0.0, None, ALU.max).then_inc(relu_done, 1)
                    if ahead and h == 1 + 3 * s:
                        norm_stats(g + 1, s)
                    if ahead and h == 2 + 3 * s:
                        norm_variance(g + 1, s)
                    first = 6 + 4 * s
                    if ahead and h in (first, first + 1):
                        norm_apply(g + 1, s, (2 * (h - first), 2 * (h - first) + 1))
                    if i == OUT + LAG:
                        output_lo(0)
                    if not ahead and i % 4 == 1 and i > 4:
                        qkv_rest(i // 4 - 1)
                if not ahead:
                    qkv_rest(NS // 4 - 1)
                add_output(0)
                if ahead:
                    split_x(g + 1)
                output_lo(1)
                add_output(1)

            dve.sem_inc(exp_done, BANKS)
            dve.memset(neghalf[:, :], -0.5).then_inc(s_pad, 1)
            norm_stats(0, 0)
            norm_variance(0, 0)
            for i in range(2):
                dve.memset(qs[i][:, :, 3 * HD + 2:3 * HD + 4].bitcast(F32), 1.0)
                dve.memset(qs[i][:, :, 3 * HD + 4:ROW].bitcast(F32), 0.0)
                dve.memset(ks[i][:, :, 3 * HD:3 * HD + 2].bitcast(F32), 1.0)
                dve.memset(ks[i][:, :, 3 * HD + 4:ROW].bitcast(F32), 0.0).then_inc(s_pad, 1)
            norm_apply(0, 0, range(GT))
            dve.wait_ge(s_vec, 16 * VECS)
            dve.wait_ge(xn_ready, 1)
            dve.tensor_tensor(X[:, 0:GT, :], xn[:, :, :], fs[:, :].unsqueeze(1).broadcast_to([P, GT, D]), ALU.mult).then_inc(h_mul, 1)
            dve.wait_ge(h_mul, 1)
            dve.tensor_tensor(X[:, 0:GT, :], X[:, 0:GT, :], fb[:, :].unsqueeze(1).broadcast_to([P, GT, D]), ALU.add).then_inc(h_ready, 1)
            norm_stats(0, 1)
            norm_variance(0, 1)
            dve.memset(v[:, :, :, HD:2 * HD], 0.0).then_inc(s_pad, 1)
            dve.tensor_scalar(gsc[:, :], gam[:, :], -SCALE, None, ALU.mult).then_inc(s_gsc, 1)
            norm_apply(0, 1, range(GT))
            dve.wait_ge(s_pad, 4)
            split_x(0)
            with dve.Fori(0, NG - 1) as g:
                group(g, True)
            group(NG - 1, False)

        @block.gpsimd
        def _(pool):
            def rstd(g, k):
                pool.wait_ge(ve_done, g * 2 + k + 1)
                pool.tensor_tensor(rs[:, :], ve[:, :], neghalf[:, :], ALU.pow).then_inc(rs_done, 1)

            def scale_h(g, t):
                if t == 0:
                    reach(pool, xn_ready, g * 2 + 1)
                ins = pool.tensor_tensor(X[:, ds(g * GT + t, 1), :].rearrange("p a d -> p (a d)"), xn[:, t, :], fs[:, :], ALU.mult)
                if t == GT - 1:
                    ins.then_inc(h_mul, 1)

            def bias_h(g, t):
                if t == 0:
                    reach(pool, h_mul, g + 1)
                xt = X[:, ds(g * GT + t, 1), :].rearrange("p a d -> p (a d)")
                ins = pool.tensor_tensor(xt, xt, fb[:, :], ALU.add)
                if t == GT - 1:
                    ins.then_inc(h_ready, 1)

            def group(g, ahead):
                for s in range(SEQS):
                    for h in range(H):
                        n = g * NS + s * H + h
                        reach(pool, exp_done, n + BANKS + 1)
                        diag = e[:, h % SLOTS, P:3 * P]
                        pool.affine_select(out=diag, in_=diag, compare_op=ALU.is_gt, fill=zero, base=0,
                                           pattern=[[0, 2], [-1, P]], channel_multiplier=1).then_inc(masked, 1)
                        if ahead and h == 2 + 3 * s:
                            rstd(g + 1, s)
                        if ahead and s == 0 and 8 <= h < 12:
                            scale_h(g + 1, h - 8)
                        if ahead and s == 0 and h >= 12:
                            bias_h(g + 1, h - 12)

            pool.memset(ident[:, :], 0.0).then_inc(s_ident, 1)
            pool.wait_ge(s_ident, 1)
            pool.affine_select(out=ident[:, :], in_=ident[:, :], compare_op=ALU.not_equal, fill=1.0, base=0,
                               pattern=[[-1, P]], channel_multiplier=1).then_inc(s_ident, 1)
            pool.wait_ge(s_pad, 1)
            rstd(0, 0)
            rstd(0, 1)
            pool.wait_ge(s_vec, 16 * VECS)
            zero = pool.to_reg(0.0)
            with pool.Fori(0, NG - 1) as g:
                group(g, True)
            group(NG - 1, False)


WINDOW, HEADS3, HD3 = 128, 8, 64


def constants():
    n, f = 2 * P, np.float32
    half = np.arange(0, HD3, 2).astype(f)
    inv_freq = (f(1.0) / np.power(f(10000.0), half / f(HD3))).astype(f)
    t = np.arange(n).astype(f)
    freqs = np.concatenate([t[:, None] * inv_freq[None, :]] * 2, axis=-1).astype(f)
    base = ((half + f(0.4 * HD3)) / f(1.4 * HD3)).astype(f)
    power = ((t - f(n // 2)) / f(WINDOW // 2)).astype(f)
    scale = np.power(base[None, :].astype(np.float64), power[:, None])
    scale = np.concatenate([scale, scale], axis=-1)
    cos, sin = np.cos(freqs.astype(np.float64)), np.sin(freqs.astype(np.float64))
    sin = sin * np.where(np.arange(HD3) < HD3 // 2, -1.0, 1.0)[None, :]
    return {"rotary": np.stack([-8 * cos * scale, -8 * sin * scale, cos / scale, sin / scale]).astype(f)}


def window_phase(nc, sems, X, dram, out, raw, qkv):
    L, H, HD, INNER, HID = 2, HEADS3, HD3, HEADS3 * HD3, 682
    FC = -(-HID // P)
    HIDP = FC * P
    LAST = HID - (FC - 1) * P
    IC = INNER // P
    SEQS = 2
    NH = SEQS * H
    QUAD = 4
    NQ = NH // QUAD
    SC = 3 * P
    FAR = float(np.finfo(np.float32).max)
    STEPS = L * NG
    NLOAD = 4 + 2 * (1 + 2 * L) + 4 * L
    SPLIT_AT = 4
    NORM_AT = {2: (0, 1), 3: (2, 3)}
    STATS_AT, SHIFT_AT = 0, 1
    FINISH_AT = (5, 8, 11)
    X0_AT = (2, 7, 10)
    PIECES = [("G", 0), ("G", 1), ("A", 0), ("A", 1), ("G", 2), ("G", 3), ("O", 0), ("O", 1), ("A", 2), ("A", 3),
              ("G", 4), ("G", 5), ("O", 2), ("O", 3), ("A", 4), ("A", 5), ("O", 4), ("O", 5)]

    def past(v):
        return max(v, 0) if isinstance(v, int) else v

    with ExitStack() as ctx:
        def sb(name, shape, dt=F32):
            return ctx.enter_context(nc.sbuf_tensor("w_" + name, shape, dt))

        def sem(name):
            sems.append(nc.alloc_semaphore("w_" + name))
            return sems[-1]

        def bank(name, n=1):
            return ctx.enter_context(nc.psum_tensor("w_" + name, [P, n, 512], F32))

        raw_qkv = raw[:, :].rearrange("p (c n) -> p c n", c=DC)
        raw_1 = raw[:, :].rearrange("p (c u n) -> p c u n", c=DC, u=2)
        raw_o = raw[:, 0:IC * D].rearrange("p (c n) -> p c n", c=IC)
        raw_2 = raw[:, IC * D:(IC + FC) * D].rearrange("p (c n) -> p c n", c=FC)
        qkv_hi, qkv_lo = qkv
        wo_hi = sb("wo_hi", [P, IC, D], F32R)
        wo_lo = sb("wo_lo", [P, IC, D], F32R)
        w1_hi = sb("w1_hi", [P, DC, 2, HIDP], F32R)
        w1_lo = sb("w1_lo", [P, DC, 2, HIDP], F32R)
        w2_hi = sb("w2_hi", [P, FC, D], F32R)
        w2_lo = sb("w2_lo", [P, FC, D], F32R)
        ln_all = sb("ln_all", [P, 2, L * DC])
        b1_all = sb("b1_all", [P, L, 2, FC])
        b2_all = sb("b2_all", [P, L * D])
        scl = sb("scl", [P, 2, 2, L * HD])
        tab = sb("tab", [P, L, 4, 2, HD])
        neghalf = sb("neghalf", [P, GT])
        ident = sb("ident", [P, P])
        mask = sb("mask", [P, SC])
        st = sb("st", [P, GT, 2, 6])
        mv = sb("mv", [P, GT, 2])
        ve = sb("ve", [P, GT])
        rs = sb("rs", [P, GT])
        nmr = sb("nmr", [P, GT])
        xn = sb("xn", [P, GT, D])
        xs = sb("xs", [P, GT, P])
        ah = sb("ah", [P, DC, GTOK], F32R)
        al = sb("al", [P, DC, GTOK], F32R)
        nh = sb("nh", [P, DC, GTOK], F32R)
        nl = sb("nl", [P, DC, GTOK], F32R)
        ss = sb("ss", [P, 2, H])
        sc = sb("sc", [P, 2, H])
        iv = sb("iv", [P, 2, H])
        y0 = sb("y0", [P, 2, H])
        ya = sb("ya", [P, 2, H])
        yb = sb("yb", [P, 2, H])
        rn = sb("rn", [P, GT, 2, H])
        m1 = sb("m1", [P, 2, 2, INNER])
        m2 = sb("m2", [P, 2, INNER])
        qt = sb("qt", [P, IC, GTOK])
        kt = sb("kt", [P, IC, GTOK])
        v = sb("v", [P, GT, INNER])
        sm = sb("sm", [P, 2, SC])
        mx = sb("mx", [P, NH, 2])
        rsum = sb("rsum", [P, 2, 2, QUAD])
        rinv = sb("rinv", [P, 2, QUAD])
        pr = sb("pr", [P, 2, SC])
        pt = sb("pt", [P, 2, SC])
        o = sb("o", [P, GT, INNER])
        ot_hi = sb("ot_hi", [P, 2, IC, P], F32R)
        ot_lo = sb("ot_lo", [P, 2, IC, P], F32R)
        gate = sb("gate", [P, 2, GTOK])
        nf = gate
        hid = sb("hid", [P, 2, GTOK])
        h_hi = sb("h_hi", [P, 2, GTOK], F32R)
        h_lo = sb("h_lo", [P, 2, GTOK], F32R)
        hres = [a[:, k, :].rearrange("p (t d) -> p t d", d=D) for a in (v.rearrange("p (k t) n -> p k (t n)", k=2),
                                                                        o.rearrange("p (k t) n -> p k (t n)", k=2)) for k in range(2)]

        ps_d = bank("ps_d", 2)
        ps_x = bank("ps_x", 2)
        ps_p = ps_x[:, 0:1, :]
        ps_a = ps_x[:, 1:2, :]
        ps_f = bank("ps_f", 2)
        ps_o = bank("ps_o", 2)

        names = ("h_out h_in h_last b2_added fin_last stored vec ident maskz mask pad fill raw_qkv raw_ow raw_1 hi_qkv hi_o hi_2 hi_1 split_qkv split_o split_2 "
                 "split_1 tab x_ready x0_st x0_mv x0_ve x0_rs staged t1_full ah_done split1 q_full k_full v_full sq v_done "
                 "qk_read ss_done sc_done iv_done y0_done ya_done yb_done rn_done rota kscaled s_full qt_done kt_done d_full sm_done "
                 "p_done p_full pt_done pv_done ri o_done ot_full ot_h ot_split y_tile x_mid shifted st mv ve rs xn t2_full nf_done "
                 "split2 nmr g_full a_full gelu_done gated h_hi h_split h_used xb padp fin")
        S = {x: sem(x) for x in names.split()}
        block = ctx.enter_context(nc.Block())

        def xt(g, t):
            return X[:, ds(g * GT + t, 1), :].rearrange("p a d -> p (a d)")

        def x2(g, s):
            return X[:, ds(g * GT + 2 * s, 2), :].rearrange("p t d -> p (t d)")

        def steps(eng, step):
            step(0, 0, None)
            with eng.Fori(1, NG - 1) as n:
                step(n, 0, 0)
            step(NG - 1, 0, 0)
            step(NG, 1, 0)
            with eng.Fori(NG + 1, STEPS - 1) as n:
                step(n, 1, 1)
            step(STEPS - 1, 1, 1)
            step(STEPS, None, 1)

        def at(n, k):
            return isinstance(n, int) and n == k

        def group_rows(n, la):
            return X[:, ds((n - NG * la) * GT, GT), :]

        def turned_in(t):
            return ps_x if t == GT - 1 else ps_d

        out_v = out.rearrange("s (t p) d -> p (s t) d", p=P)

        @block.sync
        def _(sp):
            def load_ow(l):
                sp.dma_start(raw_o, dram["L0_ffn_wo"][l].rearrange("(c p) n -> p c n", p=P)).then_inc(S["raw_ow"], 16)
                w2 = dram["L0_ffn_w2"][l]
                sp.dma_start(raw_2[:, 0:FC - 1, :], w2[0:(FC - 1) * P, :].rearrange("(c p) n -> p c n", p=P)).then_inc(S["raw_ow"], 16)
                sp.dma_start(raw_2[0:LAST, FC - 1, :], w2[(FC - 1) * P:HID, :]).then_inc(S["raw_ow"], 16)

            def load_qkv(l):
                sp.dma_start(raw_qkv, dram["L0_ffn_wqkv"][l].rearrange("(c p) n -> p c n", p=P)).then_inc(S["raw_qkv"], 16)

            def load_1(l):
                w1 = dram["L0_ffn_w1"][l].rearrange("(c p) (u n) -> p c u n", p=P, u=2)
                for u in range(2):
                    sp.dma_start(raw_1[:, :, u, 0:HID], w1[:, :, u, :]).then_inc(S["raw_1"], 16)

            def step(n, la, lf):
                if at(n, NG - 1):
                    sp.wait_ge(S["split_1"], 1)
                    load_qkv(1)
                    sp.wait_ge(S["split_qkv"], 1)
                    load_ow(1)
                if at(n, NG):
                    sp.wait_ge(S["split_o"], 2)
                    sp.wait_ge(S["split_2"], 2)
                    load_1(1)
                if la is not None:
                    sp.wait_ge(S["x_mid"], n * SEQS + SEQS)
                    sp.wait_ge(S["xn"], n)
                    xg = group_rows(n, la)
                    sp.dma_start(xs[1:P, :, :], xg[0:P - 1, :, P:D]).then_inc(S["shifted"], 16)
                    sp.dma_start(xs[0:1, :, :].rearrange("p (s t) d -> p s t d", s=SEQS)[:, :, 1, :],
                                 xg[P - 1:P, :, P:D].rearrange("p (s t) d -> p s t d", s=SEQS)[:, :, 0, :]).then_inc(S["shifted"], 16)

            last = slice(GT * (NG - 1), GT * NG)
            sp.dma_start(out_v[:, last, :], X[:, last, :]).then_inc(S["h_out"], 16)
            load_ow(0)
            for k, name in enumerate(("L0_ffn_ln_g", "L0_ffn_ln_b")):
                sp.dma_start(ln_all[:, k, :], dram[name].rearrange("l (c p) -> p (l c)", p=P)).then_inc(S["vec"], 16)
            sp.dma_start(tab[:, 0, :, :, :].rearrange("p k t d -> p (k t) d"),
                         dram["rotary"].rearrange("k (t p) d -> p (k t) d", p=P)).then_inc(S["vec"], 16)
            sp.dma_start(b2_all[:, :], dram["L0_ffn_b2"].rearrange("(a l) d -> a (l d)", a=1).broadcast_to([P, L * D])).then_inc(S["vec"], 16)
            for k, name in enumerate(("L0_ffn_q_scale", "L0_ffn_k_scale")):
                src = dram[name].rearrange("(a l) (u d) -> a l u d", a=1, u=2)
                sp.dma_start(scl[:, k, 0, :], dram[name].rearrange("(a l) d -> a (l d)", a=1).broadcast_to([P, L * HD])).then_inc(S["vec"], 16)
                for i in range(L):
                    for u in range(2):
                        sp.dma_start(scl[:, k, 1, i * HD + u * (HD // 2):i * HD + (u + 1) * (HD // 2)],
                                     src[:, i, 1 - u, :].broadcast_to([P, HD // 2])).then_inc(S["vec"], 16)
            sp.wait_ge(S["pad"], 1)
            for i in range(L):
                for u in range(2):
                    b1 = dram["L0_ffn_b1"][i, u * HID:(u + 1) * HID]
                    sp.dma_start(b1_all[:, i, u, 0:FC - 1], b1[0:(FC - 1) * P].rearrange("(c p) -> p c", p=P)).then_inc(S["vec"], 16)
                    sp.dma_start(b1_all[0:LAST, i, u, FC - 1:FC], b1[(FC - 1) * P:HID].rearrange("(p c) -> p c", c=1)).then_inc(S["vec"], 16)
            sp.wait_ge(S["split_o"], 1)
            sp.wait_ge(S["split_2"], 1)
            load_1(0)
            steps(sp, step)
            sp.wait_ge(S["h_out"], 16)
            sp.wait_ge(S["pv_done"], STEPS * NH)
            sp.wait_ge(S["ot_full"], STEPS * GT)
            sp.dma_start(hres[NG - 1], out_v[:, GT * (NG - 1):GT * NG, :]).then_inc(S["h_last"], 16)
            for g in range(NG - 1):
                sp.dma_start(hres[g], out_v[:, GT * g:GT * g + GT, :]).then_inc(S["h_in"], 16)
            for g in range(NG - 1):
                sp.wait_ge(S["fin"], g + 1)
                sp.dma_start(out_v[:, GT * g:GT * g + GT, :], X[:, GT * g:GT * g + GT, :]).then_inc(S["stored"], 16)
            for s in range(SEQS):
                sp.wait_ge(S["fin_last"], s + 1)
                t = GT * (NG - 1) + 2 * s
                sp.dma_start(out_v[:, t:t + 2, :], X[:, t:t + 2, :]).then_inc(S["stored"], 16)
            sp.wait_ge(S["stored"], 16 * (NG - 1 + SEQS))

        @block.tensor
        def _(pe):
            def turn_x(dst):
                for c in range(DC):
                    for t in range(GT):
                        mm = pe.transpose(dst[:, c, t * P:(t + 1) * P], xn[:, t, c * P:(c + 1) * P], ident[:, :])
                return mm

            def turn_in(n):
                pe.wait_ge(S["staged"], n + 1)
                turn_x(ps_x).then_inc(S["t1_full"], 1)

            def step(n, la, lf):
                def project(t, i):
                    m = n * GT + t
                    tok = slice(t * P, (t + 1) * P)
                    dst, full = ((ps_f[:, 0, :], "q_full"), (ps_f[:, 1, :], "k_full"), (ps_p[:, 0, :], "v_full"))[i]
                    if i < 2 and t == 0:
                        pe.wait_ge(S["x_mid"], past(n * SEQS + i - 1))
                    pe.wait_ge(S["v_done" if i == 2 else "qk_read"], m if i == 2 else past(2 * m + i - 1))
                    cols = slice(i * INNER, (i + 1) * INNER)
                    for c in range(DC):
                        pe.matmul(dst, ah[:, c, tok], qkv_hi[:, c, cols], start=(c == 0), stop=False)
                        pe.matmul(dst, ah[:, c, tok], qkv_lo[:, c, cols], start=False, stop=False)
                        mm = pe.matmul(dst, al[:, c, tok], qkv_hi[:, c, cols], start=False, stop=(c == DC - 1))
                    mm.then_inc(S[full], 1)

                def turn(t, i):
                    m = n * GT + t
                    pe.wait_ge(S["kscaled" if i else "rota"], m + 1 if i else 2 * m + 1)
                    pe.wait_ge(S["kt_done" if i else "qt_done"], m)
                    if t == GT - 1:
                        pe.wait_ge(S["v_done"], n * GT + GT)
                    for c in range(IC):
                        mm = pe.transpose(turned_in(t)[:, i, c * P:(c + 1) * P], m1[:, t % 2, i, c * P:(c + 1) * P], ident[:, :])
                    mm.then_inc(S["s_full"], 1)

                def scores(i):
                    s, h = divmod(i, H)
                    m = n * NH + i
                    if i in (0, 1, H):
                        pe.wait_ge(S["qt_done"], n * GT + (GT if i == H else GT - 1))
                        pe.wait_ge(S["kt_done"], n * GT + (GT - 2 if i == 0 else GT - 1 if i == 1 else GT))
                    pe.wait_ge(S["sm_done"], past(m - 1))
                    rows = slice(HD * (h % 2), HD * (h % 2) + HD)
                    t0, t1, t2 = 2 * s * P, (2 * s + 1) * P, (2 * s + 2) * P
                    b = ps_d[:, i % 2, :]
                    pe.matmul(b[:, 0:P], qt[rows, h // 2, t0:t1], kt[rows, h // 2, t0:t1], start=True, stop=True)
                    pe.matmul(b[:, P:SC], qt[rows, h // 2, t1:t2], kt[rows, h // 2, t0:t2], start=True, stop=True).then_inc(S["d_full"], 1)

                def turn_p(i):
                    m = n * NH + i
                    if i == 0:
                        pe.wait_ge(S["qt_done"], n * GT + GT)
                        pe.wait_ge(S["kt_done"], n * GT + GT)
                    pe.wait_ge(S["p_done"], m + 1)
                    pe.wait_ge(S["pt_done"], m)
                    for b in range(3):
                        mm = pe.transpose(ps_p[:, 0, b * P:(b + 1) * P], pr[:, i % 2, b * P:(b + 1) * P], ident[:, :])
                    mm.then_inc(S["p_full"], 1)

                def values(i):
                    s, h = divmod(i, H)
                    if i % QUAD == 0:
                        pe.wait_ge(S["o_done"], n * NQ + i // QUAD)
                    pe.wait_ge(S["pt_done"], n * NH + i + 1)
                    vs = slice(h * HD, (h + 1) * HD)
                    o0 = ps_a[:, 0, (i % QUAD) * HD:(i % QUAD + 1) * HD]
                    o1 = ps_a[:, 0, (QUAD + i % QUAD) * HD:(QUAD + i % QUAD + 1) * HD]
                    pe.matmul(o0, pt[:, i % 2, 0:P], v[:, 2 * s, vs], start=True, stop=True)
                    pe.matmul(o1, pt[:, i % 2, P:2 * P], v[:, 2 * s, vs], start=True, stop=False)
                    pe.matmul(o1, pt[:, i % 2, 2 * P:3 * P], v[:, 2 * s + 1, vs], start=False, stop=True).then_inc(S["pv_done"], 1)

                def turn_o(k):
                    if k == 0:
                        pe.wait_ge(S["o_done"], n * NQ + NQ // 2)
                        pe.wait_ge(S["sm_done"], n * NH + NH)
                    pe.wait_ge(S["ot_split"], past(n * GT + k - 1))
                    for c in range(IC):
                        mm = pe.transpose(ps_d[:, k % 2, c * P:(c + 1) * P], o[:, k, c * P:(c + 1) * P], ident[:, :])
                    mm.then_inc(S["ot_full"], 1)

                def project_out(k):
                    pe.wait_ge(S["ot_split"], n * GT + k + 1)
                    dst = ps_f[:, k // 2, (k % 2) * D:(k % 2 + 1) * D]
                    for c in range(IC):
                        pe.matmul(dst, ot_hi[:, k % 2, c, :], wo_hi[:, c, :], start=(k % 2 == 0 and c == 0), stop=False, skip_group_check=True)
                        pe.matmul(dst, ot_hi[:, k % 2, c, :], wo_lo[:, c, :], start=False, stop=False, skip_group_check=True)
                        mm = pe.matmul(dst, ot_lo[:, k % 2, c, :], wo_hi[:, c, :], start=False, stop=(k % 2 == 1 and c == IC - 1), skip_group_check=True)
                    mm.then_inc(S["y_tile"], 1)

                def piece(i):
                    what, j = PIECES[i]
                    m = (n - 1) * FC + j
                    if what == "O":
                        pe.wait_ge(S["h_split"], m + 3)
                        for t in range(GT):
                            tok = slice(t * P, (t + 1) * P)
                            dst = ps_o[:, t // 2, (t % 2) * D:(t % 2 + 1) * D]
                            pe.matmul(dst, h_hi[:, j % 2, tok], w2_hi[:, j, :], start=(j == 0 and t % 2 == 0), stop=False, skip_group_check=True)
                            pe.matmul(dst, h_hi[:, j % 2, tok], w2_lo[:, j, :], start=False, stop=False, skip_group_check=True)
                            mm = pe.matmul(dst, h_lo[:, j % 2, tok], w2_hi[:, j, :], start=False, stop=(j == FC - 1 and t % 2 == 1), skip_group_check=True)
                        mm.then_inc(S["h_used"], 1)
                        return
                    if i == 0:
                        pe.wait_ge(S["split_1"], lf + 1)
                        pe.wait_ge(S["split_2"], lf + 1)
                        pe.wait_ge(S["split2"], n * DC)
                    if what == "A":
                        pe.wait_ge(S["gelu_done"], m + 1)
                    elif j < 2:
                        pe.wait_ge(S["qk_read"], n * GT * 2 if la is None else (n * GT + GT) * 2)
                        pe.wait_ge(S["x_mid"], n * SEQS)
                    else:
                        pe.wait_ge(S["gated"], m + 1)
                    u = 1 if what == "G" else 0
                    cols = slice(j * P, (j + 1) * P)
                    for c in range(DC):
                        pe.matmul(ps_f[:, j % 2, :], w1_hi[:, c, u, cols], nh[:, c, :], start=(c == 0), stop=False)
                        pe.matmul(ps_f[:, j % 2, :], w1_lo[:, c, u, cols], nh[:, c, :], start=False, stop=False)
                        mm = pe.matmul(ps_f[:, j % 2, :], w1_hi[:, c, u, cols], nl[:, c, :], start=False, stop=(c == DC - 1))
                    mm.then_inc(S["g_full" if u else "a_full"], 1)

                def turn_normed():
                    pe.wait_ge(S["xn"], n)
                    pe.wait_ge(S["x_ready"], n - 1 + NG)
                    turn_x(ps_o).then_inc(S["t2_full"], 1)

                if la is not None:
                    pe.wait_ge(S["split_qkv"], la)
                    pe.wait_ge(S["split1"], n * DC + DC)
                    for t in range(GT):
                        project(t, 2)
                        project(t, 0)
                        if t >= 2:
                            turn(t - 2, 1)
                        project(t, 1)
                        if t >= 1:
                            turn(t - 1, 0)
                    turn(GT - 2, 1)
                    if lf is not None:
                        turn_normed()
                    turn(GT - 1, 0)
                    scores(0)
                    turn(GT - 1, 1)
                else:
                    turn_normed()
                for i in range(NH + 2):
                    if la is not None and 1 <= i < NH:
                        scores(i)
                    if la is not None and 1 <= i <= NH:
                        turn_p(i - 1)
                    if la is not None and i >= NH:
                        turn_o(i - NH)
                    if lf is not None:
                        piece(i)
                    if la is not None and i >= 2:
                        values(i - 2)
                if la is not None:
                    pe.wait_ge(S["split_o"], la + 1)
                    if lf is not None:
                        pe.wait_ge(S["gated"], n * FC + 2)
                    for k in range(GT):
                        project_out(k)
                        if k == 0:
                            pe.wait_ge(S["o_done"], n * NQ + NQ)
                        if k == 0 and not at(n, STEPS - 1):
                            turn_in(n + 1)
                        if k < GT - 2:
                            turn_o(k + 2)

            for x in ("gated", "h_used", "h_split"):
                pe.sem_inc(S[x], 2)
            pe.wait_ge(S["ident"], 2)
            pe.wait_ge(S["fill"], 1)
            turn_in(0)
            steps(pe, step)

        @block.scalar
        def _(act):
            def split_qkv(l):
                act.wait_ge(S["raw_qkv"], 16 * l)
                act.wait_ge(S["v_full"], l * NG * GT)
                act.activation(qkv_hi[:, :, :], raw_qkv, ACT.Copy).then_inc(S["hi_qkv"], 1)

            def split_o(l):
                act.wait_ge(S["raw_ow"], 48 * l + 48)
                act.wait_ge(S["y_tile"], l * NG * GT)
                act.activation(wo_hi[:, :, :], raw_o, ACT.Copy).then_inc(S["hi_o"], 1)

            def split_2(l):
                act.wait_ge(S["raw_ow"], 48 * l + 48)
                act.wait_ge(S["h_used"], l * NG * FC + 2)
                act.activation(w2_hi[0:LAST, FC - 1, :], raw_2[0:LAST, FC - 1, :], ACT.Copy)
                act.activation(w2_hi[:, 0:FC - 1, :], raw_2[:, 0:FC - 1, :], ACT.Copy).then_inc(S["hi_2"], 1)

            def split_1(l):
                act.wait_ge(S["raw_1"], 32 * l + 32)
                act.activation(w1_hi[:, :, :, 0:HID].rearrange("p c u n -> p (c u) n"),
                               raw_1[:, :, :, 0:HID].rearrange("p c u n -> p (c u) n"), ACT.Copy).then_inc(S["hi_1"], 1)

            def spread(n):
                act.wait_ge(S["t1_full"], n + 1)
                act.activation(ah[:, 0, :], ps_x[:, 0, :], ACT.Copy).then_inc(S["ah_done"], 1)
                act.activation(ah[:, 1, :].rearrange("p (s t) -> p s t", s=SEQS)[:, :, 1:2 * P],
                               ps_x[:, 1, :].rearrange("p (s t) -> p s t", s=SEQS)[:, :, 0:2 * P - 1], ACT.Copy).then_inc(S["ah_done"], 1)

            def step(n, la, lf):
                def keep_values(t):
                    m = n * GT + t
                    act.wait_ge(S["v_full"], m + 1)
                    act.wait_ge(S["pv_done"], n * NH)
                    act.activation(v[:, t, :], ps_p[:, 0, :], ACT.Copy).then_inc(S["v_done"], 1)

                def squares(t, i):
                    m = n * GT + t
                    act.wait_ge(S["rota"], past(2 * m + i - 1))
                    act.wait_ge(S["k_full" if i else "q_full"], m + 1)
                    act.activation(m2[:, i, :], ps_f[:, i, :], ACT.Square).then_inc(S["sq"], 1)

                def root(t):
                    act.wait_ge(S["iv_done"], n * GT + t + 1)
                    act.activation(y0[:, :, :], iv[:, :, :], ACT.Sqrt).then_inc(S["y0_done"], 1)

                def turned(t, i):
                    act.wait_ge(S["s_full"], 2 * (n * GT + t) + i + 1)
                    dst = kt if i else qt
                    act.activation(dst[:, :, t * P:(t + 1) * P], turned_in(t)[:, i, :].rearrange("p (c t) -> p c t", t=P),
                                   ACT.Copy).then_inc(S["kt_done" if i else "qt_done"], 1)

                def norm(tiles):
                    g = n - 1 - NG * lf
                    act.wait_ge(S["nmr"], n)
                    act.wait_ge(S["t1_full"], n if la is None else n + 1)
                    for t in tiles:
                        act.activation(xn[:, t, 0:P], xt(g, t)[:, 0:P], ACT.Identity, bias=nmr[:, t:t + 1], scale=rs[:, t:t + 1])
                        ins = act.activation(xn[:, t, P:D], xs[:, t, :], ACT.Identity, bias=nmr[:, t:t + 1], scale=rs[:, t:t + 1])
                    if tiles[-1] == GT - 1:
                        ins.then_inc(S["xn"], 1)

                if la is not None:
                    for t in range(GT):
                        keep_values(t)
                        if t >= 1:
                            root(t - 1)
                        squares(t, 0)
                        if t >= 2:
                            turned(t - 2, 1)
                        squares(t, 1)
                        if t >= 1:
                            turned(t - 1, 0)
                        if t in NORM_AT and lf is not None:
                            norm(NORM_AT[t])
                    turned(GT - 2, 1)
                    root(GT - 1)
                elif lf is not None:
                    norm(range(GT))
                if lf is not None:
                    act.wait_ge(S["t2_full"], n)
                    act.wait_ge(S["gated"], (n - 1) * FC + 2)
                    for c in range(DC):
                        s, b = (ln_all[:, k, lf * DC + c:lf * DC + c + 1] for k in range(2))
                        act.activation(nf[:, c, :], ps_o[:, c, :], ACT.Identity, bias=b, scale=s)
                        act.activation(nh[:, c, :], ps_o[:, c, :], ACT.Identity, bias=b, scale=s).then_inc(S["nf_done"], 1)
                if la is not None:
                    turned(GT - 1, 0)
                    turned(GT - 1, 1)

                def probabilities(i):
                    m = n * NH + i
                    q = n * NQ + i // QUAD
                    if i % QUAD == 0:
                        act.wait_ge(S["ri"], past(q - 1))
                    act.wait_ge(S["sm_done"], m + 1)
                    act.wait_ge(S["p_full"], past(m - 1))
                    act.activation(pr[:, i % 2, 0:P], sm[:, i % 2, 0:P], ACT.Exp, scale=-1.0,
                                   bias=mx[:, i, 0:1], accum_out=rsum[:, i // QUAD % 2, 0, i % QUAD:i % QUAD + 1])
                    act.activation(pr[:, i % 2, P:SC], sm[:, i % 2, P:SC], ACT.Exp, scale=-1.0,
                                   bias=mx[:, i, 1:2], accum_out=rsum[:, i // QUAD % 2, 1, i % QUAD:i % QUAD + 1]).then_inc(S["p_done"], 1)

                def gelu(j):
                    m = (n - 1) * FC + j
                    act.wait_ge(S["g_full"], m + 1)
                    act.wait_ge(S["gated"], m + 1)
                    if j < 2:
                        act.wait_ge(S["split2"], n * DC)
                    act.activation(gate[:, j % 2, :], ps_f[:, j % 2, :], ACT.Gelu, bias=b1_all[:, lf, 1, j:j + 1]).then_inc(S["gelu_done"], 1)

                def hidden_hi(j):
                    m = (n - 1) * FC + j
                    act.wait_ge(S["gated"], m + 3)
                    act.wait_ge(S["h_used"], m + 1)
                    act.activation(h_hi[:, j % 2, :], hid[:, j % 2, :], ACT.Copy).then_inc(S["h_hi"], 1)

                for i in range(NH + 2):
                    if la is not None and i < NH:
                        probabilities(i)
                    if lf is not None:
                        what, j = PIECES[i]
                        if what == "G" and j % 2 == 1:
                            gelu(j - 1)
                            gelu(j)
                        if i >= 1 and PIECES[i - 1][0] == "A":
                            hidden_hi(PIECES[i - 1][1])
                    if i == SPLIT_AT and at(n, NG - 1):
                        split_qkv(1)
                    if i == SPLIT_AT and at(n, NG):
                        split_o(1)
                    if i == SPLIT_AT and at(n, 0):
                        split_o(0)
                        split_2(0)
                if at(n, NG):
                    split_2(1)
                if at(n, 0):
                    act.wait_ge(S["vec"], 16 * NLOAD)
                    split_1(0)
                if la is not None:
                    for k in range(GT):
                        act.wait_ge(S["ot_full"], n * GT + k + 1)
                        act.wait_ge(S["y_tile"], past(n * GT + k - 1))
                        act.activation(ot_hi[:, k % 2, :, :].rearrange("p c t -> p (c t)"), ps_d[:, k % 2, :], ACT.Copy).then_inc(S["ot_h"], 1)
                        if k == 1 and not at(n, STEPS - 1):
                            spread(n + 1)
                if at(n, NG):
                    split_1(1)

            act.wait_ge(S["x_ready"], 1)
            act.activation(xn[:, :, :], X[:, 0:GT, :], ACT.Copy).then_inc(S["staged"], 1)
            act.wait_ge(S["fill"], 1)
            spread(0)
            steps(act, step)

        @block.vector
        def _(dve):
            def x0_variance(g):
                for t in range(GT):
                    ins = dve.bn_stats(st[:, t, 0, :], X[:, GT * g + t, :])
                ins.then_inc(S["x0_st"], 1)
                dve.wait_ge(S["x0_st"], g + 1)
                for t in range(GT):
                    ins = dve.bn_aggr(mv[:, t, :], st[:, t, 0, :])
                ins.then_inc(S["x0_mv"], 1)
                dve.wait_ge(S["x0_mv"], g + 1)
                dve.tensor_scalar(ve[:, :], mv[:, :, 1], EPS, None, ALU.add).then_inc(S["x0_ve"], 1)

            def x0_norm(g):
                dve.wait_ge(S["x0_rs"], g + 1)
                if g == NG - 1:
                    dve.wait_ge(S["h_out"], 16)
                for t in range(GT):
                    xg = X[:, GT * g + t, :]
                    ins = dve.tensor_scalar(xg, xg, mv[:, t, 0:1], rs[:, t:t + 1], ALU.subtract, ALU.mult)
                ins.then_inc(S["x_ready"], 1)

            def split_in(n):
                dve.wait_ge(S["ah_done"], n * DC + 1)
                dve.tensor_tensor(al[:, 0, :], ps_x[:, 0, :], ah[:, 0, :].bitcast(F32), ALU.subtract).then_inc(S["split1"], 1)
                dve.wait_ge(S["ah_done"], n * DC + 2)
                dve.tensor_tensor(al[:, 1, :].rearrange("p (s t) -> p s t", s=SEQS)[:, :, 1:2 * P],
                                  ps_x[:, 1, :].rearrange("p (s t) -> p s t", s=SEQS)[:, :, 0:2 * P - 1],
                                  ah[:, 1, :].bitcast(F32).rearrange("p (s t) -> p s t", s=SEQS)[:, :, 1:2 * P], ALU.subtract).then_inc(S["split1"], 1)

            def step(n, la, lf):
                def rotate(t, i, between=lambda: None):
                    m = n * GT + t
                    dve.wait_ge(S["sq"], 2 * m + i + 1)
                    dve.tensor_reduce(ss[:, i, :], m2[:, i, :].rearrange("p (h d) -> p h d", d=HD), AX.X, ALU.add).then_inc(S["ss_done"], 1)
                    between()
                    src = ps_f[:, i, :].rearrange("p (h d) -> p h d", d=HD)
                    src4 = ps_f[:, i, :].rearrange("p (h u d) -> p h u d", u=2, d=HD // 2)
                    cs = tab[:, la, 2 * i, t % 2, :].unsqueeze(1).broadcast_to([P, H, HD])
                    sn = tab[:, la, 2 * i + 1, t % 2, :].rearrange("p (u d) -> p u d", u=2)
                    dve.wait_ge(S["s_full"], past(2 * (m - 2) + i + 1))
                    dve.tensor_tensor(m1[:, t % 2, i, :].rearrange("p (h d) -> p h d", d=HD), src, cs, ALU.mult)
                    dst = m2[:, i, :].rearrange("p (h u d) -> p h u d", u=2, d=HD // 2)
                    dve.wait_ge(S["ss_done"], 2 * m + i + 1)
                    for u in range(2):
                        ins = dve.tensor_tensor(dst[:, :, u, :], src4[:, :, 1 - u, :], sn[:, u, :].unsqueeze(1).broadcast_to([P, H, HD // 2]), ALU.mult)
                    ins.then_inc(S["qk_read"], 1)

                def reciprocals(t):
                    m = n * GT + t
                    dve.tensor_scalar(sc[:, :, :], ss[:, :, :], 1e-24, None, ALU.max).then_inc(S["sc_done"], 1)
                    dve.wait_ge(S["sc_done"], m + 1)
                    dve.reciprocal(iv[:, :, :], sc[:, :, :]).then_inc(S["iv_done"], 1)

                def inverse_root(t):
                    m = n * GT + t
                    dve.wait_ge(S["y0_done"], m + 1)
                    dve.tensor_tensor(ya[:, :, :], y0[:, :, :], y0[:, :, :], ALU.mult).then_inc(S["ya_done"], 1)
                    dve.wait_ge(S["ya_done"], m + 1)
                    dve.scalar_tensor_tensor(yb[:, :, :], ya[:, :, :], -0.5, sc[:, :, :], ALU.mult, ALU.mult).then_inc(S["yb_done"], 1)
                    dve.wait_ge(S["yb_done"], m + 1)
                    dve.scalar_tensor_tensor(rn[:, t, :, :], yb[:, :, :], 1.5, y0[:, :, :], ALU.add, ALU.mult).then_inc(S["rn_done"], 1)

                def norm_stats():
                    reach(dve, S["shifted"], n * 32)
                    for t in range(GT):
                        ins = dve.bn_stats(st[:, t, 1, :], xs[:, t, :])
                    ins.then_inc(S["st"], 1)
                    reach(dve, S["st"], n)
                    for t in range(GT):
                        ins = dve.bn_aggr(mv[:, t, :], st[:, t, :, :].rearrange("p a b -> p (a b)"))
                    ins.then_inc(S["mv"], 1)
                    dve.wait_ge(S["mv"], n)
                    dve.tensor_scalar(ve[:, :], mv[:, :, 1], EPS, None, ALU.add).then_inc(S["ve"], 1)

                def norm_shift():
                    dve.wait_ge(S["rs"], n)
                    dve.scalar_tensor_tensor(nmr[:, :], mv[:, :, 0], -1.0, rs[:, :], ALU.mult, ALU.mult).then_inc(S["nmr"], 1)

                if la is not None:
                    for t in range(GT):
                        rotate(t, 0, (lambda: inverse_root(t - 1)) if t >= 1 else lambda: None)
                        if lf is not None and t == SHIFT_AT:
                            norm_shift()
                        rotate(t, 1)
                        reciprocals(t)
                        if lf is not None and t == STATS_AT:
                            norm_stats()
                    inverse_root(GT - 1)
                else:
                    norm_stats()
                    norm_shift()
                if lf is not None:
                    for c in range(DC):
                        dve.wait_ge(S["nf_done"], (n - 1) * DC + c + 1)
                        dve.tensor_tensor(nl[:, c, :], nf[:, c, :], nh[:, c, :].bitcast(F32), ALU.subtract).then_inc(S["split2"], 1)

                def soft(i):
                    s, h = divmod(i, H)
                    m = n * NH + i
                    reach(dve, S["d_full"], m + 1, S["p_done"], past(m - 1))
                    dve.tensor_tensor_reduce(sm[:, i % 2, 0:P], ps_d[:, i % 2, 0:P], mask[:, 0:P], rn[:, 2 * s, 0, h:h + 1], FAR, ALU.add, ALU.min,
                                             mx[:, i, 0:1])
                    dve.tensor_tensor_reduce(sm[:, i % 2, P:SC], ps_d[:, i % 2, P:SC], mask[:, P:SC], rn[:, 2 * s + 1, 0, h:h + 1], FAR, ALU.add, ALU.min,
                                             mx[:, i, 1:2]).then_inc(S["sm_done"], 1)

                def turned_p(i):
                    m = n * NH + i
                    dve.wait_ge(S["pv_done"], past(m - 1))
                    dve.wait_ge(S["p_full"], m + 1)
                    dve.tensor_copy(pt[:, i % 2, :], ps_p[:, 0, 0:SC]).then_inc(S["pt_done"], 1)

                def normalise(i):
                    s, h = divmod(i + 1 - QUAD, H)
                    q = n * NQ + i // QUAD
                    dve.wait_ge(S["p_done"], n * NH + i + 1)
                    dve.wait_ge(S["o_done"], q)
                    dve.reciprocal(rinv[:, :, :], rsum[:, i // QUAD % 2, :, :]).then_inc(S["ri"], 1)
                    dve.wait_ge(S["ri"], q + 1)
                    dve.wait_ge(S["pv_done"], n * NH + i + 1)
                    dve.wait_ge(S["ot_full"], n * GT)
                    dve.tensor_tensor(o[:, 2 * s:2 * s + 2, h * HD:(h + QUAD) * HD].rearrange("p w (h d) -> p w h d", d=HD),
                                      ps_a[:, 0, :].rearrange("p (w h d) -> p w h d", w=2, d=HD),
                                      rinv[:, :, :].unsqueeze(3).broadcast_to([P, 2, QUAD, HD]), ALU.mult).then_inc(S["o_done"], 1)

                def gated(j):
                    m = (n - 1) * FC + j
                    dve.wait_ge(S["a_full"], m + 1)
                    dve.wait_ge(S["h_split"], m + 1)
                    dve.scalar_tensor_tensor(hid[:, j % 2, :], ps_f[:, j % 2, :], b1_all[:, lf, 0, j:j + 1], gate[:, j % 2, :],
                                             ALU.add, ALU.mult).then_inc(S["gated"], 1)

                def hidden_lo(j):
                    m = (n - 1) * FC + j
                    dve.wait_ge(S["h_hi"], m + 1)
                    dve.tensor_tensor(h_lo[:, j % 2, :], hid[:, j % 2, :], h_hi[:, j % 2, :].bitcast(F32), ALU.subtract).then_inc(S["h_split"], 1)

                def add_output():
                    g = n - 1 - NG * lf
                    dve.wait_ge(S["xb"], n)
                    dve.wait_ge(S["h_used"], n * FC + 2)
                    for s in range(SEQS):
                        ins = dve.tensor_tensor(x2(g, s), ps_o[:, s, :], x2(g, s), ALU.add)
                        if at(n, STEPS):
                            ins.then_inc(S["fin_last"], 1)
                    if not at(n, STEPS):
                        ins.then_inc(S["x_ready"], 1)

                def add_attention(s):
                    dve.wait_ge(S["y_tile"], n * GT + 2 * s + 2)
                    g = n - NG * la
                    dve.tensor_tensor(x2(g, s), ps_f[:, s, :], x2(g, s), ALU.add).then_inc(S["x_mid"], 1)

                def output_lo(k):
                    dve.wait_ge(S["ot_h"], n * GT + k + 1)
                    dve.tensor_tensor(ot_lo[:, k % 2, :, :].rearrange("p c t -> p (c t)"), ps_d[:, k % 2, :],
                                      ot_hi[:, k % 2, :, :].rearrange("p c t -> p (c t)").bitcast(F32), ALU.subtract).then_inc(S["ot_split"], 1)

                for i in range(NH + 3):
                    if la is not None:
                        if i == NH + 2:
                            output_lo(0)
                        if i >= 3 and (i - 2) % QUAD == 0:
                            normalise(i - 3)
                        if i < NH:
                            soft(i)
                        if 1 <= i <= NH:
                            turned_p(i - 1)
                    if at(n, 0) and i in X0_AT:
                        x0_variance(X0_AT.index(i) + 1)
                    if at(n, 0) and i - 1 in X0_AT:
                        x0_norm(X0_AT.index(i - 1) + 1)
                    if lf is not None:
                        if i >= 2 and PIECES[i - 2][0] == "A":
                            hidden_lo(PIECES[i - 2][1])
                        if 1 <= i <= NH + 2 and PIECES[i - 1][0] == "A":
                            gated(PIECES[i - 1][1])
                    if at(n, STEPS) and i in FINISH_AT:
                        g = FINISH_AT.index(i)
                        dve.wait_ge(S["h_in"], 16 * (NG - 1))
                        dve.wait_ge(S["x_ready"], NG + STEPS - 1)
                        xg = X[:, GT * g:GT * g + GT, :]
                        dve.tensor_tensor(xg, xg, hres[g], ALU.add).then_inc(S["fin"], 1)
                if la is not None:
                    for k in range(GT):
                        if k >= 1:
                            output_lo(k)
                        if k == 0 and lf is not None:
                            add_output()
                        if k == 1 and not at(n, STEPS - 1):
                            split_in(n + 1)
                        if k == 2:
                            add_attention(0)
                    add_attention(1)
                    g = n - NG * la
                    reach(dve, S["x_mid"], n * SEQS + SEQS)
                    for t in range(GT):
                        dve.bn_stats(st[:, t, 0, :], xt(g, t)[:, 0:P])
                else:
                    add_output()

            dve.memset(neghalf[:, :], -0.5).then_inc(S["padp"], 1)
            dve.memset(b1_all[:, :, :, :], 0.0).then_inc(S["pad"], 1)
            x0_variance(0)
            dve.memset(xs[0:1, :, :], 0.0)
            for a in (ah, al):
                dve.memset(a[:, 1, :].rearrange("p (s t) -> p s t", s=SEQS)[:, :, 0:1].bitcast(F32), 0.0)
            for w in (w1_hi, w1_lo):
                dve.memset(w[:, :, :, HID:HIDP].bitcast(F32), 0.0)
            for w in (w2_hi, w2_lo):
                dve.memset(w[:, FC - 1, :].bitcast(F32), 0.0)
            dve.memset(mx[:, :, :], 0.0).then_inc(S["fill"], 1)
            x0_norm(0)
            dve.wait_ge(S["fill"], 1)
            split_in(0)
            dve.wait_ge(S["vec"], 16 * NLOAD)
            for l in reversed(range(L)):
                for i in range(2):
                    for u in range(2):
                        ins = dve.tensor_tensor(tab[:, l, 2 * i + u, :, :], tab[:, 0, 2 * i + u, :, :],
                                                scl[:, i, u, l * HD:(l + 1) * HD].unsqueeze(1).broadcast_to([P, 2, HD]), ALU.mult)
            ins.then_inc(S["tab"], 1)
            dve.wait_ge(S["tab"], 1)
            steps(dve, step)

        @block.gpsimd
        def _(pool):
            def x0_root(g):
                pool.wait_ge(S["x0_ve"], g + 1)
                pool.tensor_tensor(rs[:, :], ve[:, :], neghalf[:, :], ALU.pow).then_inc(S["x0_rs"], 1)

            def lo_qkv(l):
                pool.wait_ge(S["hi_qkv"], l)
                pool.tensor_tensor(qkv_lo[:, :, :], raw_qkv, qkv_hi[:, :, :].bitcast(F32), ALU.subtract).then_inc(S["split_qkv"], 1)

            def lo_o(l):
                pool.wait_ge(S["hi_o"], l + 1)
                pool.tensor_tensor(wo_lo[:, :, :], raw_o, wo_hi[:, :, :].bitcast(F32), ALU.subtract).then_inc(S["split_o"], 1)

            def lo_2(l):
                pool.wait_ge(S["hi_2"], l + 1)
                pool.tensor_tensor(w2_lo[0:LAST, FC - 1, :], raw_2[0:LAST, FC - 1, :], w2_hi[0:LAST, FC - 1, :].bitcast(F32), ALU.subtract)
                pool.tensor_tensor(w2_lo[:, 0:FC - 1, :], raw_2[:, 0:FC - 1, :], w2_hi[:, 0:FC - 1, :].bitcast(F32), ALU.subtract).then_inc(S["split_2"], 1)

            def lo_1(l):
                pool.wait_ge(S["hi_1"], l + 1)
                pool.tensor_tensor(w1_lo[:, :, :, 0:HID].rearrange("p c u n -> p (c u) n"), raw_1[:, :, :, 0:HID].rearrange("p c u n -> p (c u) n"),
                                   w1_hi[:, :, :, 0:HID].rearrange("p c u n -> p (c u) n").bitcast(F32), ALU.subtract).then_inc(S["split_1"], 1)

            def stage(n, l):
                reach(pool, S["x_ready"], n + 1)
                pool.tensor_copy(xn[:, :, :], X[:, ds((n - NG * l) * GT, GT), :]).then_inc(S["staged"], 1)

            def step(n, la, lf):
                if la is not None:
                    for t in range(GT):
                        m = n * GT + t
                        for i in range(2):
                            pool.wait_ge(S["qk_read"], 2 * m + i + 1)
                            pool.tensor_tensor(m1[:, t % 2, i, :], m1[:, t % 2, i, :], m2[:, i, :], ALU.add).then_inc(S["rota"], 1)
                        pool.wait_ge(S["rota"], 2 * m + 2)
                        pool.wait_ge(S["rn_done"], m + 1)
                        mk = m1[:, t % 2, 1, :].rearrange("p (h d) -> p h d", d=HD)
                        pool.tensor_tensor(mk, mk, rn[:, t, 1, :].unsqueeze(2).broadcast_to([P, H, HD]), ALU.mult).then_inc(S["kscaled"], 1)
                        if t == STATS_AT and lf is not None:
                            pool.wait_ge(S["ve"], n)
                            pool.tensor_tensor(rs[:, :], ve[:, :], neghalf[:, :], ALU.pow).then_inc(S["rs"], 1)
                else:
                    pool.wait_ge(S["ve"], n)
                    pool.tensor_tensor(rs[:, :], ve[:, :], neghalf[:, :], ALU.pow).then_inc(S["rs"], 1)
                if lf is not None:
                    g = n - 1 - NG * lf
                    reach(pool, S["xn"], n)
                    for t in range(GT):
                        ins = pool.tensor_tensor(xt(g, t), xt(g, t), b2_all[:, lf * D:(lf + 1) * D], ALU.add)
                    if at(n, STEPS):
                        ins.then_inc(S["b2_added"], 1)
                        pool.wait_ge(S["h_last"], 16)
                        pool.wait_ge(S["b2_added"], 1)
                        xg = X[:, GT * (NG - 1):GT * NG, :]
                        ins = pool.tensor_tensor(xg, xg, hres[NG - 1], ALU.add)
                    ins.then_inc(S["xb"], 1)

            def between(n, la, lf):
                step(n, la, lf)
                if at(n, 0):
                    x0_root(1)
                if lf is None:
                    pool.wait_ge(S["t1_full"], n + 1)
                else:
                    pool.wait_ge(S["t2_full"], n)
                if la is not None and not at(n, STEPS - 1):
                    stage(n + 1, 1 if isinstance(n, int) and n + 1 >= NG else la)
                if at(n, 0):
                    x0_root(2)
                    x0_root(3)
                    lo_o(0)
                    lo_2(0)
                    lo_1(0)
                if at(n, NG - 1):
                    lo_qkv(1)
                if at(n, NG):
                    lo_o(1)
                    lo_2(1)
                    lo_1(1)

            pool.memset(ident[:, :], 0.0).then_inc(S["ident"], 1)
            pool.memset(mask[:, :], 0.0).then_inc(S["maskz"], 1)
            pool.wait_ge(S["ident"], 1)
            pool.affine_select(out=ident[:, :], in_=ident[:, :], compare_op=ALU.not_equal, fill=1.0, base=0,
                               pattern=[[-1, P]], channel_multiplier=1).then_inc(S["ident"], 1)
            pool.wait_ge(S["maskz"], 1)
            for i, sign in ((0, 1), (1, -1), (2, 1)):
                m = mask[:, i * P:(i + 1) * P]
                ins = pool.affine_select(out=m, in_=m, compare_op=ALU.is_ge, fill=FAR, base=0, pattern=[[-sign, P]], channel_multiplier=sign)
            ins.then_inc(S["mask"], 1)
            pool.wait_ge(S["padp"], 1)
            x0_root(0)

            steps(pool, between)


def program(nc, dram, out, phases=3):
    def run(phase, *args):
        sems = []
        phase(nc, sems, X, dram, *args)
        nc.clear_and_free_semaphores(sems)
        nc.all_engine_barrier()

    with ExitStack() as ctx:
        ctx.enter_context(nc.allow_non_contiguous_dma(reason="short vectors, loaded once"))
        X = ctx.enter_context(nc.sbuf_tensor("X", [P, NT, D], F32))
        raw = ctx.enter_context(nc.sbuf_tensor("raw", [P, 3072], F32))
        qkv = [ctx.enter_context(nc.sbuf_tensor("qkv_" + x, [P, DC, 3 * HEADS3 * HD3], F32R)) for x in ("hi", "lo")]
        with ExitStack() as early:
            wa = [early.enter_context(nc.sbuf_tensor(f"wa_{x}", [P, n, w], F32R))
                  for n, w, k in ((DC, 3 * D, "w"), (4, D, "o")) for x in (k + "hi", k + "lo")]
            run(tower_phase, raw, wa)
            if phases >= 2:
                run(attention_phase, wa, out, raw, qkv)
        if phases >= 3:
            run(window_phase, out, raw, qkv)
            return
        s_out = ctx.enter_context(nc.semaphore("s_out"))
        with nc.Block() as block:
            @block.sync
            def _(sp):
                sp.dma_start(out.rearrange("s (t p) d -> p (s t) d", p=P), X[:, :, :]).then_inc(s_out, 16)
                sp.wait_ge(s_out, 16)


_INS = ["x", "L0_tok_emb", "L0_tok_pos_emb", "L0_tok_A_diag", "L0_tok_B", "L0_tok_C", "L0_tok_D", "L0_tok_w1", "L0_tok_b1",
        "L0_tok_w2", "L0_tok_b2", "L0_tok_ln1_s", "L0_tok_ln1_b", "L0_tok_ln2_s", "L0_tok_ln2_b", "L0_tok_lnf_s", "L0_tok_lnf_b",
        "L0_attn_Wq", "L0_attn_Wk", "L0_attn_Wv", "L0_attn_Wo", "L0_attn_gamma", "L0_ffn_wqkv", "L0_ffn_q_scale", "L0_ffn_k_scale",
        "L0_ffn_wo", "L0_ffn_ln_g", "L0_ffn_ln_b", "L0_ffn_w1", "L0_ffn_b1", "L0_ffn_w2", "L0_ffn_b2"]


def kernel(**inputs):
    import concourse.bacc as bacc
    from concourse.bass_utils import run_bass_kernel_spmd

    nc = bacc.Bacc("TRN2", target_bir_lowering=False, num_devices=1)
    arrays, dram = {}, {}
    for name, a in {**{n: inputs[n] for n in _INS}, **constants()}.items():
        a = np.ascontiguousarray(a)
        arrays[f"in_{name}"] = a
        dram[name] = nc.dram_tensor(f"in_{name}", a.shape, mybir.dt.from_np(a.dtype), kind="ExternalInput").ap()
    out = nc.dram_tensor("out", (8, 2 * P, D), F32, kind="ExternalOutput").ap()
    program(nc, dram, out)
    return run_bass_kernel_spmd(nc, [arrays], core_ids=[0]).results[0]["out"]
```
